# Optimizing a Trainium2 kernel written in Bass

```python
import numpy as np
import jax
import jax.numpy as jnp

def _softmax(x, axis=-1):
    return jax.nn.softmax(x, axis=axis)

def _gelu(x):
    return jax.nn.gelu(x, approximate=True)

def _silu(x):
    return jax.nn.silu(x)

def _sigmoid(x):
    return jax.nn.sigmoid(x)

def _layernorm(x, axis=-1, eps=1e-05):
    m = jnp.mean(x, axis=axis, keepdims=True)
    v = jnp.var(x, axis=axis, keepdims=True)
    return (x - m) / jnp.sqrt(v + eps)

def _scatter_add(tgt, idx, src, axis=0):
    return tgt.at[idx].add(src)

def _segment_sum(src, seg, n):
    return jax.ops.segment_sum(src, seg, n)
kernel_name = 'mk_decoder_preln_d4_seqx_r8_b6c9bd'

def setup_inputs(seed: int=0):
    np.random.seed(seed)
    _w = jnp.asarray

    def _rec_inputs():
        import jax
        import jax.numpy as jnp
        _rk = jax.random.key(seed)
        x = 7.22e-05 + 1 * jax.random.normal(jax.random.fold_in(_rk, 1), (16, 64, 256), jnp.float32)
        _lenS = 64 - jax.random.randint(jax.random.fold_in(_rk, 7), (16,), 0, max(1, 64 // 4) + 1, jnp.int32)
        _lenS2 = 64 - jax.random.randint(jax.random.fold_in(_rk, 8), (16,), 0, max(1, 64 // 4) + 1, jnp.int32)
        _ctx_512P = jax.random.normal(jax.random.fold_in(_rk, 11), (16, 16, 64), jnp.float32)
        _ctx_512c = jax.random.dirichlet(jax.random.fold_in(_rk, 511), 0.3 * jnp.ones((16,), jnp.float32), (16, 64))
        _ctx_512t = jnp.einsum('bsk,bkd->bsd', _ctx_512c, _ctx_512P)
        _ctx_512t = _ctx_512t * jax.lax.rsqrt(jnp.mean(jnp.square(_ctx_512t)) + 1e-12) * 0.953939
        ctx_512 = -0.000514642 + 1.00011 * (_ctx_512t + 0.3 * jax.random.normal(jax.random.fold_in(_rk, 611), (16, 64, 64), jnp.float32))
        return (x, ctx_512)
    x, ctx_512 = _rec_inputs()

    def _L0_attn_setup():
        import jax, jax.numpy as jnp
        import numpy as np
        H, DK, DV = (6, 32, 64)
        HID = 256
        CONV = 4
        NORM_EPS = 1e-05

        def causal_dwconv_silu(x, w):
            K = w.shape[1]
            xp = jnp.pad(x, ((0, 0), (K - 1, 0), (0, 0)))
            y = jax.lax.conv_general_dilated(jnp.transpose(xp, (0, 2, 1)), w[:, None, :], (1,), 'VALID', feature_group_count=w.shape[0])
            return jax.nn.silu(jnp.transpose(y, (0, 2, 1)))

        def l2norm(x, eps=1e-06):
            return x * jax.lax.rsqrt(jnp.sum(x * x, axis=-1, keepdims=True) + eps)
        key = jax.random.key(seed)
        ks = jax.random.split(key, 16)
        B, T = (2, 512)
        s = HID ** (-0.5)
        return dict(hidden_states=jax.random.normal(ks[0], (B, T, HID), jnp.float32), Wq=jax.random.normal(ks[1], (H * DK, HID), jnp.float32) * s, Wk=jax.random.normal(ks[2], (H * DK, HID), jnp.float32) * s, Wv=jax.random.normal(ks[3], (H * DV, HID), jnp.float32) * s, Wb=jax.random.normal(ks[4], (H, HID), jnp.float32) * s, Wa=jax.random.normal(ks[5], (H, HID), jnp.float32) * s, A_log=jnp.log(jax.random.uniform(ks[6], (H,), jnp.float32, 0.5, 16.0)), dt_bias=jax.random.normal(ks[7], (H,), jnp.float32) * 0.1, conv_wq=jax.random.normal(ks[8], (H * DK, CONV), jnp.float32) * 0.5, conv_wk=jax.random.normal(ks[9], (H * DK, CONV), jnp.float32) * 0.5, conv_wv=jax.random.normal(ks[10], (H * DV, CONV), jnp.float32) * 0.5, Wg=jax.random.normal(ks[11], (H * DV, HID), jnp.float32) * s, norm_w=jnp.ones((DV,), jnp.float32), Wo=jax.random.normal(ks[12], (HID, H * DV), jnp.float32) * (H * DV) ** (-0.5))
    _L0_attn_all = _L0_attn_setup()
    _L0_attn_in = {k: v for k, v in _L0_attn_all.items() if k in ('Wq', 'Wk', 'Wv', 'Wb', 'Wa', 'A_log', 'dt_bias', 'conv_wq', 'conv_wk', 'conv_wv', 'Wg', 'norm_w', 'Wo')}
    del _L0_attn_all

    def _L0_xattn_setup():
        import jax, jax.numpy as jnp
        import numpy as np
        import math
        NUM_Q_HEADS = 32
        NUM_KV_HEADS = 8
        key = jax.random.key(seed)
        k1, k2, k3 = jax.random.split(key, 3)
        B, S, E = (2, 256, 256)
        kv_E = NUM_KV_HEADS * (E // NUM_Q_HEADS)
        q = jax.random.normal(k1, (B, S, E), dtype=jnp.float32)
        k = jax.random.normal(k2, (B, S, kv_E), dtype=jnp.float32)
        v = jax.random.normal(k3, (B, S, kv_E), dtype=jnp.float32)
        return {'q': q, 'k': k, 'v': v}
    _L0_xattn_all = _L0_xattn_setup()
    _L0_xattn_in = {k: v for k, v in _L0_xattn_all.items() if k in ()}
    del _L0_xattn_all

    def _L0_ffn_setup():
        import jax, jax.numpy as jnp
        import numpy as np
        NUM_EXPERTS = 8
        HIDDEN = 256
        INTER = 256
        TOP_K = 2
        key = jax.random.key(seed)
        ks = jax.random.split(key, 7)
        hidden_states = jax.random.normal(ks[0], (4, 256, HIDDEN), dtype=jnp.float32)
        gate_w = jax.random.normal(ks[1], (HIDDEN, NUM_EXPERTS), dtype=jnp.float32) * 0.02
        fc1_w = jax.random.normal(ks[2], (NUM_EXPERTS, HIDDEN, INTER), dtype=jnp.float32) * 0.02
        fc1_b = jnp.zeros((NUM_EXPERTS, INTER), dtype=jnp.float32)
        fc2_w = jax.random.normal(ks[3], (NUM_EXPERTS, INTER, HIDDEN), dtype=jnp.float32) * 0.02
        fc2_b = jnp.zeros((NUM_EXPERTS, HIDDEN), dtype=jnp.float32)
        alpha = jax.random.normal(ks[4], (NUM_EXPERTS,), dtype=jnp.float32)
        return {'hidden_states': hidden_states, 'gate_w': gate_w, 'fc1_w': fc1_w, 'fc1_b': fc1_b, 'fc2_w': fc2_w, 'fc2_b': fc2_b, 'alpha': alpha}
    _L0_ffn_all = _L0_ffn_setup()
    _L0_ffn_in = {k: v for k, v in _L0_ffn_all.items() if k in ('gate_w', 'fc1_w', 'fc1_b', 'fc2_w', 'fc2_b', 'alpha')}
    del _L0_ffn_all

    def _L1_attn_setup():
        import jax, jax.numpy as jnp
        import numpy as np
        B, T, D, S = (8, 512, 256, 64)
        key = jax.random.key(seed)
        ks = jax.random.split(key, 7)
        sd_in = 1.0 / np.sqrt(D)
        sd_s = 1.0 / np.sqrt(S)
        x = jax.random.normal(ks[0], (B, T, D), jnp.float32)
        Wa = jax.random.uniform(ks[1], (S, D), jnp.float32, -sd_in, sd_in)
        ba = jax.random.uniform(ks[2], (S,), jnp.float32, -sd_in, sd_in)
        Wb = jax.random.uniform(ks[3], (S, D), jnp.float32, -sd_in, sd_in)
        bb = jax.random.uniform(ks[4], (S,), jnp.float32, -sd_in, sd_in)
        Wout = jax.random.uniform(ks[5], (D, S), jnp.float32, -sd_s, sd_s)
        bout = jax.random.uniform(ks[6], (D,), jnp.float32, -sd_s, sd_s)
        return {'x': x, 'Wa': Wa, 'ba': ba, 'Wb': Wb, 'bb': bb, 'Wout': Wout, 'bout': bout}
    _L1_attn_all = _L1_attn_setup()
    _L1_attn_in = {k: v for k, v in _L1_attn_all.items() if k in ('Wa', 'ba', 'Wb', 'bb', 'Wout', 'bout')}
    del _L1_attn_all

    def _L1_xattn_setup():
        import jax, jax.numpy as jnp
        import numpy as np
        B, S, L = (2, 128, 128)
        DIM_Q, H, K, D_C, D_CQ, R = (256, 16, 128, 64, 192, 64)

        def _rope_tables(seq_len, dim, dtype):
            inv_freq = 1.0 / 10000.0 ** (jnp.arange(0, dim, 2, dtype=dtype) / dim)
            t = jnp.arange(seq_len, dtype=dtype)
            freqs = t[:, None] * inv_freq[None, :]
            sin = jnp.repeat(jnp.sin(freqs), 2, axis=-1)
            cos = jnp.repeat(jnp.cos(freqs), 2, axis=-1)
            return (sin, cos)

        def _rotate_half(x):
            h = x.shape[-1] // 2
            return jnp.concatenate([-x[..., h:], x[..., :h]], axis=-1)
        key = jax.random.key(seed)
        ks = jax.random.split(key, 8)
        s_in = 1.0 / np.sqrt(DIM_Q)
        s_k = 1.0 / np.sqrt(K)
        s_cq = 1.0 / np.sqrt(D_CQ)
        s_c = 1.0 / np.sqrt(D_C)
        return {'hidden_q': jax.random.normal(ks[0], (B, S, DIM_Q), jnp.float32), 'kv_c': jax.random.normal(ks[1], (B, L, D_C), jnp.float32), 'Wq': jax.random.normal(ks[2], (H * K, DIM_Q), jnp.float32) * s_in, 'w_kc_q': jax.random.normal(ks[3], (H, K, D_CQ), jnp.float32) * s_k, 'w_kc_kv': jax.random.normal(ks[4], (H, K, D_C), jnp.float32) * s_k, 'W_qr': jax.random.normal(ks[5], (H, D_CQ, R), jnp.float32) * s_cq / np.sqrt(R), 'W_kr': jax.random.normal(ks[6], (H, D_C, R), jnp.float32) * s_c, 'Wo': jax.random.normal(ks[7], (DIM_Q, H * K), jnp.float32) * s_k}
    _L1_xattn_all = _L1_xattn_setup()
    _L1_xattn_in = {k: v for k, v in _L1_xattn_all.items() if k in ('Wq', 'w_kc_q', 'w_kc_kv', 'W_qr', 'W_kr', 'Wo')}
    del _L1_xattn_all

    def _L1_ffn_setup():
        import jax, jax.numpy as jnp
        import numpy as np
        import math
        GOLDEN_CENTER = 1.0 / math.e
        GOLDEN_LOWER = 0.5 - math.log(4.0 / 3.0)
        GOLDEN_UPPER = 0.5
        B, T, D = (4, 128, 256)
        E = 8
        F = 1024 // (E // 2)
        R = 64
        NL = 2

        def _router_weights(x, Wr, temperature):
            logits = jnp.einsum('btd,de->bte', x, Wr)
            inhibition = jax.nn.sigmoid(logits / temperature)
            in_zone = (inhibition >= GOLDEN_LOWER) & (inhibition <= GOLDEN_UPPER)
            distance = jnp.abs(inhibition - GOLDEN_CENTER)
            w = jnp.exp(-distance / 0.1) * in_zone.astype(x.dtype)
            wsum = w.sum(axis=-1, keepdims=True)
            no_expert = wsum < 1e-08
            fb = jnp.exp(-distance / 0.3)
            _, top2 = jax.lax.top_k(fb, 2)
            fb_mask = jax.nn.one_hot(top2, E, dtype=x.dtype).sum(axis=-2)
            fb_w = fb * fb_mask
            fb_w = fb_w / jnp.clip(fb_w.sum(axis=-1, keepdims=True), 1e-08)
            w = jnp.where(no_expert, fb_w, w)
            return w / jnp.clip(w.sum(axis=-1, keepdims=True), 1e-08)
        key = jax.random.key(seed)
        ks = jax.random.split(key, 13)
        s = 0.02
        x = jax.random.normal(ks[0], (B, T, D), dtype=jnp.float32)
        Wg = jax.random.normal(ks[1], (E, D, F), dtype=jnp.float32) * s
        Wu = jax.random.normal(ks[2], (E, D, F), dtype=jnp.float32) * s
        Wd = jax.random.normal(ks[3], (E, F, D), dtype=jnp.float32) * s
        Ga = jax.random.normal(ks[4], (NL, D, R), dtype=jnp.float32) * s
        Gb = jax.random.normal(ks[5], (NL, R, F), dtype=jnp.float32) * s
        Ua = jax.random.normal(ks[6], (NL, D, R), dtype=jnp.float32) * s
        Ub = jax.random.normal(ks[7], (NL, R, F), dtype=jnp.float32) * s
        Da = jax.random.normal(ks[8], (NL, F, R), dtype=jnp.float32) * s
        Db = jax.random.normal(ks[9], (NL, R, D), dtype=jnp.float32) * s
        Wr = jax.random.normal(ks[10], (D, E), dtype=jnp.float32) * s
        temperature = jnp.ones((1,), dtype=jnp.float32)
        return {'x': x, 'Wg': Wg, 'Wu': Wu, 'Wd': Wd, 'Ga': Ga, 'Gb': Gb, 'Ua': Ua, 'Ub': Ub, 'Da': Da, 'Db': Db, 'Wr': Wr, 'temperature': temperature}
    _L1_ffn_all = _L1_ffn_setup()
    _L1_ffn_in = {k: v for k, v in _L1_ffn_all.items() if k in ('Wg', 'Wu', 'Wd', 'Ga', 'Gb', 'Ua', 'Ub', 'Da', 'Db', 'Wr', 'temperature')}
    del _L1_ffn_all

    def _L2_attn_setup():
        import jax, jax.numpy as jnp
        import numpy as np
        D_MODEL = 256
        N_HEADS = 16
        HEAD_DIM = D_MODEL // N_HEADS
        B, T = (2, 256)
        key = jax.random.key(seed)
        ks = jax.random.split(key, 9)
        s = 0.02
        x = jax.random.normal(ks[0], (B, T, D_MODEL), dtype=jnp.float32)
        Wq = jax.random.normal(ks[1], (N_HEADS, D_MODEL, HEAD_DIM), dtype=jnp.float32) * s
        bq = jax.random.normal(ks[2], (N_HEADS, HEAD_DIM), dtype=jnp.float32) * s
        Wk = jax.random.normal(ks[3], (N_HEADS, D_MODEL, HEAD_DIM), dtype=jnp.float32) * s
        bk = jax.random.normal(ks[4], (N_HEADS, HEAD_DIM), dtype=jnp.float32) * s
        Wv = jax.random.normal(ks[5], (N_HEADS, D_MODEL, HEAD_DIM), dtype=jnp.float32) * s
        bv = jax.random.normal(ks[6], (N_HEADS, HEAD_DIM), dtype=jnp.float32) * s
        Wo = jax.random.normal(ks[7], (D_MODEL, D_MODEL), dtype=jnp.float32) * s
        bo = jax.random.normal(ks[8], (D_MODEL,), dtype=jnp.float32) * s
        return {'x': x, 'Wq': Wq, 'bq': bq, 'Wk': Wk, 'bk': bk, 'Wv': Wv, 'bv': bv, 'Wo': Wo, 'bo': bo}
    _L2_attn_all = _L2_attn_setup()
    _L2_attn_in = {k: v for k, v in _L2_attn_all.items() if k in ('Wq', 'bq', 'Wk', 'bk', 'Wv', 'bv', 'Wo', 'bo')}
    del _L2_attn_all

    def _L2_xattn_setup():
        import jax, jax.numpy as jnp
        import numpy as np
        B, S, L = (2, 128, 128)
        DIM_Q, H, K, D_C, D_CQ, R = (256, 16, 128, 64, 192, 64)

        def _rope_tables(length, dim):
            inv = 1.0 / 10000.0 ** (jnp.arange(0, dim, 2, dtype=jnp.float32) / dim)
            f = jnp.arange(length, dtype=jnp.float32)[:, None] * inv[None, :]
            sin = jnp.repeat(jnp.sin(f), 2, axis=-1)
            cos = jnp.repeat(jnp.cos(f), 2, axis=-1)
            return (sin, cos)

        def _rotate_half(x):
            half = x.shape[-1] // 2
            return jnp.concatenate([-x[..., half:], x[..., :half]], axis=-1)

        def _apply_rope(x, sin, cos):
            return x * cos + _rotate_half(x) * sin
        key = jax.random.key(seed)
        ks = jax.random.split(key, 8)
        return {'hidden_q': jax.random.normal(ks[0], (B, S, DIM_Q), jnp.float32), 'kv_c': jax.random.normal(ks[1], (B, L, D_C), jnp.float32), 'Wq': jax.random.normal(ks[2], (H * K, DIM_Q), jnp.float32) / np.sqrt(DIM_Q).astype(np.float32), 'w_kc_q': jax.random.normal(ks[3], (H, K, D_CQ), jnp.float32) / np.sqrt(K).astype(np.float32), 'w_kc_kv': jax.random.normal(ks[4], (H, K, D_C), jnp.float32) / np.sqrt(K).astype(np.float32), 'W_qr': jax.random.normal(ks[5], (H, D_CQ, R), jnp.float32) / np.float32(np.sqrt(D_CQ) * np.sqrt(R)), 'W_kr': jax.random.normal(ks[6], (H, D_C, R), jnp.float32) / np.sqrt(D_C).astype(np.float32), 'Wo': jax.random.normal(ks[7], (DIM_Q, H * K), jnp.float32) / np.sqrt(H * K).astype(np.float32)}
    _L2_xattn_all = _L2_xattn_setup()
    _L2_xattn_in = {k: v for k, v in _L2_xattn_all.items() if k in ('Wq', 'w_kc_q', 'w_kc_kv', 'W_qr', 'W_kr', 'Wo')}
    del _L2_xattn_all

    def _L2_ffn_setup():
        import jax, jax.numpy as jnp
        import numpy as np
        B, S, D_IN, D_OUT, E = (4, 128, 256, 256, 32)
        MASK_DENSITY = 0.3
        THRESH = 0.5
        key = jax.random.key(seed)
        k_x, k_w, k_m, k_r = jax.random.split(key, 4)
        x = jax.random.normal(k_x, (B, S, D_IN), dtype=jnp.float32)
        bound = np.sqrt(1.0 / D_IN) * np.sqrt(3.0)
        weight = jax.random.uniform(k_w, (D_OUT, D_IN), minval=-bound, maxval=bound, dtype=jnp.float32)
        scale = jnp.ones((D_OUT,), dtype=jnp.float32)
        expert_masks = (jax.random.uniform(k_m, (E, D_OUT, D_IN)) < MASK_DENSITY).astype(jnp.float32)
        router_w = 0.01 * jax.random.normal(k_r, (E, D_IN), dtype=jnp.float32)
        return {'x': x, 'weight': weight, 'scale': scale, 'expert_masks': expert_masks, 'router_w': router_w}
    _L2_ffn_all = _L2_ffn_setup()
    _L2_ffn_in = {k: v for k, v in _L2_ffn_all.items() if k in ('weight', 'scale', 'expert_masks', 'router_w')}
    del _L2_ffn_all

    def _L3_attn_setup():
        import jax, jax.numpy as jnp
        import numpy as np
        H = 16
        D_NOPE = 128
        D_ROPE = 64
        D_QK = 192
        D_V = 128
        THETA = 10000.0
        EPS = 1e-06

        def rmsnorm(x, w):
            x32 = x.astype(jnp.float32)
            x32 = x32 * jax.lax.rsqrt(jnp.mean(x32 * x32, axis=-1, keepdims=True) + EPS)
            return (x32 * w).astype(x.dtype)

        def rope_cos_sin(seq_len, dim, dtype):
            inv_freq = 1.0 / THETA ** (jnp.arange(0, dim, 2, dtype=jnp.float32) / dim)
            t = jnp.arange(seq_len, dtype=jnp.float32)
            freqs = jnp.outer(t, inv_freq)
            return (jnp.cos(freqs).astype(dtype), jnp.sin(freqs).astype(dtype))

        def apply_rope(x, cos, sin):
            d2 = x.shape[-1] // 2
            x1, x2 = (x[..., :d2], x[..., d2:])
            c = cos[None, :, None, :]
            s = sin[None, :, None, :]
            return jnp.concatenate([x1 * c - x2 * s, x2 * c + x1 * s], axis=-1)
        key = jax.random.key(seed)
        ks = jax.random.split(key, 8)
        B, T, D = (2, 256, 256)
        q_lora, kv_lora = (192, 64)

        def w(k, fan_in, fan_out):
            return jax.random.normal(k, (fan_in, fan_out), dtype=jnp.float32) * (1.0 / np.sqrt(fan_in))
        return {'hidden_states': jax.random.normal(ks[0], (B, T, D), dtype=jnp.float32), 'Wq_a': w(ks[1], D, q_lora), 'q_norm_w': jnp.ones((q_lora,), dtype=jnp.float32), 'Wq_b': w(ks[2], q_lora, H * D_QK), 'Wk_rope': w(ks[3], D, D_ROPE), 'Wkv_a': w(ks[4], D, kv_lora), 'kv_norm_w': jnp.ones((kv_lora,), dtype=jnp.float32), 'Wkv_b': w(ks[5], kv_lora, H * (D_NOPE + D_V)), 'Wo': w(ks[6], H * D_V, D)}
    _L3_attn_all = _L3_attn_setup()
    _L3_attn_in = {k: v for k, v in _L3_attn_all.items() if k in ('Wq_a', 'q_norm_w', 'Wq_b', 'Wk_rope', 'Wkv_a', 'kv_norm_w', 'Wkv_b', 'Wo')}
    del _L3_attn_all

    def _L3_xattn_setup():
        import jax, jax.numpy as jnp
        import numpy as np
        B, S, E = (2, 256, 256)
        QH, KVH = (32, 8)
        D = E // QH
        G = QH // KVH
        DROPOUT = 1.0
        key = jax.random.key(seed)
        k1, k2, k3 = jax.random.split(key, 3)
        q = jax.random.normal(k1, (B, S, E), dtype=jnp.float32)
        k = jax.random.normal(k2, (B, S, E // G), dtype=jnp.float32)
        v = jax.random.normal(k3, (B, S, E // G), dtype=jnp.float32)
        return {'q': q, 'k': k, 'v': v}
    _L3_xattn_all = _L3_xattn_setup()
    _L3_xattn_in = {k: v for k, v in _L3_xattn_all.items() if k in ()}
    del _L3_xattn_all

    def _L3_ffn_setup():
        import jax, jax.numpy as jnp
        import numpy as np
        B, S, D, R, E = (4, 256, 256, 64, 8)
        SCALING = 64.0 / 16.0
        key = jax.random.key(seed)
        k1, k2, k3, k4 = jax.random.split(key, 4)
        x = jax.random.normal(k1, (B, S, D), dtype=jnp.float32)
        A = jax.random.normal(k2, (E, R, D), dtype=jnp.float32) * 0.02
        Bw = jax.random.normal(k3, (E, D, R), dtype=jnp.float32) * 0.02
        Wg = jax.random.normal(k4, (E, D), dtype=jnp.float32) * 0.02
        return {'x': x, 'A': A, 'Bw': Bw, 'Wg': Wg}
    _L3_ffn_all = _L3_ffn_setup()
    _L3_ffn_in = {k: v for k, v in _L3_ffn_all.items() if k in ('A', 'Bw', 'Wg')}
    del _L3_ffn_all
    return {'x': x, 'ctx_512': ctx_512, 'L0_attn_Wq': _L0_attn_in['Wq'], 'L0_attn_Wk': _L0_attn_in['Wk'], 'L0_attn_Wv': _L0_attn_in['Wv'], 'L0_attn_Wb': _L0_attn_in['Wb'], 'L0_attn_Wa': _L0_attn_in['Wa'], 'L0_attn_A_log': _L0_attn_in['A_log'], 'L0_attn_dt_bias': _L0_attn_in['dt_bias'], 'L0_attn_conv_wq': _L0_attn_in['conv_wq'], 'L0_attn_conv_wk': _L0_attn_in['conv_wk'], 'L0_attn_conv_wv': _L0_attn_in['conv_wv'], 'L0_attn_Wg': _L0_attn_in['Wg'], 'L0_attn_norm_w': _L0_attn_in['norm_w'], 'L0_attn_Wo': _L0_attn_in['Wo'], 'L0_ffn_gate_w': _L0_ffn_in['gate_w'], 'L0_ffn_fc1_w': _L0_ffn_in['fc1_w'], 'L0_ffn_fc1_b': _L0_ffn_in['fc1_b'], 'L0_ffn_fc2_w': _L0_ffn_in['fc2_w'], 'L0_ffn_fc2_b': _L0_ffn_in['fc2_b'], 'L0_ffn_alpha': _L0_ffn_in['alpha'], 'L1_attn_Wa': _L1_attn_in['Wa'], 'L1_attn_ba': _L1_attn_in['ba'], 'L1_attn_Wb': _L1_attn_in['Wb'], 'L1_attn_bb': _L1_attn_in['bb'], 'L1_attn_Wout': _L1_attn_in['Wout'], 'L1_attn_bout': _L1_attn_in['bout'], 'L1_xattn_Wq': _L1_xattn_in['Wq'], 'L1_xattn_w_kc_q': _L1_xattn_in['w_kc_q'], 'L1_xattn_w_kc_kv': _L1_xattn_in['w_kc_kv'], 'L1_xattn_W_qr': _L1_xattn_in['W_qr'], 'L1_xattn_W_kr': _L1_xattn_in['W_kr'], 'L1_xattn_Wo': _L1_xattn_in['Wo'], 'L1_ffn_Wg': _L1_ffn_in['Wg'], 'L1_ffn_Wu': _L1_ffn_in['Wu'], 'L1_ffn_Wd': _L1_ffn_in['Wd'], 'L1_ffn_Ga': _L1_ffn_in['Ga'], 'L1_ffn_Gb': _L1_ffn_in['Gb'], 'L1_ffn_Ua': _L1_ffn_in['Ua'], 'L1_ffn_Ub': _L1_ffn_in['Ub'], 'L1_ffn_Da': _L1_ffn_in['Da'], 'L1_ffn_Db': _L1_ffn_in['Db'], 'L1_ffn_Wr': _L1_ffn_in['Wr'], 'L1_ffn_temperature': _L1_ffn_in['temperature'], 'L2_attn_Wq': _L2_attn_in['Wq'], 'L2_attn_bq': _L2_attn_in['bq'], 'L2_attn_Wk': _L2_attn_in['Wk'], 'L2_attn_bk': _L2_attn_in['bk'], 'L2_attn_Wv': _L2_attn_in['Wv'], 'L2_attn_bv': _L2_attn_in['bv'], 'L2_attn_Wo': _L2_attn_in['Wo'], 'L2_attn_bo': _L2_attn_in['bo'], 'L2_xattn_Wq': _L2_xattn_in['Wq'], 'L2_xattn_w_kc_q': _L2_xattn_in['w_kc_q'], 'L2_xattn_w_kc_kv': _L2_xattn_in['w_kc_kv'], 'L2_xattn_W_qr': _L2_xattn_in['W_qr'], 'L2_xattn_W_kr': _L2_xattn_in['W_kr'], 'L2_xattn_Wo': _L2_xattn_in['Wo'], 'L2_ffn_weight': _L2_ffn_in['weight'], 'L2_ffn_scale': _L2_ffn_in['scale'], 'L2_ffn_expert_masks': _L2_ffn_in['expert_masks'], 'L2_ffn_router_w': _L2_ffn_in['router_w'], 'L3_attn_Wq_a': _L3_attn_in['Wq_a'], 'L3_attn_q_norm_w': _L3_attn_in['q_norm_w'], 'L3_attn_Wq_b': _L3_attn_in['Wq_b'], 'L3_attn_Wk_rope': _L3_attn_in['Wk_rope'], 'L3_attn_Wkv_a': _L3_attn_in['Wkv_a'], 'L3_attn_kv_norm_w': _L3_attn_in['kv_norm_w'], 'L3_attn_Wkv_b': _L3_attn_in['Wkv_b'], 'L3_attn_Wo': _L3_attn_in['Wo'], 'L3_ffn_A': _L3_ffn_in['A'], 'L3_ffn_Bw': _L3_ffn_in['Bw'], 'L3_ffn_Wg': _L3_ffn_in['Wg']}

def reference(x, ctx_512, L0_attn_Wq, L0_attn_Wk, L0_attn_Wv, L0_attn_Wb, L0_attn_Wa, L0_attn_A_log, L0_attn_dt_bias, L0_attn_conv_wq, L0_attn_conv_wk, L0_attn_conv_wv, L0_attn_Wg, L0_attn_norm_w, L0_attn_Wo, L0_ffn_gate_w, L0_ffn_fc1_w, L0_ffn_fc1_b, L0_ffn_fc2_w, L0_ffn_fc2_b, L0_ffn_alpha, L1_attn_Wa, L1_attn_ba, L1_attn_Wb, L1_attn_bb, L1_attn_Wout, L1_attn_bout, L1_xattn_Wq, L1_xattn_w_kc_q, L1_xattn_w_kc_kv, L1_xattn_W_qr, L1_xattn_W_kr, L1_xattn_Wo, L1_ffn_Wg, L1_ffn_Wu, L1_ffn_Wd, L1_ffn_Ga, L1_ffn_Gb, L1_ffn_Ua, L1_ffn_Ub, L1_ffn_Da, L1_ffn_Db, L1_ffn_Wr, L1_ffn_temperature, L2_attn_Wq, L2_attn_bq, L2_attn_Wk, L2_attn_bk, L2_attn_Wv, L2_attn_bv, L2_attn_Wo, L2_attn_bo, L2_xattn_Wq, L2_xattn_w_kc_q, L2_xattn_w_kc_kv, L2_xattn_W_qr, L2_xattn_W_kr, L2_xattn_Wo, L2_ffn_weight, L2_ffn_scale, L2_ffn_expert_masks, L2_ffn_router_w, L3_attn_Wq_a, L3_attn_q_norm_w, L3_attn_Wq_b, L3_attn_Wk_rope, L3_attn_Wkv_a, L3_attn_kv_norm_w, L3_attn_Wkv_b, L3_attn_Wo, L3_ffn_A, L3_ffn_Bw, L3_ffn_Wg):
    import jax
    import jax.numpy as jnp

    def _L0_attn_ref(hidden_states, Wq, Wk, Wv, Wb, Wa, A_log, dt_bias, conv_wq, conv_wk, conv_wv, Wg, norm_w, Wo):
        import jax, jax.numpy as jnp
        import numpy as np
        H, DK, DV = (6, 32, 64)
        HID = 256
        CONV = 4
        NORM_EPS = 1e-05

        def causal_dwconv_silu(x, w):
            K = w.shape[1]
            xp = jnp.pad(x, ((0, 0), (K - 1, 0), (0, 0)))
            y = jax.lax.conv_general_dilated(jnp.transpose(xp, (0, 2, 1)), w[:, None, :], (1,), 'VALID', feature_group_count=w.shape[0])
            return jax.nn.silu(jnp.transpose(y, (0, 2, 1)))

        def l2norm(x, eps=1e-06):
            return x * jax.lax.rsqrt(jnp.sum(x * x, axis=-1, keepdims=True) + eps)
        x = hidden_states
        B, T, _ = x.shape
        q = causal_dwconv_silu(x @ Wq.T, conv_wq).reshape(B, T, H, DK)
        k = causal_dwconv_silu(x @ Wk.T, conv_wk).reshape(B, T, H, DK)
        v = causal_dwconv_silu(x @ Wv.T, conv_wv).reshape(B, T, H, DV)
        beta = jax.nn.sigmoid(x @ Wb.T)
        g = -jnp.exp(A_log) * jax.nn.softplus(x @ Wa.T + dt_bias)
        q = l2norm(q) * DK ** (-0.5)
        k = l2norm(k)

        def step(S, inp):
            qt, kt, vt, gt, bt = inp
            S = S * jnp.exp(gt)[..., None, None]
            v_new = vt - jnp.einsum('bhk,bhkv->bhv', kt, S)
            S = S + bt[..., None, None] * (kt[..., :, None] * v_new[..., None, :])
            o = jnp.einsum('bhk,bhkv->bhv', qt, S)
            return (S, o)
        S0 = jnp.zeros((B, H, DK, DV), x.dtype)
        tm = lambda a: jnp.moveaxis(a, 1, 0)
        _, o = jax.lax.scan(step, S0, (tm(q), tm(k), tm(v), tm(g), tm(beta)))
        o = jnp.moveaxis(o, 0, 1)
        var = jnp.mean(jnp.square(o.astype(jnp.float32)), axis=-1, keepdims=True)
        o = o * jax.lax.rsqrt(var + NORM_EPS).astype(o.dtype) * norm_w
        gate = (x @ Wg.T).reshape(B, T, H, DV)
        o = o * jax.nn.silu(gate)
        return o.reshape(B, T, H * DV) @ Wo.T

    def _L0_xattn_ref(q, k, v):
        import jax, jax.numpy as jnp
        import numpy as np
        import math
        NUM_Q_HEADS = 32
        NUM_KV_HEADS = 8
        B, S, E = q.shape
        H, KV = (NUM_Q_HEADS, NUM_KV_HEADS)
        D = E // H
        G = H // KV
        scale = math.sqrt(D)
        qh = q.reshape(B, S, KV, G, D).transpose(0, 2, 3, 1, 4)
        kh = k.reshape(B, S, KV, D).transpose(0, 2, 1, 3)
        vh = v.reshape(B, S, KV, D).transpose(0, 2, 1, 3)
        scores = jnp.einsum('bkgsd,bktd->bkgst', qh, kh) / scale
        weights = jax.nn.softmax(scores, axis=-1)
        out = jnp.einsum('bkgst,bktd->bkgsd', weights, vh)
        return out.transpose(0, 3, 1, 2, 4).reshape(B, S, E)

    def _L0_ffn_ref(hidden_states, gate_w, fc1_w, fc1_b, fc2_w, fc2_b, alpha):
        import jax, jax.numpy as jnp
        import numpy as np
        NUM_EXPERTS = 8
        HIDDEN = 256
        INTER = 256
        TOP_K = 2
        B, S, H = hidden_states.shape
        x = hidden_states.reshape(-1, H)
        probs = jax.nn.softmax(x @ gate_w, axis=-1)
        gate_score, gate_idx = jax.lax.top_k(probs, TOP_K)
        gate_score = gate_score / jnp.sum(gate_score, axis=-1, keepdims=True)
        onehot = jax.nn.one_hot(gate_idx, NUM_EXPERTS, dtype=x.dtype)
        combine = jnp.einsum('tk,tke->te', gate_score, onehot) * alpha[None, :]
        h = jnp.einsum('th,ehi->eti', x, fc1_w) + fc1_b[:, None, :]
        h = jax.nn.gelu(h, approximate=False)
        y = jnp.einsum('eti,eih->eth', h, fc2_w) + fc2_b[:, None, :]
        out = jnp.einsum('eth,te->th', y, combine)
        return out.reshape(B, S, H)

    def _L1_attn_ref(x, Wa, ba, Wb, bb, Wout, bout):
        import jax, jax.numpy as jnp
        import numpy as np
        B, T, D, S = (8, 512, 256, 64)
        a = jnp.tanh(jnp.einsum('btd,sd->bts', x, Wa) + ba)
        b = jnp.tanh(jnp.einsum('btd,sd->bts', x, Wb) + bb)

        def step(h, ab):
            at, bt = ab
            h = at * h + bt
            return (h, h)
        h0 = jnp.zeros((x.shape[0], Wa.shape[0]), x.dtype)
        _, hs = jax.lax.scan(step, h0, (jnp.swapaxes(a, 0, 1), jnp.swapaxes(b, 0, 1)))
        hs = jnp.swapaxes(hs, 0, 1)
        return x + jnp.einsum('bts,ds->btd', hs, Wout) + bout

    def _L1_xattn_ref(hidden_q, kv_c, Wq, w_kc_q, w_kc_kv, W_qr, W_kr, Wo):
        import jax, jax.numpy as jnp
        import numpy as np
        B, S, L = (2, 128, 128)
        DIM_Q, H, K, D_C, D_CQ, R = (256, 16, 128, 64, 192, 64)

        def _rope_tables(seq_len, dim, dtype):
            inv_freq = 1.0 / 10000.0 ** (jnp.arange(0, dim, 2, dtype=dtype) / dim)
            t = jnp.arange(seq_len, dtype=dtype)
            freqs = t[:, None] * inv_freq[None, :]
            sin = jnp.repeat(jnp.sin(freqs), 2, axis=-1)
            cos = jnp.repeat(jnp.cos(freqs), 2, axis=-1)
            return (sin, cos)

        def _rotate_half(x):
            h = x.shape[-1] // 2
            return jnp.concatenate([-x[..., h:], x[..., :h]], axis=-1)
        b, s, _ = hidden_q.shape
        l = kv_c.shape[1]
        q_hk = (hidden_q @ Wq.T).reshape(b, s, H, K)
        q_big = jnp.einsum('bshk,hkq->bshq', q_hk, w_kc_q)
        sin, cos = _rope_tables(l, D_C, kv_c.dtype)
        kv_rope = kv_c * cos[None] + _rotate_half(kv_c) * sin[None]
        q_r = jnp.einsum('bshq,hqr->bhsr', q_big, W_qr)
        k_r = jnp.einsum('bld,hdr->bhlr', kv_rope, W_kr)
        scores = jnp.einsum('bhsr,bhlr->bhsl', q_r, k_r)
        attn = jax.nn.softmax(scores, axis=-1)
        ctx_c = jnp.einsum('bhsl,bld->bhsd', attn, kv_rope)
        ctx_lat = jnp.einsum('bhsd,hkd->bshk', ctx_c, w_kc_kv)
        out = ctx_lat.reshape(b, s, H * K) @ Wo.T
        return out

    def _L1_ffn_ref(x, Wg, Wu, Wd, Ga, Gb, Ua, Ub, Da, Db, Wr, temperature):
        import jax, jax.numpy as jnp
        import numpy as np
        import math
        GOLDEN_CENTER = 1.0 / math.e
        GOLDEN_LOWER = 0.5 - math.log(4.0 / 3.0)
        GOLDEN_UPPER = 0.5
        B, T, D = (4, 128, 256)
        E = 8
        F = 1024 // (E // 2)
        R = 64
        NL = 2

        def _router_weights(x, Wr, temperature):
            logits = jnp.einsum('btd,de->bte', x, Wr)
            inhibition = jax.nn.sigmoid(logits / temperature)
            in_zone = (inhibition >= GOLDEN_LOWER) & (inhibition <= GOLDEN_UPPER)
            distance = jnp.abs(inhibition - GOLDEN_CENTER)
            w = jnp.exp(-distance / 0.1) * in_zone.astype(x.dtype)
            wsum = w.sum(axis=-1, keepdims=True)
            no_expert = wsum < 1e-08
            fb = jnp.exp(-distance / 0.3)
            _, top2 = jax.lax.top_k(fb, 2)
            fb_mask = jax.nn.one_hot(top2, E, dtype=x.dtype).sum(axis=-2)
            fb_w = fb * fb_mask
            fb_w = fb_w / jnp.clip(fb_w.sum(axis=-1, keepdims=True), 1e-08)
            w = jnp.where(no_expert, fb_w, w)
            return w / jnp.clip(w.sum(axis=-1, keepdims=True), 1e-08)
        weights = _router_weights(x, Wr, temperature)
        gate = jnp.einsum('btd,edf->ebtf', x, Wg)
        up = jnp.einsum('btd,edf->ebtf', x, Wu)
        gate = gate.at[:NL].add(jnp.einsum('btd,edr,erf->ebtf', x, Ga, Gb))
        up = up.at[:NL].add(jnp.einsum('btd,edr,erf->ebtf', x, Ua, Ub))
        mid = jax.nn.silu(gate) * up
        out = jnp.einsum('ebtf,efd->ebtd', mid, Wd)
        out = out.at[:NL].add(jnp.einsum('ebtf,efr,erd->ebtd', mid[:NL], Da, Db))
        return jnp.einsum('bte,ebtd->btd', weights, out)

    def _L2_attn_ref(x, Wq, bq, Wk, bk, Wv, bv, Wo, bo):
        import jax, jax.numpy as jnp
        import numpy as np
        D_MODEL = 256
        N_HEADS = 16
        HEAD_DIM = D_MODEL // N_HEADS
        B, T = (2, 256)
        Bn, Tn, C = x.shape
        H, _, D = Wq.shape
        scale = D ** (-0.5)
        q = jnp.einsum('btc,hcd->bhtd', x, Wq) + bq[None, :, None, :]
        k = jnp.einsum('btc,hcd->bhtd', x, Wk) + bk[None, :, None, :]
        v = jnp.einsum('btc,hcd->bhtd', x, Wv) + bv[None, :, None, :]
        scores = jnp.einsum('bhtd,bhsd->bhts', q, k) * scale
        neg = jnp.finfo(scores.dtype).min
        causal = jnp.triu(jnp.full((Tn, Tn), neg, dtype=scores.dtype), k=1)
        probs = jax.nn.softmax(scores + causal, axis=-1)
        y = jnp.einsum('bhts,bhsd->bhtd', probs, v)
        y = y.transpose(0, 2, 1, 3).reshape(Bn, Tn, H * D)
        return y @ Wo + bo

    def _L2_xattn_ref(hidden_q, kv_c, Wq, w_kc_q, w_kc_kv, W_qr, W_kr, Wo):
        import jax, jax.numpy as jnp
        import numpy as np
        B, S, L = (2, 128, 128)
        DIM_Q, H, K, D_C, D_CQ, R = (256, 16, 128, 64, 192, 64)

        def _rope_tables(length, dim):
            inv = 1.0 / 10000.0 ** (jnp.arange(0, dim, 2, dtype=jnp.float32) / dim)
            f = jnp.arange(length, dtype=jnp.float32)[:, None] * inv[None, :]
            sin = jnp.repeat(jnp.sin(f), 2, axis=-1)
            cos = jnp.repeat(jnp.cos(f), 2, axis=-1)
            return (sin, cos)

        def _rotate_half(x):
            half = x.shape[-1] // 2
            return jnp.concatenate([-x[..., half:], x[..., :half]], axis=-1)

        def _apply_rope(x, sin, cos):
            return x * cos + _rotate_half(x) * sin
        Bv, Sv, _ = hidden_q.shape
        _, Lv, _ = kv_c.shape
        q_hk = (hidden_q @ Wq.T).reshape(Bv, Sv, H, K)
        q_big = jnp.einsum('bshk,hkq->bshq', q_hk, w_kc_q)
        sin_q, cos_q = _rope_tables(Sv, D_CQ)
        q_big = _apply_rope(q_big, sin_q[None, :, None, :], cos_q[None, :, None, :])
        sin_k, cos_k = _rope_tables(Lv, D_C)
        kv_r = _apply_rope(kv_c, sin_k[None], cos_k[None])
        q_r = jnp.einsum('bshq,hqr->bhsr', q_big, W_qr)
        k_r = jnp.einsum('bld,hdr->bhlr', kv_r, W_kr)
        scores = jnp.einsum('bhsr,bhlr->bhsl', q_r, k_r)
        attn = jax.nn.softmax(scores, axis=-1)
        ctx_c = jnp.einsum('bhsl,bld->bhsd', attn, kv_r)
        ctx_lat = jnp.einsum('bhsd,hkd->bhsk', ctx_c, w_kc_kv)
        ctx = ctx_lat.transpose(0, 2, 1, 3).reshape(Bv, Sv, H * K)
        return ctx @ Wo.T

    def _L2_ffn_ref(x, weight, scale, expert_masks, router_w):
        import jax, jax.numpy as jnp
        import numpy as np
        B, S, D_IN, D_OUT, E = (4, 128, 256, 256, 32)
        MASK_DENSITY = 0.3
        THRESH = 0.5
        logits = jnp.einsum('bsd,ed->bse', x, router_w)
        probs = jax.nn.softmax(logits, axis=-1)
        top1_w = jnp.max(probs, axis=-1)
        top1_idx = jnp.argmax(probs, axis=-1)
        w_q = jnp.clip(jnp.round(weight / THRESH), -1.0, 1.0)
        w_scaled = w_q * scale[:, None]
        out0 = jnp.zeros((x.shape[0], x.shape[1], weight.shape[0]), dtype=x.dtype)

        def body(out, inputs):
            e_idx, mask_e = inputs
            y = jnp.einsum('bsi,oi->bso', x, w_scaled * mask_e)
            sel = (top1_idx == e_idx)[..., None]
            out = jnp.where(sel, y * top1_w[..., None], out)
            return (out, None)
        out, _ = jax.lax.scan(body, out0, (jnp.arange(E), expert_masks))
        return out

    def _L3_attn_ref(hidden_states, Wq_a, q_norm_w, Wq_b, Wk_rope, Wkv_a, kv_norm_w, Wkv_b, Wo):
        import jax, jax.numpy as jnp
        import numpy as np
        H = 16
        D_NOPE = 128
        D_ROPE = 64
        D_QK = 192
        D_V = 128
        THETA = 10000.0
        EPS = 1e-06

        def rmsnorm(x, w):
            x32 = x.astype(jnp.float32)
            x32 = x32 * jax.lax.rsqrt(jnp.mean(x32 * x32, axis=-1, keepdims=True) + EPS)
            return (x32 * w).astype(x.dtype)

        def rope_cos_sin(seq_len, dim, dtype):
            inv_freq = 1.0 / THETA ** (jnp.arange(0, dim, 2, dtype=jnp.float32) / dim)
            t = jnp.arange(seq_len, dtype=jnp.float32)
            freqs = jnp.outer(t, inv_freq)
            return (jnp.cos(freqs).astype(dtype), jnp.sin(freqs).astype(dtype))

        def apply_rope(x, cos, sin):
            d2 = x.shape[-1] // 2
            x1, x2 = (x[..., :d2], x[..., d2:])
            c = cos[None, :, None, :]
            s = sin[None, :, None, :]
            return jnp.concatenate([x1 * c - x2 * s, x2 * c + x1 * s], axis=-1)
        B, T, D = hidden_states.shape
        q = rmsnorm(hidden_states @ Wq_a, q_norm_w) @ Wq_b
        q = q.reshape(B, T, H, D_QK)
        q_pass, q_rot = (q[..., :D_NOPE], q[..., D_NOPE:])
        kv = rmsnorm(hidden_states @ Wkv_a, kv_norm_w) @ Wkv_b
        kv = kv.reshape(B, T, H, D_NOPE + D_V)
        k_pass, v = (kv[..., :D_NOPE], kv[..., D_NOPE:])
        k_rot = (hidden_states @ Wk_rope)[:, :, None, :]
        cos, sin = rope_cos_sin(T, D_ROPE, hidden_states.dtype)
        q_rot = apply_rope(q_rot, cos, sin)
        k_rot = apply_rope(k_rot, cos, sin)
        k_rot = jnp.broadcast_to(k_rot, (B, T, H, D_ROPE))
        qf = jnp.concatenate([q_pass, q_rot], axis=-1)
        kf = jnp.concatenate([k_pass, k_rot], axis=-1)
        scale = 1.0 / np.sqrt(D_QK)
        scores = jnp.einsum('bqhd,bkhd->bhqk', qf, kf) * scale
        mask = jnp.tril(jnp.ones((T, T), dtype=bool))
        scores = jnp.where(mask[None, None], scores, jnp.finfo(scores.dtype).min)
        p = jax.nn.softmax(scores, axis=-1)
        o = jnp.einsum('bhqk,bkhd->bqhd', p, v)
        o = o.reshape(B, T, H * D_V) @ Wo
        return o

    def _L3_xattn_ref(q, k, v):
        import jax, jax.numpy as jnp
        import numpy as np
        B, S, E = (2, 256, 256)
        QH, KVH = (32, 8)
        D = E // QH
        G = QH // KVH
        DROPOUT = 1.0
        b, s, _ = q.shape
        qh = q.reshape(b, s, KVH, G, D).transpose(0, 2, 3, 1, 4)
        kh = k.reshape(b, s, KVH, D).transpose(0, 2, 1, 3)
        vh = v.reshape(b, s, KVH, D).transpose(0, 2, 1, 3)
        scale = 1.0 / jnp.sqrt(jnp.float32(D))
        scores = jnp.einsum('bkgsd,bktd->bkgst', qh, kh) * scale
        attn = jax.nn.softmax(scores, axis=-1) / DROPOUT
        out = jnp.einsum('bkgst,bktd->bkgsd', attn, vh)
        return out.transpose(0, 3, 1, 2, 4).reshape(b, s, E)

    def _L3_ffn_ref(x, A, Bw, Wg):
        import jax, jax.numpy as jnp
        import numpy as np
        B, S, D, R, E = (4, 256, 256, 64, 8)
        SCALING = 64.0 / 16.0
        bsz, seq_len, dim = x.shape
        xf = x.reshape(-1, dim)
        logits = jnp.einsum('nd,ed->ne', xf, Wg)
        prob = jax.nn.softmax(logits, axis=-1)
        gate = jnp.argmax(prob, axis=-1)
        prob_sel = jnp.take_along_axis(prob, gate[:, None], axis=1)
        mask = jax.nn.one_hot(gate, E, dtype=xf.dtype)
        h = jnp.einsum('nd,erd->ner', xf, A)
        h = h * mask[:, :, None]
        y = jnp.einsum('ner,eor->no', h, Bw)
        y = y * SCALING * prob_sel
        return y.reshape(bsz, seq_len, -1)
    x = x + _L0_attn_ref(_layernorm(x, axis=-1), L0_attn_Wq, L0_attn_Wk, L0_attn_Wv, L0_attn_Wb, L0_attn_Wa, L0_attn_A_log, L0_attn_dt_bias, L0_attn_conv_wq, L0_attn_conv_wk, L0_attn_conv_wv, L0_attn_Wg, L0_attn_norm_w, L0_attn_Wo)
    x = x + _L0_xattn_ref(_layernorm(x, axis=-1), ctx_512, ctx_512)
    x = x + _L0_ffn_ref(_layernorm(x, axis=-1), L0_ffn_gate_w, L0_ffn_fc1_w, L0_ffn_fc1_b, L0_ffn_fc2_w, L0_ffn_fc2_b, L0_ffn_alpha)
    x = x + _L1_attn_ref(_layernorm(x, axis=-1), L1_attn_Wa, L1_attn_ba, L1_attn_Wb, L1_attn_bb, L1_attn_Wout, L1_attn_bout)
    x = x + _L1_xattn_ref(_layernorm(x, axis=-1), ctx_512, L1_xattn_Wq, L1_xattn_w_kc_q, L1_xattn_w_kc_kv, L1_xattn_W_qr, L1_xattn_W_kr, L1_xattn_Wo)
    x = x + _L1_ffn_ref(_layernorm(x, axis=-1), L1_ffn_Wg, L1_ffn_Wu, L1_ffn_Wd, L1_ffn_Ga, L1_ffn_Gb, L1_ffn_Ua, L1_ffn_Ub, L1_ffn_Da, L1_ffn_Db, L1_ffn_Wr, L1_ffn_temperature)
    x = x + _L2_attn_ref(_layernorm(x, axis=-1), L2_attn_Wq, L2_attn_bq, L2_attn_Wk, L2_attn_bk, L2_attn_Wv, L2_attn_bv, L2_attn_Wo, L2_attn_bo)
    x = x + _L2_xattn_ref(_layernorm(x, axis=-1), ctx_512, L2_xattn_Wq, L2_xattn_w_kc_q, L2_xattn_w_kc_kv, L2_xattn_W_qr, L2_xattn_W_kr, L2_xattn_Wo)
    x = x + _L2_ffn_ref(_layernorm(x, axis=-1), L2_ffn_weight, L2_ffn_scale, L2_ffn_expert_masks, L2_ffn_router_w)
    x = x + _L3_attn_ref(_layernorm(x, axis=-1), L3_attn_Wq_a, L3_attn_q_norm_w, L3_attn_Wq_b, L3_attn_Wk_rope, L3_attn_Wkv_a, L3_attn_kv_norm_w, L3_attn_Wkv_b, L3_attn_Wo)
    x = x + _L3_xattn_ref(_layernorm(x, axis=-1), ctx_512, ctx_512)
    x = x + _L3_ffn_ref(_layernorm(x, axis=-1), L3_ffn_A, L3_ffn_Bw, L3_ffn_Wg)
    return x

_drawn_inputs = setup_inputs


def setup_inputs(seed=0):
    import zlib

    import numpy as np

    out = dict(_drawn_inputs(seed))
    spreads = {'L0_attn_norm_w': (1.0, 0.2),
     'L0_ffn_fc1_b': (0.0, 0.8),
     'L0_ffn_fc2_b': (0.0, 0.1),
     'L2_ffn_scale': (1.0, 0.2),
     'L3_attn_q_norm_w': (1.0, 0.6),
     'L3_attn_kv_norm_w': (1.0, 0.6)}
    factors = {'L0_attn_dt_bias': 6.418,
     'L1_attn_ba': 8.0,
     'L1_attn_bb': 8.0,
     'L1_ffn_Wg': 8.0,
     'L1_ffn_Wu': 8.0,
     'L1_ffn_Wd': 8.0,
     'L1_ffn_Ga': 8.0,
     'L1_ffn_Gb': 8.0,
     'L1_ffn_Ua': 8.0,
     'L1_ffn_Ub': 8.0,
     'L1_ffn_Da': 8.0,
     'L1_ffn_Db': 8.0,
     'L1_ffn_Wr': 8.0,
     'L2_attn_Wq': 8.0,
     'L2_attn_bq': 58.428,
     'L2_attn_Wk': 8.0,
     'L2_attn_bk': 64.0,
     'L2_attn_Wv': 2.997,
     'L2_attn_bv': 34.952,
     'L2_attn_Wo': 2.921,
     'L2_attn_bo': 48.374,
     'L3_ffn_A': 5.042,
     'L3_ffn_Bw': 4.978,
     'L3_ffn_Wg': 5.307,
     'L2_xattn_Wq': 4.96,
     'L2_xattn_w_kc_q': 4.564,
     'L2_xattn_W_qr': 4.151,
     'L2_xattn_W_kr': 4.931,
     'L3_attn_Wk_rope': 3.663}
    for name, (base, spread) in spreads.items():
        noise = np.random.default_rng([zlib.crc32(name.encode()), seed]).standard_normal(out[name].shape)
        drawn = base * np.exp(spread * noise) if base else spread * noise
        out[name] = jnp.asarray(drawn.astype(out[name].dtype))
    for name, factor in factors.items():
        out[name] = (out[name] * factor).astype(out[name].dtype)
    return out
```

```python
from contextlib import ExitStack, contextmanager

import concourse.bass as bass
from concourse import mybir

P = 128
BATCH, SEQ, D = 16, 64, 256
TOK = BATCH * SEQ
NT = TOK // P
KC = D // P
BANK = 512
EPS_LN = 1e-5

ALU = mybir.AluOpType
ACT = mybir.ActivationFunctionType
AX = mybir.AxisListType
F32 = mybir.dt.float32
BF16 = mybir.dt.bfloat16
U32 = mybir.dt.uint32

W_COLS = 16384
STAGES = list(range(12))


class Region:

    def __init__(self, tensor, cols):
        self.tensor, self.cols, self.at = tensor, cols, 0

    def take(self, *dims, rows=P, dt=F32):
        n = 1
        for d in dims:
            n *= d
        words = n if dt == F32 or dt == U32 else (n + 1) // 2
        assert self.at + words <= self.cols, (self.at, words, self.cols)
        ap = self.tensor[0:rows, self.at:self.at + words]
        self.at += words
        if dt != F32:
            ap = ap.bitcast(dt)
        if len(dims) > 1:
            names = "abcde"[:len(dims)]
            ap = ap.rearrange("p (" + " ".join(names) + ") -> p " + " ".join(names),
                              **{c: d for c, d in zip(names[1:], dims[1:])})
        return ap

    def clear(self):
        self.at = 0


class Named:
    pass


class Kit:

    @contextmanager
    def stage(self, *names):
        nc = self.nc
        self.serial += 1
        named = {n: nc.alloc_semaphore(f"{n}_{self.serial}") for n in names}
        if self.former:
            nc.clear_and_free_semaphores(self.former)
        self.former = list(named.values())
        with nc.Block() as block:
            yield block, named



class Chain:

    def __init__(self, eng, sem):
        self.eng, self.sem, self.n = eng, sem, 0

    def step(self, ins):
        self.n += 1
        ins.then_inc(self.sem, 1)
        self.eng.wait_ge(self.sem, self.n)

    def add(self, ins):
        self.n += 1
        ins.then_inc(self.sem, 1)

    def settle(self):
        self.eng.wait_ge(self.sem, self.n)


def bc(ap, dim, n):
    lst = [list(p) for p in ap.ap]
    lst.insert(dim, [0, n])
    return bass.AP(tensor=ap.tensor, offset=ap.offset, ap=lst)



def constants(k):
    nc = k.nc
    causal = k.h.rearrange("p j d -> p (j d)")[:, 0:NT * SEQ]
    with k.stage("zeroed", "ident", "x_in", "causal_in", "halves") as (block, s):
        @block.sync
        def _(sp):
            sp.dma_start(k.x, k.dram["x"].rearrange("b t d -> (b t) d").rearrange("(j p) d -> p j d", p=P)).then_inc(s["x_in"], 16)
            sp.dma_start(causal, k.dram["const_causal"]).then_inc(s["causal_in"], 16)
            sp.dma_start(k.rev, k.dram["const_rev"]).then_inc(s["x_in"], 16)
            sp.wait_ge(s["x_in"], 32)

        @block.vector
        def _(dve):
            dve.wait_ge(s["causal_in"], 16)
            nc.vector.tensor_copy(k.causal, causal).then_inc(s["halves"], 1)
            dve.wait_ge(s["ident"], 1)
            nc.vector.tensor_copy(k.ident16, k.ident).then_inc(s["halves"], 1)

        @block.gpsimd
        def _(pool):
            nc.gpsimd.memset(k.ident, 0.0).then_inc(s["zeroed"], 1)
            pool.wait_ge(s["zeroed"], 1)
            nc.gpsimd.affine_select(out=k.ident, in_=k.ident, compare_op=ALU.not_equal, fill=1.0, base=0,
                                    pattern=[[-1, P]], channel_multiplier=1).then_inc(s["ident"], 1)



def layernorm(k, eps=EPS_LN):
    nc, x, h, hT, ps = k.nc, k.x, k.h, k.hT, k.ps
    k.work.clear()
    stats = k.work.take(NT, 6)
    mv = k.work.take(NT, 2)
    std = k.work.take(NT)
    rstd = k.work.take(NT)
    with k.stage("stats", "aggr", "veps", "std", "rstd", "normed", "turned", "hT") as (block, s):
        @block.vector
        def _(dve):
            for j in range(NT):
                nc.vector.bn_stats(stats[:, j, :], x[:, j, :]).then_inc(s["stats"], 1)
            for j in range(NT):
                dve.wait_ge(s["stats"], j + 1)
                nc.vector.bn_aggr(mv[:, j, :], stats[:, j, :]).then_inc(s["aggr"], 1)
            dve.wait_ge(s["aggr"], NT)
            nc.vector.tensor_scalar(std, mv[:, :, 1], eps, None, ALU.add).then_inc(s["veps"], 1)
            dve.wait_ge(s["std"], 1)
            nc.vector.reciprocal(rstd, std).then_inc(s["rstd"], 1)
            dve.wait_ge(s["rstd"], 1)
            for j in range(NT):
                nc.vector.tensor_scalar(h[:, j, :], x[:, j, :], mv[:, j, 0:1], rstd[:, j:j + 1],
                                        ALU.subtract, ALU.mult).then_inc(s["normed"], 1)

        @block.tensor
        def _(pe):
            for j in range(NT):
                pe.wait_ge(s["normed"], j + 1)
                for c in range(KC):
                    at = (j % 4) * P
                    last = nc.tensor.transpose(ps[:, (j // 4) * KC + c, at:at + P], h[:, j, c * P:(c + 1) * P], k.ident)
                last.then_inc(s["turned"], 1)

        @block.scalar
        def _(act):
            act.wait_ge(s["veps"], 1)
            nc.scalar.activation(std, std, ACT.Sqrt).then_inc(s["std"], 1)
            for half in range(2):
                act.wait_ge(s["turned"], 4 * half + 4)
                for c in range(KC):
                    nc.scalar.copy(hT[:, c, half * BANK:(half + 1) * BANK], ps[:, half * KC + c, :]).then_inc(s["hT"], 1)



def load_L1_attn(k, w, sem):
    d, eng = k.dram, k.nc.sync
    w.wab = w.region.take(KC, P)
    w.wout = w.region.take(D, rows=64)
    w.bias = w.region.take(2, rows=64)
    w.bout = w.region.take(D)
    eng.dma_start(w.wab, d["L1_attn_WabT"].rearrange("(c p) s -> p c s", p=P)).then_inc(sem, 16)
    eng.dma_start(w.wout, d["L1_attn_WoutT"]).then_inc(sem, 16)
    eng.dma_start(w.bias, d["L1_attn_bab"]).then_inc(sem, 16)
    eng.dma_start(w.bout, row_on_all(d["L1_attn_bout"])).then_inc(sem, 16)
    return 64


def row_on_all(ap, n=P):
    return bass.AP(tensor=ap.tensor, offset=ap.offset, ap=[[0, n]] + [list(p) for p in ap.ap])


def stage_L1_attn(k, w):
    nc, ps = k.nc, k.ps
    k.work.clear()
    a = k.work.take(TOK, rows=64)
    b = k.work.take(TOK, rows=64)
    hs = k.work.take(TOK, rows=64)
    S = 64
    with k.stage("proj", "tanh", "cut", "scan", "out", "hb", "xh", "xs") as (block, s):
        @block.tensor
        def _(pe):
            pe.wait_ge(w.sem, w.loaded)
            for g in range(2):
                for half in range(2):
                    for c in range(KC):
                        last = nc.tensor.matmul(ps[0:S, 2 * g + half, :], w.wab[:, c, g * S:(g + 1) * S],
                                                k.hT[:, c, half * BANK:(half + 1) * BANK], start=c == 0, stop=c == KC - 1)
                last.then_inc(s["proj"], 1)
            pe.wait_ge(s["scan"], 1)
            for j in range(NT):
                last = nc.tensor.matmul(ps[:, 4 + j // 2, (j % 2) * D:(j % 2 + 1) * D], hs[:, j * P:(j + 1) * P],
                                        w.wout, start=True, stop=True)
                if j % 2:
                    last.then_inc(s["out"], 1)

        @block.scalar
        def _(act):
            act.wait_ge(w.sem, w.loaded)
            for g, dst in enumerate((a, b)):
                act.wait_ge(s["proj"], g + 1)
                nc.scalar.activation(dst, ps[0:S, 2 * g:2 * g + 2, :].rearrange("p a b -> p (a b)"), ACT.Tanh,
                                     bias=w.bias[:, g:g + 1]).then_inc(s["tanh"], 1)

        @block.gpsimd
        def _(pool):
            pool.wait_ge(w.sem, w.loaded)
            nc.gpsimd.tensor_tensor(k.h, k.h, bc(w.bout, 1, NT), ALU.add).then_inc(s["hb"], 1)
            pool.wait_ge(s["hb"], 1)
            nc.gpsimd.tensor_tensor(k.x, k.x, k.h, ALU.add).then_inc(s["xh"], 1)

        @block.vector
        def _(dve):
            dve.wait_ge(s["tanh"], 1)
            nc.vector.memset(a.rearrange("p (b t) -> p b t", t=SEQ)[:, :, 0:1], 0.0).then_inc(s["cut"], 1)
            dve.wait_ge(s["cut"], 1)
            dve.wait_ge(s["tanh"], 2)
            nc.vector.tensor_tensor_scan(hs, a, b, 0.0, ALU.mult, ALU.add).then_inc(s["scan"], 1)
            dve.wait_ge(s["xh"], 1)
            for i in range(NT // 2):
                dve.wait_ge(s["out"], i + 1)
                nc.vector.tensor_tensor(k.x[:, 2 * i:2 * i + 2, :].rearrange("p a b -> p (a b)"),
                                        k.x[:, 2 * i:2 * i + 2, :].rearrange("p a b -> p (a b)"), ps[:, 4 + i, :],
                                        ALU.add).then_inc(s["xs"], 1)



GQA_KV, GQA_G, GQA_D = 8, 4, 8


def load_gqa(k, w, sem):
    d, eng = k.dram, k.nc.sync
    w.krep = w.region.take(2, TOK)
    w.vt = w.region.take(BATCH, GQA_KV * GQA_D)
    w.gmask = w.region.take(GQA_G)
    for c in range(2):
        for kv in range(4):
            r0 = (4 * c + kv) * GQA_D
            src = d["ctxT"][r0:r0 + GQA_D, :]
            eng.dma_start(w.krep[32 * kv:32 * kv + 32, c, :],
                          bass.AP(tensor=src.tensor, offset=src.offset, ap=[[0, GQA_G], [TOK, GQA_D], [1, TOK]])).then_inc(sem, 16)
    for half in range(2):
        eng.dma_start(w.vt[64 * half:64 * half + 64, :, :], d["ctx_512"].rearrange("b t d -> t b d")).then_inc(sem, 16)
    eng.dma_start(w.gmask, d["const_gmask"]).then_inc(sem, 16)
    return 16 * 11


def stage_gqa(k, w):
    nc, ps, x = k.nc, k.ps, k.x
    k.work.clear()
    kexp = w.region.take(2, BATCH, GQA_G, SEQ)
    vblk = w.region.take(BATCH, GQA_KV, 2, 9)
    pr = k.work.take(2, 16, SEQ)
    pT = k.work.take(2, 8, P)
    mx = k.work.take(2, 16)
    rs = k.work.take(2, 16)
    o = k.work.take(2, P)
    U = 2 * NT
    scale = float(GQA_D) ** -0.5
    hv = k.hT

    def pv_bank(u):
        return ps[:, 6 + u % 2, 0:144]

    with k.stage("spread", "vzero", "vones", "vals", "scored", "maxed", "centred", "expd", "turned", "copied",
                 "pv", "rsum", "normed", "added") as (block, s):
        @block.tensor
        def _(pe):
            def scores(u):
                j, ip = divmod(u, 2)
                if u >= 2:
                    pe.wait_ge(s["centred"], u - 1)
                for c in range(2):
                    for b in range(2):
                        for ii in range(2):
                            i = 2 * ip + ii
                            tok = j * P + b * SEQ
                            last = nc.tensor.matmul(
                                ps[64 * b:64 * b + 64, 2 * ip + ii, c * 256:c * 256 + 256],
                                hv[32 * i:32 * i + 32, c, tok:tok + SEQ],
                                kexp[32 * i:32 * i + 32, c, 2 * j + b, :, :].rearrange("p g t -> p (g t)"),
                                start=True, stop=True, tile_position=(32 * i, 64 * b))
                last.then_inc(s["scored"], 1)

            def turn(u):
                pe.wait_ge(s["expd"], u + 1)
                if u >= 1:
                    pe.wait_ge(s["copied"], 2 * u)
                for n in range(8):
                    last = nc.tensor.transpose(ps[:, 4 + n // 4, (n % 4) * P:(n % 4 + 1) * P],
                                               pr[:, u % 2, 2 * n:2 * n + 2, :].rearrange("p a t -> p (a t)"), k.ident)
                last.then_inc(s["turned"], 1)

            def weigh(u):
                j, ip = divmod(u, 2)
                pe.wait_ge(s["copied"], 2 * u + 2)
                if u >= 2:
                    pe.wait_ge(s["normed"], u - 1)
                for n in range(8):
                    ii, c, gp = n // 4, (n // 2) % 2, n % 2
                    for b in range(2):
                        at = 72 * c + 36 * ii + 18 * gp
                        last = nc.tensor.matmul(pv_bank(u)[64 * b:64 * b + 64, at:at + 18],
                                                pT[:, u % 2, n, 64 * b:64 * b + 64],
                                                vblk[:, 2 * j + b, 4 * c + 2 * ip + ii, :, :].rearrange("p g d -> p (g d)"),
                                                start=True, stop=True, tile_position=(0, 64 * b))
                last.then_inc(s["pv"], 1)

            pe.wait_ge(s["spread"], 8)
            pe.wait_ge(s["vals"], 2)
            for u in range(U + 2):
                if u < U:
                    scores(u)
                if 1 <= u <= U:
                    turn(u - 1)
                if u >= 2:
                    weigh(u - 2)

        @block.gpsimd
        def _(pool):
            nc.gpsimd.memset(vblk, 0.0).then_inc(s["vzero"], 1)
            pool.wait_ge(s["vzero"], 1)
            for g in range(2):
                nc.gpsimd.memset(vblk[64 * g:64 * g + 64, :, :, g, 8:9], 1.0).then_inc(s["vones"], 1)
            pool.wait_ge(w.sem, w.loaded)
            for g in range(2):
                r = slice(64 * g, 64 * g + 64)
                nc.gpsimd.tensor_copy(vblk[r, :, :, g, 0:8], w.vt[r, :, :].rearrange("p b (h d) -> p b h d", d=8)).then_inc(s["vals"], 1)
            pool.wait_ge(s["vones"], 2)

        @block.scalar
        def _(act):
            act.wait_ge(w.sem, w.loaded)
            for g in range(2):
                for c in range(2):
                    nc.scalar.activation(kexp[:, c, :, g, :], w.krep[:, c, :].rearrange("p (b t) -> p b t", t=SEQ), ACT.Copy,
                                         scale=w.gmask[:, g:g + 1]).then_inc(s["spread"], 1)
            for u in range(U):
                act.wait_ge(s["centred"], u + 1)
                nc.scalar.activation(pr[:, u % 2, :, :], pr[:, u % 2, :, :], ACT.Exp, scale=scale).then_inc(s["expd"], 1)
                act.wait_ge(s["turned"], u + 1)
                if u >= 2:
                    act.wait_ge(s["pv"], u - 1)
                for h in range(2):
                    nc.scalar.copy(pT[:, u % 2, 4 * h:4 * h + 4, :].rearrange("p a b -> p (a b)"), ps[:, 4 + h, :]).then_inc(s["copied"], 1)

        @block.vector
        def _(dve):
            dve.wait_ge(w.sem, w.loaded)
            for g in range(2, 4):
                for c in range(2):
                    nc.vector.tensor_scalar(kexp[:, c, :, g, :], w.krep[:, c, :].rearrange("p (b t) -> p b t", t=SEQ),
                                            w.gmask[:, g:g + 1], None, ALU.mult).then_inc(s["spread"], 1)

            def centre(u):
                ip = u % 2
                sc = ps[:, 2 * ip:2 * ip + 2, :].rearrange("p a (h t) -> p (a h) t", t=SEQ)
                dve.wait_ge(s["scored"], u + 1)
                nc.vector.tensor_reduce(mx[:, u % 2, :], sc, AX.X, ALU.max).then_inc(s["maxed"], 1)
                dve.wait_ge(s["maxed"], u + 1)
                if u >= 2:
                    dve.wait_ge(s["turned"], u - 1)
                nc.vector.tensor_tensor(pr[:, u % 2, :, :], sc, bc(mx[:, u % 2, :], 2, SEQ), ALU.subtract).then_inc(s["centred"], 1)

            def finish(u):
                j, ip = divmod(u, 2)
                dve.wait_ge(s["pv"], u + 1)
                pv = pv_bank(u).rearrange("p (h d) -> p h d", d=9)
                nc.vector.reciprocal(rs[:, u % 2, :], pv[:, :, 8]).then_inc(s["rsum"], 1)
                dve.wait_ge(s["rsum"], u + 1)
                ob = o[:, u % 2, :]
                nc.vector.tensor_tensor(ob.rearrange("p (h d) -> p h d", d=8), pv[:, :, 0:8], bc(rs[:, u % 2, :], 2, 8),
                                        ALU.mult).then_inc(s["normed"], 1)
                dve.wait_ge(s["normed"], u + 1)
                xv = x[:, j, :].rearrange("p (c f) -> p c f", c=2)[:, :, 64 * ip:64 * ip + 64]
                nc.vector.tensor_tensor(xv, xv, ob.rearrange("p (c f) -> p c f", c=2), ALU.add).then_inc(s["added"], 1)

            for u in range(U + 1):
                if u < U:
                    centre(u)
                if u >= 2:
                    finish(u - 2)
            finish(U - 1)



NH, DH = 16, 64


class Latent:

    def __init__(self, room, more, kk, kvt, pm):
        self.kk = kk
        self.kvt = kvt
        self.pm = pm
        self.ctxT = room.take(NH // 2, TOK)
        self.pT = room.take(2, 4, P)
        room = more
        self.pr = room.take(3, NT, SEQ)
        self.mx = room.take(2, NT)
        self.sm = room.take(2, NT)
        self.rs = room.take(2, NT)


CORE_SEMS = ("narrowed", "q_proj", "q_ready", "scored", "maxed", "centred", "expd", "summed", "recip", "probs", "turned",
             "copied", "pv", "ctx", "out", "added")


def attend(k, block, s, t, key_rows, q_of, q_hooks, scale, causal=None, turn_banks=(2, 3)):
    nc, ps, x = k.nc, k.ps, k.x

    @block.tensor
    def _(pe):
        def scores(h):
            hh = h % 2
            if h >= 2:
                pe.wait_ge(s["centred"], h - 1)
            pe.wait_ge(s["q_ready"], q_hooks["ready"](h))
            if causal is not None:
                nc.tensor.matmul(ps[:, 4 + hh, :], k.ident16, causal, start=True, stop=False, skip_group_check=True)
            r0, r1 = key_rows(h)
            for b in range(BATCH):
                tok, at = b * SEQ, (b // 2) * SEQ
                last = nc.tensor.matmul(ps[64 * (b % 2):64 * (b % 2) + 64, 4 + hh, at:at + SEQ],
                                        q_of(h)[:, tok:tok + SEQ], t.kk[r0:r1, tok:tok + SEQ],
                                        start=causal is None, stop=True, skip_group_check=causal is not None,
                                        tile_position=(r0, 64 * (b % 2)))
            last.then_inc(s["scored"], 1)

        def turn(h):
            pe.wait_ge(s["probs"], h + 1)
            gap = 1 if turn_banks[0] == turn_banks[1] else 2
            if h >= gap:
                pe.wait_ge(s["copied"], h + 1 - gap)
            for jp in range(4):
                last = nc.tensor.transpose(ps[:, turn_banks[h % 2], jp * P:(jp + 1) * P],
                                           t.pr[:, h % 3, 2 * jp:2 * jp + 2, :].rearrange("p a t -> p (a t)"), k.ident)
            last.then_inc(s["turned"], 1)

        def weigh(h):
            hh = h % 2
            pe.wait_ge(s["copied"], h + 1)
            if hh == 0 and h >= 2:
                pe.wait_ge(s["ctx"], h)
            for jp in range(4):
                for b in range(2):
                    for jj in range(2):
                        at = jp * P + b * SEQ
                        last = nc.tensor.matmul(ps[64 * hh:64 * hh + 64, 6 + jj, at:at + SEQ],
                                                t.kvt[64 * jj:64 * jj + 64, 2 * jp + b, :],
                                                t.pT[64 * jj:64 * jj + 64, h % 2, jp, b * SEQ:b * SEQ + SEQ],
                                                start=True, stop=True, tile_position=(64 * jj, 64 * hh))
            last.then_inc(s["pv"], 1)

        for h in range(NH + 5):
            if h < NH:
                q_hooks["pe"](pe, h)
            if h == NH:
                q_hooks.get("pe_last", none)(pe)
            if 2 <= h < NH + 2:
                scores(h - 2)
            if 4 <= h < NH + 4:
                turn(h - 4)
            if h >= 5:
                weigh(h - 5)
        pe.wait_ge(s["ctx"], NH)
        pe.wait_ge(s["centred"], NH)
        for j in range(NT):
            for u in range(NH // 2):
                last = nc.tensor.matmul(ps[:, (0, 1, 4, 5)[j // 2], (j % 2) * D:(j % 2 + 1) * D],
                                        t.ctxT[:, u, j * P:(j + 1) * P], t.pm[:, u, :],
                                        start=u == 0, stop=u == NH // 2 - 1)
            if j % 2:
                last.then_inc(s["out"], 1)

    @block.scalar
    def _(act):
        def copy_context(u):
            act.wait_ge(s["pv"], 2 * u + 2)
            for jj in range(2):
                dst = t.ctxT[:, u, :].rearrange("p (a j q) -> p a j q", j=2, q=P)[:, :, jj, :]
                nc.scalar.copy(dst, ps[:, 6 + jj, :].rearrange("p (a q) -> p a q", q=P)).then_inc(s["ctx"], 1)

        for h in range(NH + 6):
            if h < NH:
                q_hooks["act"](act, h)
            if h == NH:
                q_hooks.get("act_last", none)(act)
            if 2 <= h < NH + 2:
                g = h - 2
                act.wait_ge(s["centred"], g + 1)
                nc.scalar.activation(t.pr[:, g % 3, :, :], t.pr[:, g % 3, :, :], ACT.Exp, scale=scale).then_inc(s["expd"], 1)
            if 4 <= h < NH + 4:
                g = h - 4
                act.wait_ge(s["turned"], g + 1)
                if g >= 2:
                    act.wait_ge(s["pv"], g - 1)
                nc.scalar.copy(t.pT[:, g % 2, :, :].rearrange("p a b -> p (a b)"), ps[:, turn_banks[g % 2], :]).then_inc(s["copied"], 1)
            if h >= 6 and h % 2 == 0:
                copy_context((h - 6) // 2)

    @block.vector
    def _(dve):
        def normalise(dve, g):
            pr = t.pr[:, g % 3, :, :]
            sm, rs = t.sm[:, g % 2, :], t.rs[:, g % 2, :]
            dve.wait_ge(s["expd"], g + 1)
            nc.vector.tensor_reduce(sm, pr, AX.X, ALU.add).then_inc(s["summed"], 1)
            dve.wait_ge(s["summed"], g + 1)
            nc.vector.reciprocal(rs, sm).then_inc(s["recip"], 1)
            dve.wait_ge(s["recip"], g + 1)
            nc.vector.tensor_tensor(pr, pr, bc(rs, 2, SEQ), ALU.mult).then_inc(s["probs"], 1)

        for h in range(NH + 2):
            if h < NH:
                q_hooks.get("dve", none)(dve, h)
            if h < 2:
                continue
            g = h - 2
            sc = ps[:, 4 + g % 2, :].rearrange("p (j t) -> p j t", t=SEQ)
            pr = t.pr[:, g % 3, :, :]
            mx, sm, rs = t.mx[:, g % 2, :], t.sm[:, g % 2, :], t.rs[:, g % 2, :]
            dve.wait_ge(s["scored"], g + 1)
            nc.vector.tensor_reduce(mx, sc, AX.X, ALU.max).then_inc(s["maxed"], 1)
            dve.wait_ge(s["maxed"], g + 1)
            if g >= 3:
                dve.wait_ge(s["turned"], g - 2)
            nc.vector.tensor_tensor(pr, sc, bc(mx, 2, SEQ), ALU.subtract).then_inc(s["centred"], 1)
            if g >= 1:
                normalise(dve, g - 1)
        normalise(dve, NH - 1)
        for i in range(NT // 2):
            dve.wait_ge(s["out"], i + 1)
            xv = x[:, 2 * i:2 * i + 2, :].rearrange("p a b -> p (a b)")
            nc.vector.tensor_tensor(xv, xv, ps[:, (0, 1, 4, 5)[i], :], ALU.add).then_inc(s["added"], 1)


def load_latent_cross(k, w, sem, L):
    d, eng = k.dram, k.nc.sync
    r = w.region
    w.table = r.take(2, 2, SEQ, rows=96)
    w.wq = r.take(NH, D)
    w.qr = r.take(NH // 2, 192)
    w.kr = r.take(NH // 2, DH)
    w.kckv = r.take(NH, DH)
    w.wo = r.take(NH, D)
    w.raw = r.take(8, DH)
    w.rope = r.take(2, DH)
    eng.dma_start(w.wq, d[L + "Wq"].rearrange("(h p) d -> p h d", p=P)).then_inc(sem, 16)
    n = 16
    if L == "L1_xattn_":
        w.kcqT = r.take(NH, 2, P, rows=96)
        eng.dma_start(w.kcqT, d[L + "kcqT"].rearrange("h (a q) p -> q h a p", a=2)).then_inc(sem, 16)
    else:
        w.kcq = r.take(NH, 192)
        eng.dma_start(w.table, d["const_rope192"]).then_inc(sem, 16)
        n = 32
        eng.dma_start(w.kcq, d[L + "w_kc_q"].rearrange("h p q -> p h q")).then_inc(sem, 16)
    for hh in range(2):
        rows = slice(64 * hh, 64 * hh + 64)
        eng.dma_start(w.qr[rows, :, :], d[L + "qrT"].rearrange("(a e) r q -> e r a q", e=2)[hh]).then_inc(sem, 16)
        eng.dma_start(w.kr[rows, :, :], d[L + "krT"].rearrange("(a e) r q -> e r a q", e=2)[hh]).then_inc(sem, 16)
        for jp in range(4):
            b0 = 4 * jp + 2 * hh
            eng.dma_start(w.raw[rows, 2 * jp:2 * jp + 2, :], d["ctx_512"][b0:b0 + 2].rearrange("b t d -> t b d")).then_inc(sem, 16)
    eng.dma_start(w.kckv, d[L + "w_kc_kv"].rearrange("h p q -> p h q")).then_inc(sem, 16)
    eng.dma_start(w.wo, d[L + "WoT"].rearrange("(h p) d -> p h d", p=P)).then_inc(sem, 16)
    eng.dma_start(w.rope, d["const_rope64"]).then_inc(sem, 16)
    return 16 * (1 + 12 + 3) + n


def fold_cross(k, w, t, c1, nf, qf):
    nc, ps = k.nc, k.ps
    spare = Region(k.h.rearrange("p j d -> p (j d)"), NT * D)
    kvd = spare.take(8, 2, DH)
    tmp = spare.take(8, DH)
    c2 = spare.take(4, DH)
    with k.stage("c1", "c1s", "c2", "c2s", "nf", "nfs", "pm", "pms", "qf", "qfs", "rope", "dup", "kkT", "kks") as (block, s):
        @block.tensor
        def _(pe):
            pe.wait_ge(w.sem, w.loaded)
            for g in range(4):
                if g:
                    pe.wait_ge(s["c1s"], g)
                for a in range(2):
                    for i in range(4):
                        h = 4 * g + i
                        r = slice(64 * (h % 2), 64 * (h % 2) + 64)
                        last = nc.tensor.matmul(ps[0:96, h % 2, (2 * a + i // 2) * DH:(2 * a + i // 2 + 1) * DH],
                                                w.qr[r, h // 2, a * 96:(a + 1) * 96], w.kr[r, h // 2, :],
                                                start=True, stop=True, tile_position=(64 * (h % 2), 0))
                last.then_inc(s["c1"], 1)
                if g:
                    pe.wait_ge(s["pms"], g)
                for i in range(4):
                    h = 4 * g + i
                    last = nc.tensor.matmul(ps[64 * (h % 2):64 * (h % 2) + 64, 2, (i // 2) * D:(i // 2 + 1) * D],
                                            w.kckv[:, h, :], w.wo[:, h, :], start=True, stop=True,
                                            tile_position=(0, 64 * (h % 2)))
                last.then_inc(s["pm"], 1)
                if nf is not None:
                    pe.wait_ge(s["c1s"], g + 1)
                    if g:
                        pe.wait_ge(s["c2s"], g)
                    for i in range(4):
                        for a in range(2):
                            last = nc.tensor.matmul(ps[:, 3, i * DH:(i + 1) * DH], w.kcqT[:, 4 * g + i, a, :],
                                                    c1[:, a, 4 * g + i, :], start=a == 0, stop=a == 1)
                    last.then_inc(s["c2"], 1)
                    pe.wait_ge(s["c2s"], g + 1)
                    if g:
                        pe.wait_ge(s["nfs"], g)
                    for i in range(4):
                        for c in range(KC):
                            last = nc.tensor.matmul(ps[:, 4, (c * 4 + i) * DH:(c * 4 + i + 1) * DH],
                                                    w.wq[:, 4 * g + i, c * P:(c + 1) * P], c2[:, i, :], start=True, stop=True)
                    last.then_inc(s["nf"], 1)
                else:
                    for i in range(4):
                        h = 4 * g + i
                        if h >= 2:
                            pe.wait_ge(s["qfs"], h - 1)
                        for c in range(KC):
                            last = nc.tensor.matmul(ps[:, 3 + h % 2, c * 192:(c + 1) * 192],
                                                    w.wq[:, h, c * P:(c + 1) * P], w.kcq[:, h, :], start=True, stop=True)
                        last.then_inc(s["qf"], 1)
            pe.wait_ge(s["dup"], 1)
            for n in range(8):
                last = nc.tensor.transpose(ps[:, 6 + n // 4, (n % 4) * P:(n % 4 + 1) * P],
                                           kvd[:, n, :, :].rearrange("p a d -> p (a d)"), k.ident)
            last.then_inc(s["kkT"], 1)

        @block.scalar
        def _(act):
            for g in range(4):
                act.wait_ge(s["c1"], g + 1)
                cv = c1[:, :, 4 * g:4 * g + 4, :].rearrange("p a (i e) d -> p e a i d", e=2)
                for e in range(2):
                    ins = nc.scalar.copy(cv[:, e], ps[0:96, e, 0:256].rearrange("p (a i d) -> p a i d", a=2, i=2))
                ins.then_inc(s["c1s"], 1)
                act.wait_ge(s["pm"], g + 1)
                nc.scalar.copy(t.pm[:, 2 * g:2 * g + 2, :].rearrange("p a d -> p (a d)"), ps[:, 2, :]).then_inc(s["pms"], 1)
                if nf is not None:
                    act.wait_ge(s["nf"], g + 1)
                    nc.scalar.copy(nf[:, :, 4 * g:4 * g + 4, :].rearrange("p c h d -> p c (h d)"),
                                   ps[:, 4, :].rearrange("p (c f) -> p c f", c=2)).then_inc(s["nfs"], 1)

        @block.vector
        def _(dve):
            dve.wait_ge(w.sem, w.loaded)
            cos, sin = bc(w.rope[:, 0, :], 1, 8), w.rope[:, 1, :]
            nc.vector.tensor_tensor(t.kvt, w.raw, cos, ALU.mult).then_inc(s["rope"], 1)
            for e in range(2):
                o, i = slice(32 * e, 32 * e + 32), slice(32 - 32 * e, 64 - 32 * e)
                nc.vector.tensor_tensor(tmp[:, :, o], w.raw[:, :, i], bc(sin[:, o], 1, 8), ALU.mult).then_inc(s["rope"], 1)
            dve.wait_ge(s["rope"], 3)
            nc.vector.tensor_tensor(t.kvt, t.kvt, tmp, ALU.add).then_inc(s["rope"], 1)
            dve.wait_ge(s["rope"], 4)
            nc.vector.tensor_copy(kvd, bc(t.kvt, 2, 2)).then_inc(s["dup"], 1)
            if nf is not None:
                for g in range(4):
                    dve.wait_ge(s["c2"], g + 1)
                    if g:
                        dve.wait_ge(s["nf"], g)
                    nc.vector.tensor_copy(c2, ps[:, 3, 0:256].rearrange("p (i d) -> p i d", d=DH)).then_inc(s["c2s"], 1)
            else:
                for h in range(NH):
                    dve.wait_ge(s["qf"], h + 1)
                    nc.vector.tensor_copy(qf[:, :, h, :], ps[:, 3 + h % 2, 0:384].rearrange("p (c q) -> p c q", c=2)).then_inc(s["qfs"], 1)
            dve.wait_ge(s["kkT"], 1)
            kkv = t.kk.rearrange("p (a j b t) -> p a b j t", a=4, j=2, b=2)
            for jp in range(4):
                at = (jp % 2) * 256
                nc.vector.tensor_copy(kkv[:, jp], ps[:, 6 + jp // 2, at:at + 256].rearrange("p (b j t) -> p b j t", b=2, j=2)).then_inc(s["kks"], 1)


def stage_L1_xattn(k, w):
    nc, ps = k.nc, k.ps
    k.work.clear()
    nf = k.work.take(KC, NH, DH)
    pm = k.work.take(NH // 2, D)
    kk = k.work.take(TOK)
    kvt = k.work.take(8, DH)
    mark = k.work.at
    c1 = k.work.take(2, NH, DH, rows=96)

    f = Named()
    f.pm, f.kk, f.kvt = pm, kk, kvt
    fold_cross(k, w, f, c1, nf, None)
    k.work.at = mark
    w.region.clear()
    t = Latent(w.region, w.region, kk, kvt, pm)
    qb = w.region.take(2, TOK)
    with k.stage(*CORE_SEMS) as (block, s):
        def pe_q(pe, h):
            u, half = divmod(h, 2)
            if u >= 1:
                pe.wait_ge(s["q_ready"], 2 * u - 1 + half)
            for c in range(KC):
                last = nc.tensor.matmul(ps[:, half, :], nf[:, c, 2 * u:2 * u + 2, :].rearrange("p h d -> p (h d)"),
                                        k.hT[:, c, half * BANK:(half + 1) * BANK], start=c == 0, stop=c == KC - 1)
            last.then_inc(s["q_proj"], 1)

        def act_q(act, h):
            u, half = divmod(h, 2)
            act.wait_ge(s["q_proj"], h + 1)
            if u >= 2:
                act.wait_ge(s["scored"], 2 * u - 2)
            nc.scalar.copy(qb[:, u % 2, half * BANK:(half + 1) * BANK], ps[:, half, :]).then_inc(s["q_ready"], 1)

        attend(k, block, s, t, lambda h: (64 * (h % 2), 64 * (h % 2) + 64),
               lambda h: qb[64 * (h % 2):64 * (h % 2) + 64, (h // 2) % 2, :],
               {"pe": pe_q, "act": act_q, "ready": lambda h: 2 * (h // 2) + 2}, 1.0)


def none(*_):
    pass


def stage_L2_xattn(k, w):
    nc, ps = k.nc, k.ps
    k.work.clear()
    qf = k.work.take(KC, NH, 192)
    pm = k.work.take(NH // 2, D)
    kk = k.work.take(TOK)
    kvt = k.work.take(8, DH)
    c1 = k.work.take(2, NH, DH, rows=96)
    f = Named()
    f.pm, f.kk, f.kvt = pm, kk, kvt
    fold_cross(k, w, f, c1, None, qf)
    w.region.at = 2 * 2 * SEQ
    t = Latent(w.region, w.region, kk, kvt, pm)
    qb = w.region.take(2, TOK)
    ro = w.region.take(2, 2, BANK, rows=96)
    sn = w.region.take(2, BANK, rows=96)
    swapped = ps[0:96, 0:2, :].rearrange("p a (b t) -> p a b t", t=SEQ)
    swapped = bass.AP(tensor=swapped.tensor, offset=swapped.offset + BANK,
                      ap=[list(swapped.ap[0]), [-BANK, 2]] + [list(e) for e in swapped.ap[2:]])
    with k.stage("cosed", "sined", "roped", *CORE_SEMS) as (block, s):
        def project(pe, v):
            h, half = divmod(v, 2)
            if v:
                pe.wait_ge(s["sined"], v)
            for a in range(2):
                for c in range(KC):
                    last = nc.tensor.matmul(ps[0:96, a, :], qf[:, c, h, 96 * a:96 * a + 96],
                                            k.hT[:, c, half * BANK:(half + 1) * BANK], start=c == 0, stop=c == KC - 1)
            last.then_inc(s["q_proj"], 1)

        def narrow(pe, v):
            h = v // 2
            pe.wait_ge(s["roped"], v + 1)
            if v:
                pe.wait_ge(s["q_ready"], v)
            for a in range(2):
                last = nc.tensor.matmul(ps[64 * (h % 2):64 * (h % 2) + 64, 2, :], c1[:, a, h, :], ro[:, v % 2, a, :],
                                        start=a == 0, stop=a == 1, tile_position=(0, 64 * (h % 2)))
            last.then_inc(s["narrowed"], 1)

        def pe_q(pe, h):
            for v in (2 * h, 2 * h + 1):
                project(pe, v)
                if v:
                    narrow(pe, v - 1)

        def dve_q(dve, h):
            for v in (2 * h, 2 * h + 1):
                dve.wait_ge(s["q_proj"], v + 1)
                if v >= 2:
                    dve.wait_ge(s["narrowed"], v - 1)
                rv = ro[:, v % 2, :, :].rearrange("p a (b t) -> p a b t", t=SEQ)
                nc.vector.tensor_tensor(rv, ps[0:96, 0:2, :].rearrange("p a (b t) -> p a b t", t=SEQ),
                                        bc(w.table[:, 0, :, :], 2, 8), ALU.mult).then_inc(s["cosed"], 1)
                if v:
                    dve.wait_ge(s["roped"], v)
                nc.vector.tensor_tensor(sn.rearrange("p a (b t) -> p a b t", t=SEQ), swapped,
                                        bc(w.table[:, 1, :, :], 2, 8), ALU.mult).then_inc(s["sined"], 1)

        def copy_q(act, v):
            h, half = divmod(v, 2)
            act.wait_ge(s["narrowed"], v + 1)
            if h >= 4:
                act.wait_ge(s["scored"], h - 3)
            r = slice(64 * (h % 2), 64 * (h % 2) + 64)
            nc.scalar.copy(qb[r, (h // 2) % 2, half * BANK:(half + 1) * BANK], ps[r, 2, :]).then_inc(s["q_ready"], 1)

        def act_q(act, h):
            if h:
                copy_q(act, 2 * h - 1)
            copy_q(act, 2 * h)

        @block.gpsimd
        def _(pool):
            for v in range(2 * NH):
                pool.wait_ge(s["cosed"], v + 1)
                pool.wait_ge(s["sined"], v + 1)
                nc.gpsimd.tensor_tensor(ro[:, v % 2, :, :], ro[:, v % 2, :, :], sn, ALU.add).then_inc(s["roped"], 1)

        attend(k, block, s, t, lambda h: (64 * (h % 2), 64 * (h % 2) + 64),
               lambda h: qb[64 * (h % 2):64 * (h % 2) + 64, (h // 2) % 2, :],
               {"pe": pe_q, "act": act_q, "dve": dve_q, "ready": lambda h: 2 * h + 2,
                "pe_last": lambda pe: narrow(pe, 2 * NH - 1), "act_last": lambda act: copy_q(act, 2 * NH - 1)},
               1.0, turn_banks=(3, 3))


def load_L3_attn(k, w, sem):
    d, eng, r = k.dram, k.nc.sync, w.region
    w.nr = r.take(2, NH, P, rows=96)
    w.sw = r.take(2, NH, DH, rows=96)
    w.all = r.take(KC, 384)
    w.mark = r.at
    w.qnT = r.take(NH, 192)
    w.kT = r.take(NH, DH)
    w.vT = r.take(NH, DH)
    w.wo = r.take(NH, D)
    w.rope = k.fixed.take(2, DH)
    w.ropeT = k.fixed.take(2, SEQ)
    w.qw = k.fixed.take(2, rows=96)
    w.kw = k.fixed.take(DH)
    p = "L3_attn_"
    for a in range(2):
        eng.dma_start(w.nr[:, a, :, 64:128], d[p + "Wq_rot"][96 * a:96 * a + 96]).then_inc(sem, 16)
        eng.dma_start(w.sw[:, a, :, :], d[p + "Wq_swap"][96 * a:96 * a + 96]).then_inc(sem, 16)
    eng.dma_start(w.all, d[p + "Wall"].rearrange("(c p) s -> p c s", p=P)).then_inc(sem, 16)
    eng.dma_start(w.qnT, d[p + "Wq_nopeT"]).then_inc(sem, 16)
    eng.dma_start(w.kT, d[p + "WkT"]).then_inc(sem, 16)
    eng.dma_start(w.vT, d[p + "WvT"]).then_inc(sem, 16)
    eng.dma_start(w.wo, d[p + "Wo"].rearrange("(h p) d -> p h d", p=P)).then_inc(sem, 16)
    eng.dma_start(w.rope, d["const_rope64b"]).then_inc(sem, 16)
    eng.dma_start(w.ropeT, d["const_rope64T"]).then_inc(sem, 16)
    eng.dma_start(w.qw, d[p + "q_norm_w"]).then_inc(sem, 16)
    eng.dma_start(w.kw, row_on_all(d[p + "kv_norm_w"])).then_inc(sem, 16)
    return 16 * 13


def stage_L3_attn(k, w):
    nc, ps = k.nc, k.ps
    k.work.clear()
    EPS = 1e-6
    pm = k.work.take(NH // 2, D)
    kk = k.work.take(TOK)
    kvt = k.work.take(8, DH)
    qnT = k.work.take(2, TOK, rows=96)
    ss = k.work.take(2, NT)
    rstd = k.work.take(2, NT)
    qb = k.work.take(3, TOK)
    sn = k.work.take(BANK)
    qn = k.h.rearrange("p j d -> p (j d)")[:, 0:NT * 192].rearrange("p (j d) -> p j d", j=NT)
    km = qb[:, 0, :].rearrange("p (j d) -> p j d", j=NT)
    sq = qb[:, 1, 0:192]
    kr = qb[:, 2, :].rearrange("p (a d) -> p a d", d=DH)
    with k.stage("lat", "sq", "mean", "std", "rstd", "qn", "km", "kvn", "kra", "krb") as (block, s):
        @block.tensor
        def _(pe):
            pe.wait_ge(w.sem, w.loaded)
            for j in range(NT):
                for c in range(KC):
                    last = nc.tensor.matmul(ps[:, j, 0:384], k.hT[:, c, j * P:(j + 1) * P], w.all[:, c, :],
                                            start=c == 0, stop=c == KC - 1)
                last.then_inc(s["lat"], 1)

        @block.scalar
        def _(act):
            for j in range(NT):
                act.wait_ge(s["lat"], j + 1)
                if j:
                    act.wait_ge(s["sq"], 2 * j)
                nc.scalar.activation(sq, ps[:, j, 0:192], ACT.Square, accum_out=ss[:, 0, j:j + 1]).then_inc(s["sq"], 1)
                act.wait_ge(s["sq"], 2 * j + 1)
                nc.scalar.activation(sq[:, 0:64], ps[:, j, 192:256], ACT.Square, accum_out=ss[:, 1, j:j + 1]).then_inc(s["sq"], 1)
            act.wait_ge(s["mean"], 2)
            nc.scalar.activation(rstd, ss, ACT.Sqrt).then_inc(s["std"], 1)

        @block.vector
        def _(dve):
            dve.wait_ge(s["lat"], NT)
            dve.wait_ge(s["sq"], 2 * NT)
            dve.wait_ge(w.sem, w.loaded)
            krv = kr[:, 0:8, :]
            nc.vector.tensor_tensor(km[:, :, 64:128], ps[:, :, 256:320], bc(w.rope[:, 0, :], 1, NT), ALU.mult).then_inc(s["kra"], 1)
            nc.vector.tensor_tensor(krv, ps[:, :, 320:384], bc(w.rope[:, 1, :], 1, NT), ALU.mult).then_inc(s["kra"], 1)
            dve.wait_ge(s["kra"], 2)
            nc.vector.tensor_tensor(km[:, :, 64:128], km[:, :, 64:128], krv, ALU.add).then_inc(s["krb"], 1)
            for g, n in ((0, 192), (1, 64)):
                nc.vector.tensor_scalar(ss[:, g, :], ss[:, g, :], 1.0 / n, EPS, ALU.mult, ALU.add).then_inc(s["mean"], 1)
            dve.wait_ge(s["std"], 1)
            nc.vector.reciprocal(ss, rstd).then_inc(s["rstd"], 1)
            dve.wait_ge(s["rstd"], 1)
            for j in range(NT):
                nc.vector.tensor_scalar(qn[:, j, :], ps[:, j, 0:192], ss[:, 0, j:j + 1], None, ALU.mult).then_inc(s["qn"], 1)
                nc.vector.scalar_tensor_tensor(km[:, j, 0:64], ps[:, j, 192:256], ss[:, 1, j:j + 1], w.kw,
                                               ALU.mult, ALU.mult).then_inc(s["kvn"], 1)

    lat = qb[0:64, 1, :]
    with k.stage("t_qn", "t_km", "c_qn", "c_km", "c_lat", "t_kv", "nope", "noped", "pm", "pms", "kvs") as (block, s):
        @block.tensor
        def _(pe):
            for g in range(2):
                for i in range(4):
                    j = 4 * g + i
                    for a in range(2):
                        last = nc.tensor.transpose(ps[0:96, 2 * g + a, i * P:(i + 1) * P], qn[:, j, 96 * a:96 * a + 96], k.ident)
                last.then_inc(s["t_qn"], 1)
                for i in range(4):
                    last = nc.tensor.transpose(ps[:, 4 + g, i * P:(i + 1) * P], km[:, 4 * g + i, :], k.ident)
                last.then_inc(s["t_km"], 1)
            for g in range(4):
                if g:
                    pe.wait_ge(s["noped"], g)
                for i in range(4):
                    for a in range(2):
                        last = nc.tensor.matmul(ps[0:96, 6, (a * 4 + i) * DH:(a * 4 + i + 1) * DH],
                                                w.qnT[:, 4 * g + i, 96 * a:96 * a + 96], w.kT[:, 4 * g + i, :], start=True, stop=True)
                last.then_inc(s["nope"], 1)
                if g:
                    pe.wait_ge(s["pms"], g)
                for i in range(4):
                    h = 4 * g + i
                    last = nc.tensor.matmul(ps[64 * (h % 2):64 * (h % 2) + 64, 7, (i // 2) * D:(i // 2 + 1) * D],
                                            w.vT[:, h, :], w.wo[:, h, :], start=True, stop=True, tile_position=(0, 64 * (h % 2)))
                last.then_inc(s["pm"], 1)
            pe.wait_ge(s["c_qn"], 2)
            pe.wait_ge(s["c_lat"], 2)
            for n in range(8):
                last = nc.tensor.transpose(ps[:, 0, n * DH:(n + 1) * DH], lat[:, n * P:(n + 1) * P], k.ident[0:64, 0:64])
            last.then_inc(s["t_kv"], 1)

        @block.scalar
        def _(act):
            for g in range(4):
                act.wait_ge(s["pm"], g + 1)
                nc.scalar.copy(pm[:, 2 * g:2 * g + 2, :].rearrange("p a d -> p (a d)"), ps[:, 7, :]).then_inc(s["pms"], 1)

        @block.vector
        def _(dve):
            for g in range(2):
                dve.wait_ge(s["t_qn"], g + 1)
                for a in range(2):
                    ins = nc.vector.tensor_scalar(qnT[:, a, g * BANK:(g + 1) * BANK], ps[0:96, 2 * g + a, :], w.qw[:, a:a + 1], None,
                                                  ALU.mult)
                ins.then_inc(s["c_qn"], 1)
                dve.wait_ge(s["t_km"], g + 1)
                nc.vector.tensor_copy(kk[:, g * BANK:(g + 1) * BANK], ps[:, 4 + g, :]).then_inc(s["c_km"], 1)
                for jp in range(2):
                    ins = nc.vector.tensor_copy(
                        lat[:, (2 * g + jp) * 256:(2 * g + jp + 1) * 256].rearrange("p (b j t) -> p b j t", b=2, j=2),
                        ps[0:64, 4 + g, jp * 256:(jp + 1) * 256].rearrange("p (j b t) -> p b j t", j=2, b=2))
                ins.then_inc(s["c_lat"], 1)
            for g in range(4):
                dve.wait_ge(s["nope"], g + 1)
                nc.vector.tensor_copy(w.nr[:, :, 4 * g:4 * g + 4, 0:64],
                                      ps[0:96, 6, :].rearrange("p (a i d) -> p a i d", a=2, i=4)).then_inc(s["noped"], 1)
            dve.wait_ge(s["t_kv"], 1)
            nc.vector.tensor_copy(kvt.rearrange("p n d -> p (n d)"), ps[:, 0, :]).then_inc(s["kvs"], 1)

    w.region.at = w.mark
    t = Latent(w.region, k.work, kk, kvt, pm)
    hi = slice(64, 128)
    with k.stage("q_top", "cosed", "sined", *CORE_SEMS) as (block, s):
        def pe_q(pe, h):
            for v in (2 * h, 2 * h + 1):
                half = v % 2
                if v:
                    pe.wait_ge(s["sined"], v)
                    pe.wait_ge(s["q_top"], v)
                tok = slice(half * BANK, (half + 1) * BANK)
                for a in range(2):
                    nc.tensor.matmul(ps[:, 0, :], w.nr[:, a, h, :], qnT[:, a, tok], start=a == 0, stop=a == 1)
                for a in range(2):
                    last = nc.tensor.matmul(ps[hi, 1, :], w.sw[:, a, h, :], qnT[:, a, tok], start=a == 0, stop=a == 1,
                                            tile_position=(0, 64))
                last.then_inc(s["q_proj"], 1)

        def act_q(act, h):
            for v in (2 * h, 2 * h + 1):
                act.wait_ge(s["q_proj"], v + 1)
                if h >= 3:
                    act.wait_ge(s["scored"], h - 2)
                nc.scalar.copy(qb[0:64, h % 3, (v % 2) * BANK:(v % 2 + 1) * BANK], ps[0:64, 0, :]).then_inc(s["q_top"], 1)

        def dve_q(dve, h):
            for v in (2 * h, 2 * h + 1):
                dve.wait_ge(s["q_proj"], v + 1)
                if h >= 3:
                    dve.wait_ge(s["scored"], h - 2)
                tab = lambda i: bc(w.ropeT[hi, i, :], 1, 8)
                nc.vector.tensor_tensor(qb[hi, h % 3, (v % 2) * BANK:(v % 2 + 1) * BANK].rearrange("p (b t) -> p b t", t=SEQ),
                                        ps[hi, 0, :].rearrange("p (b t) -> p b t", t=SEQ), tab(0), ALU.mult).then_inc(s["cosed"], 1)
                if v:
                    dve.wait_ge(s["q_ready"], v)
                nc.vector.tensor_tensor(sn[hi, :].rearrange("p (b t) -> p b t", t=SEQ),
                                        ps[hi, 1, :].rearrange("p (b t) -> p b t", t=SEQ), tab(1), ALU.mult).then_inc(s["sined"], 1)

        @block.gpsimd
        def _(pool):
            for v in range(2 * NH):
                q = qb[hi, (v // 2) % 3, (v % 2) * BANK:(v % 2 + 1) * BANK]
                pool.wait_ge(s["q_top"], v + 1)
                pool.wait_ge(s["cosed"], v + 1)
                pool.wait_ge(s["sined"], v + 1)
                nc.gpsimd.tensor_tensor(q, q, sn[hi, :], ALU.add).then_inc(s["q_ready"], 1)

        attend(k, block, s, t, lambda h: (0, P), lambda h: qb[:, h % 3, :],
               {"pe": pe_q, "act": act_q, "dve": dve_q, "ready": lambda h: 2 * h + 2}, 192 ** -0.5, causal=k.causal)



class First:

    def __init__(self, room, E):
        self.mx, self.eq, self.mr = room.take(NT), room.take(NT, E), room.take(NT)


def pick_first(k, chain, vals, f, sel):
    nc = k.nc
    E = vals.shape[-1]
    chain.step(nc.vector.tensor_reduce(f.mx, vals, AX.X, ALU.max))
    chain.step(nc.vector.tensor_tensor(f.eq, vals, bc(f.mx, 2, E), ALU.is_equal))
    chain.step(nc.vector.tensor_tensor(f.eq, f.eq, bc(k.rev[:, 0:E], 1, NT), ALU.mult))
    chain.step(nc.vector.tensor_reduce(f.mr, f.eq, AX.X, ALU.max))
    chain.step(nc.vector.tensor_tensor(sel, f.eq, bc(f.mr, 2, E), ALU.is_equal))


def softmax_rows(k, dve, chain, s, logits, pr, mx, sm):
    nc = k.nc
    E = pr.shape[-1]
    chain.step(nc.vector.tensor_reduce(mx, logits, AX.X, ALU.max))
    nc.vector.tensor_tensor(pr, logits, bc(mx, 2, E), ALU.subtract).then_inc(s["shifted"], 1)
    dve.wait_ge(s["exps"], 1)
    chain.step(nc.vector.tensor_reduce(sm, pr, AX.X, ALU.add))
    chain.step(nc.vector.reciprocal(sm, sm))
    chain.step(nc.vector.tensor_tensor(pr, pr, bc(sm, 2, E), ALU.mult))


def route_logits(k, pe, w_router, E, bank, sem):
    for j in range(NT):
        for c in range(KC):
            last = k.nc.tensor.matmul(k.ps[:, bank, j * E:(j + 1) * E], k.hT[:, c, j * P:(j + 1) * P],
                                      w_router[:, c, :], start=c == 0, stop=c == KC - 1)
    last.then_inc(sem, 1)


def load_L0_ffn(k, w, sem):
    d, eng, r = k.dram, k.nc.sync, w.region
    w.fc1, w.fc2 = r.take(8, KC, D), r.take(8, KC, D)
    w.gate, w.b1, w.b2, w.alpha = r.take(KC, 8), r.take(2, 8), r.take(D, rows=8), r.take(8)
    p = "L0_ffn_"
    eng.dma_start(w.gate, d[p + "gate_w"].rearrange("(c p) e -> p c e", p=P)).then_inc(sem, 16)
    eng.dma_start(w.b1, d[p + "fc1_b"]).then_inc(sem, 16)
    eng.dma_start(w.b2, d[p + "fc2_b"]).then_inc(sem, 16)
    eng.dma_start(w.alpha, row_on_all(d[p + "alpha"])).then_inc(sem, 16)
    for e in range(8):
        eng.dma_start(w.fc1[:, e], d[p + "fc1_w"][e].rearrange("(c p) i -> p c i", p=P)).then_inc(sem, 16)
        eng.dma_start(w.fc2[:, e], d[p + "fc2_w"][e].rearrange("(c p) i -> p c i", p=P)).then_inc(sem, 16)
    return 16 * 20


def stage_L0_ffn(k, w):
    nc, ps, x, E = k.nc, k.ps, k.x, 8
    k.work.clear()
    r = k.work
    pr, sel, sel2, rest, comb = (r.take(NT, E) for _ in range(5))
    f = First(r, E)
    mx, sm = r.take(NT), r.take(NT)
    act1 = r.take(2, KC, TOK)
    combT = r.take(TOK, rows=E)
    with k.stage("logits", "shifted", "exps", "chain", "comb", "combT", "cT", "h1", "gelu", "y", "acc", "bias", "biased") as (block, s):
        def accumulate_bank(i):
            return ps[:, 4 + i, :].rearrange("p (a d) -> p a d", a=2)

        @block.tensor
        def _(pe):
            pe.wait_ge(w.sem, w.loaded)
            route_logits(k, pe, w.gate, E, 7, s["logits"])
            for e in range(E + 1):
                if e < E:
                    for m in range(2):
                        for half in range(2):
                            n = 4 * e + 2 * m + half
                            if e:
                                pe.wait_ge(s["gelu"], n - 3)
                            for c in range(KC):
                                last = nc.tensor.matmul(ps[:, 2 * m + half, :], w.fc1[:, e, c, m * P:(m + 1) * P],
                                                        k.hT[:, c, half * BANK:(half + 1) * BANK], start=c == 0, stop=c == KC - 1)
                            last.then_inc(s["h1"], 1)
                if e == 0:
                    pe.wait_ge(s["comb"], 1)
                    for j in range(NT):
                        last = nc.tensor.transpose(ps[0:E, 5 + j // 4, (j % 4) * P:(j % 4 + 1) * P], comb[:, j, :], k.ident)
                    last.then_inc(s["combT"], 1)
                    pe.wait_ge(s["cT"], 1)
                    for i in range(4):
                        for jj in range(2):
                            j = 2 * i + jj
                            last = nc.tensor.matmul(ps[:, 4 + i, jj * D:(jj + 1) * D], combT[:, j * P:(j + 1) * P], w.b2,
                                                    start=True, stop=True)
                        last.then_inc(s["bias"], 1)
                if e >= 1:
                    pe.wait_ge(s["gelu"], 4 * e)
                    for i in range(4):
                        if e >= 2:
                            pe.wait_ge(s["acc"], 8 * (e - 2) + 2 * i + 2)
                        else:
                            pe.wait_ge(s["biased"], i + 1)
                        for jj in range(2):
                            j = 2 * i + jj
                            for c in range(KC):
                                last = nc.tensor.matmul(ps[:, 4 + i, jj * D:(jj + 1) * D], act1[:, (e - 1) % 2, c, j * P:(j + 1) * P],
                                                        w.fc2[:, e - 1, c, :], start=c == 0, stop=c == KC - 1)
                        last.then_inc(s["y"], 1)

        @block.scalar
        def _(act):
            act.wait_ge(w.sem, w.loaded)
            act.wait_ge(s["shifted"], 1)
            nc.scalar.activation(pr, pr, ACT.Exp).then_inc(s["exps"], 1)
            for e in range(E):
                if e >= 2:
                    act.wait_ge(s["y"], 4 * (e - 1))
                for m in range(2):
                    for half in range(2):
                        act.wait_ge(s["h1"], 4 * e + 2 * m + half + 1)
                        nc.scalar.activation(act1[:, e % 2, m, half * BANK:(half + 1) * BANK], ps[:, 2 * m + half, :], ACT.Gelu,
                                             bias=w.b1[:, m, e:e + 1]).then_inc(s["gelu"], 1)

        @block.vector
        def _(dve):
            chain = Chain(dve, s["chain"])
            dve.wait_ge(w.sem, w.loaded)
            dve.wait_ge(s["logits"], 1)
            softmax_rows(k, dve, chain, s, ps[:, 7, 0:NT * E].rearrange("p (j e) -> p j e", e=E), pr, mx, sm)
            pick_first(k, chain, pr, f, sel)
            chain.step(nc.vector.scalar_tensor_tensor(rest, sel, -2.0, pr, ALU.mult, ALU.add))
            pick_first(k, chain, rest, f, sel2)
            chain.step(nc.vector.tensor_tensor(sel, sel, sel2, ALU.add))
            chain.step(nc.vector.tensor_tensor(pr, pr, sel, ALU.mult))
            chain.step(nc.vector.tensor_reduce(sm, pr, AX.X, ALU.add))
            chain.step(nc.vector.reciprocal(sm, sm))
            chain.step(nc.vector.tensor_tensor(pr, pr, bc(sm, 2, E), ALU.mult))
            nc.vector.tensor_tensor(comb, pr, bc(w.alpha, 1, NT), ALU.mult).then_inc(s["comb"], 1)
            dve.wait_ge(s["combT"], 1)
            nc.vector.tensor_copy(combT, ps[0:E, 5:7, :].rearrange("p a b -> p (a b)")).then_inc(s["cT"], 1)
            for i in range(4):
                dve.wait_ge(s["bias"], i + 1)
                nc.vector.tensor_tensor(x[:, 2 * i:2 * i + 2, :], x[:, 2 * i:2 * i + 2, :], accumulate_bank(i), ALU.add).then_inc(s["biased"], 1)
            dve.wait_ge(s["biased"], 4)
            for e in range(E):
                for j in range(NT):
                    if j % 2 == 0:
                        dve.wait_ge(s["y"], 4 * e + j // 2 + 1)
                    if e:
                        dve.wait_ge(s["acc"], 8 * (e - 1) + j + 1)
                    nc.vector.scalar_tensor_tensor(x[:, j, :], accumulate_bank(j // 2)[:, j % 2, :], comb[:, j, e:e + 1], x[:, j, :],
                                                   ALU.mult, ALU.add).then_inc(s["acc"], 1)


def load_L1_ffn(k, w, sem):
    d, eng, r = k.dram, k.nc.sync, w.region
    w.g, w.u, w.d = r.take(8, KC, D), r.take(8, KC, D), r.take(8, KC, D)
    w.low = [(r.take(2, D, rows=64), r.take(2, D, rows=64)) for _ in range(3)]
    w.router, w.temp = r.take(KC, 8), r.take(1)
    p = "L1_ffn_"
    eng.dma_start(w.router, d[p + "Wr"].rearrange("(c p) e -> p c e", p=P)).then_inc(sem, 16)
    eng.dma_start(w.temp, row_on_all(d[p + "temperature"])).then_inc(sem, 16)
    for (a, b), n in zip(w.low, "GUD"):
        eng.dma_start(a, d[p + n + "aT"].rearrange("e r d -> r e d")).then_inc(sem, 16)
        eng.dma_start(b, d[p + n + "b"].rearrange("e r d -> r e d")).then_inc(sem, 16)
    for e in range(8):
        for t, n in ((w.g, "Wg"), (w.u, "Wu"), (w.d, "Wd")):
            eng.dma_start(t[:, e], d[p + n][e].rearrange("(c p) i -> p c i", p=P)).then_inc(sem, 16)
    return 16 * (8 + 24)


def stage_L1_ffn(k, w):
    import math
    nc, ps, x, E = k.nc, k.ps, k.x, 8
    CENTER, LOWER, UPPER = 1.0 / math.e, 0.5 - math.log(4.0 / 3.0), 0.5
    k.work.clear()
    r = k.work
    z, dist, fb, sel, sel2, zone, wt = (r.take(NT, E) for _ in range(7))
    f = First(r, E)
    sm, sm2, ne = r.take(NT), r.take(NT), r.take(NT)
    mid = r.take(2, KC, TOK)
    sil = r.take(2, BANK)
    with k.stage("low", "lowed", "logits", "z", "sig", "dist", "expd", "chain", "gu", "silu", "mid", "y", "acc") as (block, s):
        def low_targets():
            return [(t, e, c, ab) for t, ab in zip((w.g, w.u, w.d), w.low) for e in range(2) for c in range(KC)]

        @block.tensor
        def _(pe):
            pe.wait_ge(w.sem, w.loaded)
            route_logits(k, pe, w.router, E, 7, s["logits"])
            for n, (_, e, c, (a, b)) in enumerate(low_targets()):
                last = nc.tensor.matmul(ps[:, n // 2, (n % 2) * D:(n % 2 + 1) * D], a[:, e, c * P:(c + 1) * P], b[:, e, :],
                                        start=True, stop=True)
            last.then_inc(s["low"], 1)
            pe.wait_ge(s["lowed"], 6)
            for e in range(E + 1):
                if e < E:
                    for m in range(2):
                        for half in range(2):
                            n = 4 * e + 2 * m + half
                            if n >= 2:
                                pe.wait_ge(s["mid"], n - 1)
                            for i, wt_ in enumerate((w.g, w.u)):
                                for c in range(KC):
                                    last = nc.tensor.matmul(ps[:, 2 * (n % 2) + i, :], wt_[:, e, c, m * P:(m + 1) * P],
                                                            k.hT[:, c, half * BANK:(half + 1) * BANK], start=c == 0, stop=c == KC - 1)
                            last.then_inc(s["gu"], 1)
                if e >= 1:
                    pe.wait_ge(s["mid"], 4 * e)
                    for i in range(4):
                        if e >= 2:
                            pe.wait_ge(s["acc"], 8 * (e - 2) + 2 * i + 2)
                        for jj in range(2):
                            j = 2 * i + jj
                            for c in range(KC):
                                last = nc.tensor.matmul(ps[:, 4 + i, jj * D:(jj + 1) * D], mid[:, (e - 1) % 2, c, j * P:(j + 1) * P],
                                                        w.d[:, e - 1, c, :], start=c == 0, stop=c == KC - 1)
                        last.then_inc(s["y"], 1)

        @block.scalar
        def _(act):
            act.wait_ge(s["z"], 1)
            nc.scalar.activation(z, z, ACT.Sigmoid).then_inc(s["sig"], 1)
            act.wait_ge(s["dist"], 1)
            nc.scalar.activation(wt, dist, ACT.Exp, scale=-1.0 / 0.1).then_inc(s["expd"], 1)
            nc.scalar.activation(fb, dist, ACT.Exp, scale=-1.0 / 0.3).then_inc(s["expd"], 1)
            for n in range(4 * E):
                act.wait_ge(s["gu"], n + 1)
                if n >= 2:
                    act.wait_ge(s["mid"], n - 1)
                nc.scalar.activation(sil[:, n % 2, :], ps[:, 2 * (n % 2), :], ACT.Silu).then_inc(s["silu"], 1)

        @block.vector
        def _(dve):
            chain = Chain(dve, s["chain"])
            dve.wait_ge(w.sem, w.loaded)
            dve.wait_ge(s["logits"], 1)
            chain.step(nc.vector.reciprocal(w.temp, w.temp))
            nc.vector.tensor_scalar(z, ps[:, 7, 0:NT * E].rearrange("p (j e) -> p j e", e=E), w.temp, None, ALU.mult).then_inc(s["z"], 1)
            dve.wait_ge(s["low"], 1)
            for n in range(0, 12, 2):
                t, e = low_targets()[n][0:2]
                nc.vector.tensor_tensor(t[:, e], t[:, e], ps[:, n // 2, :].rearrange("p (c d) -> p c d", c=2), ALU.add).then_inc(s["lowed"], 1)
            dve.wait_ge(s["sig"], 1)
            chain.step(nc.vector.tensor_scalar(zone, z, LOWER, None, ALU.is_ge))
            chain.step(nc.vector.scalar_tensor_tensor(zone, z, UPPER, zone, ALU.is_le, ALU.mult))
            chain.step(nc.vector.tensor_scalar(dist, z, CENTER, None, ALU.subtract))
            nc.vector.scalar_tensor_tensor(dist, dist, -1.0, dist, ALU.mult, ALU.max).then_inc(s["dist"], 1)
            dve.wait_ge(s["expd"], 2)
            chain.step(nc.vector.tensor_tensor(wt, wt, zone, ALU.mult))
            chain.step(nc.vector.tensor_reduce(sm, wt, AX.X, ALU.add))
            chain.step(nc.vector.tensor_scalar(ne, sm, 1e-8, None, ALU.is_lt))
            pick_first(k, chain, fb, f, sel)
            chain.step(nc.vector.scalar_tensor_tensor(zone, sel, -2.0, fb, ALU.mult, ALU.add))
            pick_first(k, chain, zone, f, sel2)
            chain.step(nc.vector.tensor_tensor(sel, sel, sel2, ALU.add))
            chain.step(nc.vector.tensor_tensor(fb, fb, sel, ALU.mult))
            chain.step(nc.vector.tensor_reduce(sm2, fb, AX.X, ALU.add))
            chain.step(nc.vector.tensor_scalar(sm2, sm2, 1e-8, None, ALU.max))
            chain.step(nc.vector.reciprocal(sm2, sm2))
            chain.step(nc.vector.tensor_tensor(sm2, sm2, ne, ALU.mult))
            chain.step(nc.vector.tensor_tensor(fb, fb, bc(sm2, 2, E), ALU.mult))
            chain.step(nc.vector.tensor_scalar(ne, ne, -1.0, 1.0, ALU.mult, ALU.add))
            chain.step(nc.vector.tensor_tensor(wt, wt, bc(ne, 2, E), ALU.mult))
            chain.step(nc.vector.tensor_tensor(wt, wt, fb, ALU.add))
            chain.step(nc.vector.tensor_reduce(sm, wt, AX.X, ALU.add))
            chain.step(nc.vector.tensor_scalar(sm, sm, 1e-8, None, ALU.max))
            chain.step(nc.vector.reciprocal(sm, sm))
            chain.step(nc.vector.tensor_tensor(wt, wt, bc(sm, 2, E), ALU.mult))

            def products(e):
                for i in range(4):
                    n = 4 * e + i
                    dve.wait_ge(s["silu"], n + 1)
                    if i == 0 and e >= 2:
                        dve.wait_ge(s["y"], 4 * (e - 1))
                    nc.vector.tensor_tensor(mid[:, e % 2, i // 2, (i % 2) * BANK:(i % 2 + 1) * BANK], sil[:, n % 2, :],
                                            ps[:, 2 * (n % 2) + 1, :], ALU.mult).then_inc(s["mid"], 1)

            def accumulate(e):
                for j in range(NT):
                    if j % 2 == 0:
                        dve.wait_ge(s["y"], 4 * e + j // 2 + 1)
                    if e:
                        dve.wait_ge(s["acc"], 8 * (e - 1) + j + 1)
                    nc.vector.scalar_tensor_tensor(x[:, j, :], ps[:, 4 + j // 2, (j % 2) * D:(j % 2 + 1) * D], wt[:, j, e:e + 1], x[:, j, :],
                                                   ALU.mult, ALU.add).then_inc(s["acc"], 1)

            for e in range(E):
                products(e)
                if e:
                    accumulate(e - 1)
            accumulate(E - 1)


def load_L2_ffn(k, w, sem):
    d, eng, r = k.dram, k.nc.sync, w.region
    w.mask = r.take(32, KC, D)
    w.wT, w.router, w.scale = k.fixed.take(KC, D), k.fixed.take(KC, 32), k.fixed.take(D)
    p = "L2_ffn_"
    eng.dma_start(w.wT, d[p + "weightT"].rearrange("(c p) o -> p c o", p=P)).then_inc(sem, 16)
    eng.dma_start(w.router, d[p + "routerT"].rearrange("(c p) e -> p c e", p=P)).then_inc(sem, 16)
    eng.dma_start(w.scale, row_on_all(d[p + "scale"])).then_inc(sem, 16)
    for e in range(32):
        eng.dma_start(w.mask[:, e], d[p + "masksT"][e].rearrange("(c p) o -> p c o", p=P)).then_inc(sem, 16)
    return 16 * 35


def stage_L2_ffn(k, w):
    nc, ps, x, E = k.nc, k.ps, k.x, 32
    MAGIC = 1.5 * 2 ** 23
    k.work.clear()
    r = k.work
    pr, sel = r.take(NT, E), r.take(NT, E)
    f = First(r, E)
    mx, sm = r.take(NT), r.take(NT)
    acc = k.h
    with k.stage("logits", "shifted", "exps", "chain", "ternary", "masked", "y", "acc", "zero", "scaled", "added") as (block, s):
        @block.tensor
        def _(pe):
            pe.wait_ge(w.sem, w.loaded)
            route_logits(k, pe, w.router, E, 7, s["logits"])
            pe.wait_ge(s["shifted"], 1)
            for e in range(E):
                pe.wait_ge(s["masked"], e + 1)
                for i in range(4):
                    n = 4 * e + i
                    if n >= 8:
                        pe.wait_ge(s["acc"], 2 * (n - 8) + 2)
                    for jj in range(2):
                        j = 2 * i + jj
                        for c in range(KC):
                            last = nc.tensor.matmul(ps[:, n % 8, jj * D:(jj + 1) * D], k.hT[:, c, j * P:(j + 1) * P],
                                                    w.mask[:, e, c, :], start=c == 0, stop=c == KC - 1)
                    last.then_inc(s["y"], 1)

        @block.scalar
        def _(act):
            act.wait_ge(s["shifted"], 1)
            nc.scalar.activation(pr, pr, ACT.Exp).then_inc(s["exps"], 1)

        @block.gpsimd
        def _(pool):
            nc.gpsimd.memset(acc, 0.0).then_inc(s["zero"], 1)
            pool.wait_ge(s["ternary"], 1)
            for e in range(E):
                nc.gpsimd.tensor_tensor(w.mask[:, e], w.mask[:, e], w.wT, ALU.mult).then_inc(s["masked"], 1)

        @block.vector
        def _(dve):
            chain = Chain(dve, s["chain"])
            dve.wait_ge(w.sem, w.loaded)
            chain.step(nc.vector.tensor_scalar(w.wT, w.wT, 2.0, 1.0, ALU.mult, ALU.min))
            chain.step(nc.vector.tensor_scalar(w.wT, w.wT, -1.0, MAGIC, ALU.max, ALU.add))
            nc.vector.tensor_scalar(w.wT, w.wT, MAGIC, None, ALU.subtract).then_inc(s["ternary"], 1)
            dve.wait_ge(s["logits"], 1)
            softmax_rows(k, dve, chain, s, ps[:, 7, 0:NT * E].rearrange("p (j e) -> p j e", e=E), pr, mx, sm)
            pick_first(k, chain, pr, f, sel)
            chain.step(nc.vector.tensor_tensor(sel, sel, bc(f.mx, 2, E), ALU.mult))
            dve.wait_ge(s["zero"], 1)
            for e in range(E):
                for j in range(NT):
                    n = 4 * e + j // 2
                    if j % 2 == 0:
                        dve.wait_ge(s["y"], n + 1)
                    if e:
                        dve.wait_ge(s["acc"], 8 * (e - 1) + j + 1)
                    nc.vector.scalar_tensor_tensor(acc[:, j, :], ps[:, n % 8, (j % 2) * D:(j % 2 + 1) * D], sel[:, j, e:e + 1],
                                                   acc[:, j, :], ALU.mult, ALU.add).then_inc(s["acc"], 1)
            dve.wait_ge(s["acc"], 8 * E)
            nc.vector.tensor_tensor(acc, acc, bc(w.scale, 1, NT), ALU.mult).then_inc(s["scaled"], 1)
            dve.wait_ge(s["scaled"], 1)
            nc.vector.tensor_tensor(x, x, acc, ALU.add).then_inc(s["added"], 1)


def load_L3_ffn(k, w, sem):
    d, eng, r = k.dram, k.nc.sync, w.region
    w.a, w.b, w.router = r.take(KC, BANK), r.take(4, D), r.take(KC, 8)
    p = "L3_ffn_"
    eng.dma_start(w.a, d[p + "AT"].rearrange("(c p) r -> p c r", p=P)).then_inc(sem, 16)
    eng.dma_start(w.b, d[p + "BT"].rearrange("(q p) o -> p q o", p=P)).then_inc(sem, 16)
    eng.dma_start(w.router, d[p + "WgT"].rearrange("(c p) e -> p c e", p=P)).then_inc(sem, 16)
    return 48


def stage_L3_ffn(k, w):
    nc, ps, x, E, R = k.nc, k.ps, k.x, 8, 64
    SCALING = 64.0 / 16.0
    k.work.clear()
    r = k.work
    pr, sel = r.take(NT, E), r.take(NT, E)
    f = First(r, E)
    mx, sm = r.take(NT), r.take(NT)
    low, lowT = r.take(2, BANK), r.take(2, BANK)
    with k.stage("logits", "shifted", "exps", "chain", "low", "kept", "turned", "copied", "y", "added") as (block, s):
        @block.tensor
        def _(pe):
            pe.wait_ge(w.sem, w.loaded)
            route_logits(k, pe, w.router, E, 7, s["logits"])
            for i in range(NT + 2):
                if i < NT:
                    if i >= 2:
                        pe.wait_ge(s["kept"], i - 1)
                    for c in range(KC):
                        last = nc.tensor.matmul(ps[:, i % 2, :], k.hT[:, c, i * P:(i + 1) * P], w.a[:, c, :], start=c == 0, stop=c == KC - 1)
                    last.then_inc(s["low"], 1)
                if 1 <= i <= NT:
                    j = i - 1
                    pe.wait_ge(s["kept"], j + 1)
                    if j >= 2:
                        pe.wait_ge(s["copied"], j - 1)
                    for q in range(4):
                        last = nc.tensor.transpose(ps[:, 2 + j % 2, q * P:(q + 1) * P], low[:, j % 2, q * P:(q + 1) * P], k.ident)
                    last.then_inc(s["turned"], 1)
                if i >= 2:
                    j = i - 2
                    pe.wait_ge(s["copied"], j + 1)
                    if j >= 2:
                        pe.wait_ge(s["added"], j - 1)
                    for q in range(4):
                        last = nc.tensor.matmul(ps[:, 4 + j % 2, 0:D], lowT[:, j % 2, q * P:(q + 1) * P], w.b[:, q, :], start=q == 0, stop=q == 3)
                    last.then_inc(s["y"], 1)

        @block.scalar
        def _(act):
            act.wait_ge(s["shifted"], 1)
            nc.scalar.activation(pr, pr, ACT.Exp).then_inc(s["exps"], 1)
            for j in range(NT):
                act.wait_ge(s["turned"], j + 1)
                if j >= 2:
                    act.wait_ge(s["y"], j - 1)
                nc.scalar.copy(lowT[:, j % 2, :], ps[:, 2 + j % 2, :]).then_inc(s["copied"], 1)

        @block.vector
        def _(dve):
            chain = Chain(dve, s["chain"])
            dve.wait_ge(s["logits"], 1)
            softmax_rows(k, dve, chain, s, ps[:, 7, 0:NT * E].rearrange("p (j e) -> p j e", e=E), pr, mx, sm)
            pick_first(k, chain, pr, f, sel)
            chain.step(nc.vector.tensor_tensor(sel, sel, bc(f.mx, 2, E), ALU.mult))
            chain.step(nc.vector.tensor_scalar(sel, sel, SCALING, None, ALU.mult))
            for j in range(NT + 2):
                if j < NT:
                    dve.wait_ge(s["low"], j + 1)
                    if j >= 2:
                        dve.wait_ge(s["turned"], j - 1)
                    nc.vector.tensor_tensor(low[:, j % 2, :].rearrange("p (e r) -> p e r", r=R),
                                            ps[:, j % 2, :].rearrange("p (e r) -> p e r", r=R), bc(sel[:, j, :], 2, R), ALU.mult).then_inc(s["kept"], 1)
                if j >= 2:
                    dve.wait_ge(s["y"], j - 1)
                    nc.vector.tensor_tensor(x[:, j - 2, :], x[:, j - 2, :], ps[:, 4 + j % 2, 0:D], ALU.add).then_inc(s["added"], 1)



def load_L2_attn(k, w, sem):
    d, eng, r = k.dram, k.nc.sync, w.region
    w.q, w.k, w.v, w.o = (r.take(KC, D) for _ in range(4))
    w.bias = r.take(3, KC)
    w.bo, w.pmask = r.take(D), r.take(2)
    p = "L2_attn_"
    for t, n in ((w.q, "Wq"), (w.k, "Wk"), (w.v, "Wv"), (w.o, "Wo")):
        eng.dma_start(t, d[p + n].rearrange("(c p) o -> p c o", p=P)).then_inc(sem, 16)
    eng.dma_start(w.bias, d[p + "bias"]).then_inc(sem, 16)
    eng.dma_start(w.bo, row_on_all(d[p + "bo"])).then_inc(sem, 16)
    eng.dma_start(w.pmask, d["const_pmask"]).then_inc(sem, 16)
    return 16 * 7


def stage_L2_attn(k, w):
    nc, ps, x = k.nc, k.ps, k.x
    k.work.clear()
    r = w.region
    qT, kexp = r.take(KC, TOK), r.take(KC, 2, TOK)
    vblk = r.take(BATCH, 8, 2, 16)
    bk = r.take(2, KC)
    yT = k.work.take(KC, TOK)
    pr, pT = k.work.take(2, 16, SEQ), k.work.take(2, NT, P)
    mx, sm, rs = k.work.take(2, 16), k.work.take(2, 16), k.work.take(2, 16)
    with k.stage("bk", "qk", "copied", "xb") as (block, s):
        @block.tensor
        def _(pe):
            pe.wait_ge(w.sem, w.loaded)
            for i, t in enumerate((w.q, w.k)):
                for m in range(2):
                    for half in range(2):
                        for c in range(KC):
                            last = nc.tensor.matmul(ps[:, 4 * i + 2 * m + half, :], t[:, c, m * P:(m + 1) * P],
                                                    k.hT[:, c, half * BANK:(half + 1) * BANK], start=c == 0, stop=c == KC - 1)
                    last.then_inc(s["qk"], 1)

        @block.gpsimd
        def _(pool):
            pool.wait_ge(w.sem, w.loaded)
            nc.gpsimd.tensor_tensor(x, x, bc(w.bo, 1, NT), ALU.add).then_inc(s["xb"], 1)

        @block.vector
        def _(dve):
            dve.wait_ge(w.sem, w.loaded)
            for g in range(2):
                nc.vector.tensor_scalar(bk[:, g, :], w.bias[:, 1, :], w.pmask[:, g:g + 1], None, ALU.mult).then_inc(s["bk"], 1)
            for m in range(2):
                dve.wait_ge(s["qk"], m + 1)
                nc.vector.tensor_scalar(qT[:, m, :], ps[:, 2 * m:2 * m + 2, :].rearrange("p a b -> p (a b)"), w.bias[:, 0, m:m + 1], None,
                                        ALU.add).then_inc(s["copied"], 1)

        @block.scalar
        def _(act):
            act.wait_ge(w.sem, w.loaded)
            act.wait_ge(s["bk"], 2)
            for m in range(2):
                act.wait_ge(s["qk"], m + 3)
                for g in range(2):
                    nc.scalar.activation(kexp[:, m, g, :], ps[:, 4 + 2 * m:6 + 2 * m, :].rearrange("p a b -> p (a b)"), ACT.Identity,
                                         bias=bk[:, g, m:m + 1], scale=w.pmask[:, g:g + 1]).then_inc(s["copied"], 1)

    with k.stage("v", "vzero", "vals", "scored", "maxed", "centred", "expd", "summed", "recip", "probs", "turned", "copied", "pv",
                 "yT", "out", "added") as (block, s):
        @block.tensor
        def _(pe):
            for b in range(BATCH):
                for g in range(2):
                    for c in range(KC):
                        last = nc.tensor.matmul(ps[64 * g:64 * g + 64, b // 4, (b % 4) * P:(b % 4 + 1) * P],
                                                k.hT[:, c, b * SEQ:(b + 1) * SEQ], w.v[:, c, g * P:(g + 1) * P],
                                                start=c == 0, stop=c == KC - 1, tile_position=(0, 64 * g))
                if b % 4 == 3:
                    last.then_inc(s["v"], 1)

            def scores(u):
                c, i = divmod(u, 4)
                if u == 0:
                    pe.wait_ge(s["vals"], 4)
                else:
                    pe.wait_ge(s["centred"], u)
                rows = slice(32 * i, 32 * i + 32)
                for bank in range(2):
                    nc.tensor.matmul(ps[:, bank, :], k.ident16, k.causal, start=True, stop=False, skip_group_check=True)
                for b in range(BATCH):
                    j = b // 2
                    last = nc.tensor.matmul(ps[64 * (b % 2):64 * (b % 2) + 64, j // 4, (j % 4) * P:(j % 4 + 1) * P],
                                            qT[rows, c, b * SEQ:(b + 1) * SEQ], kexp[rows, c, :, b * SEQ:(b + 1) * SEQ],
                                            start=False, stop=True, skip_group_check=True, tile_position=(32 * i, 64 * (b % 2)))
                last.then_inc(s["scored"], 1)

            def turn(u):
                pe.wait_ge(s["probs"], u + 1)
                if u:
                    pe.wait_ge(s["copied"], 2 * u)
                for j in range(NT):
                    last = nc.tensor.transpose(ps[:, 2 + j // 4, (j % 4) * P:(j % 4 + 1) * P],
                                               pr[:, u % 2, 2 * j:2 * j + 2, :].rearrange("p a t -> p (a t)"), k.ident)
                last.then_inc(s["turned"], 1)

            def weigh(u):
                c, i = divmod(u, 4)
                pe.wait_ge(s["copied"], 2 * u + 2)
                for b in range(BATCH):
                    last = nc.tensor.matmul(ps[32 * i:32 * i + 32, 4 + 2 * c + b // 8, (b % 8) * SEQ:(b % 8 + 1) * SEQ],
                                            vblk[:, b, u, :, :].rearrange("p g d -> p (g d)"),
                                            pT[:, u % 2, b // 2, 64 * (b % 2):64 * (b % 2) + 64], start=True, stop=True,
                                            tile_position=(0, 32 * i))
                last.then_inc(s["pv"], 1)

            for u in range(8 + 2):
                if u < 8:
                    scores(u)
                if 1 <= u <= 8:
                    turn(u - 1)
                if u >= 2:
                    weigh(u - 2)
            pe.wait_ge(s["yT"], KC)
            pe.wait_ge(s["centred"], 8)
            pe.wait_ge(s["copied"], 16)
            for j in range(NT):
                for c in range(KC):
                    last = nc.tensor.matmul(ps[:, j // 2, (j % 2) * D:(j % 2 + 1) * D], yT[:, c, j * P:(j + 1) * P], w.o[:, c, :],
                                            start=c == 0, stop=c == KC - 1)
                if j % 2:
                    last.then_inc(s["out"], 1)

        @block.gpsimd
        def _(pool):
            nc.gpsimd.memset(vblk, 0.0).then_inc(s["vzero"], 1)

        def copy_turned(act, u):
            act.wait_ge(s["turned"], u + 1)
            if u >= 2:
                act.wait_ge(s["pv"], u - 1)
            for n in range(2):
                nc.scalar.copy(pT[:, u % 2, 4 * n:4 * n + 4, :].rearrange("p a b -> p (a b)"), ps[:, 2 + n, :]).then_inc(s["copied"], 1)

        def copy_out(act, c):
            act.wait_ge(s["pv"], 4 * c + 4)
            nc.scalar.activation(yT[:, c, :], ps[:, 4 + 2 * c:6 + 2 * c, :].rearrange("p a b -> p (a b)"), ACT.Identity,
                                 bias=w.bias[:, 2, c:c + 1]).then_inc(s["yT"], 1)

        @block.scalar
        def _(act):
            for u in range(8):
                act.wait_ge(s["centred"], u + 1)
                nc.scalar.activation(pr[:, u % 2, :, :], pr[:, u % 2, :, :], ACT.Exp, scale=0.25).then_inc(s["expd"], 1)
                if u >= 1:
                    copy_turned(act, u - 1)
                if u == 5:
                    copy_out(act, 0)
            copy_turned(act, 7)
            copy_out(act, 1)

        @block.vector
        def _(dve):
            dve.wait_ge(s["vzero"], 1)
            for n in range(4):
                dve.wait_ge(s["v"], n + 1)
                for g in range(2):
                    rows = slice(64 * g, 64 * g + 64)
                    ins = nc.vector.tensor_copy(vblk[rows, 4 * n:4 * n + 4, :, g, :],
                                                ps[rows, n, :].rearrange("p (b h d) -> p b h d", b=4, d=16))
                ins.then_inc(s["vals"], 1)

            def centre(u):
                sc = ps[:, 0:2, :].rearrange("p a (h t) -> p (a h) t", t=SEQ)
                dve.wait_ge(s["scored"], u + 1)
                nc.vector.tensor_reduce(mx[:, u % 2, :], sc, AX.X, ALU.max).then_inc(s["maxed"], 1)
                dve.wait_ge(s["maxed"], u + 1)
                if u >= 2:
                    dve.wait_ge(s["turned"], u - 1)
                nc.vector.tensor_tensor(pr[:, u % 2, :, :], sc, bc(mx[:, u % 2, :], 2, SEQ), ALU.subtract).then_inc(s["centred"], 1)

            def normalise(u):
                p, a, b = pr[:, u % 2, :, :], sm[:, u % 2, :], rs[:, u % 2, :]
                dve.wait_ge(s["expd"], u + 1)
                nc.vector.tensor_reduce(a, p, AX.X, ALU.add).then_inc(s["summed"], 1)
                dve.wait_ge(s["summed"], u + 1)
                nc.vector.reciprocal(b, a).then_inc(s["recip"], 1)
                dve.wait_ge(s["recip"], u + 1)
                nc.vector.tensor_tensor(p, p, bc(b, 2, SEQ), ALU.mult).then_inc(s["probs"], 1)

            for u in range(8):
                centre(u)
                normalise(u)
            for i in range(4):
                dve.wait_ge(s["out"], i + 1)
                xv = x[:, 2 * i:2 * i + 2, :].rearrange("p a b -> p (a b)")
                nc.vector.tensor_tensor(xv, xv, ps[:, i, :], ALU.add).then_inc(s["added"], 1)



DH0, DV0, NH0 = 32, 64, 6
LEVELS = 6


def load_L0_attn(k, w, sem):
    d, eng, r = k.dram, k.nc.sync, w.region
    w.qkv = r.take(KC, 768)
    w.gate = r.take(KC, 384)
    w.ba = r.take(KC, 12)
    w.o = r.take(3, D)
    w.conv = r.take(7, 4)
    w.rows = r.take(2, NH0)
    w.norm = r.take(DV0)
    w.tri = r.take(2, P)
    w.level = r.take(LEVELS, P)
    w.head = r.take(96)
    p = "L0_attn_"
    eng.dma_start(w.qkv, d[p + "WqkvT"].rearrange("(c p) s -> p c s", p=P)).then_inc(sem, 16)
    eng.dma_start(w.gate, d[p + "WgT"].rearrange("(c p) s -> p c s", p=P)).then_inc(sem, 16)
    eng.dma_start(w.ba, d[p + "WbaT"].rearrange("(c p) s -> p c s", p=P)).then_inc(sem, 16)
    eng.dma_start(w.o, d[p + "WoT"].rearrange("(c p) s -> p c s", p=P)).then_inc(sem, 16)
    eng.dma_start(w.conv[0:96, 0:4, :], d[p + "conv_qk"]).then_inc(sem, 16)
    eng.dma_start(w.conv[:, 4:7, :], d[p + "conv_v"]).then_inc(sem, 16)
    eng.dma_start(w.rows[:, 0, :], row_on_all(d[p + "A_log"])).then_inc(sem, 16)
    eng.dma_start(w.rows[:, 1, :], row_on_all(d[p + "dt_bias"])).then_inc(sem, 16)
    eng.dma_start(w.norm, row_on_all(d[p + "norm_w"])).then_inc(sem, 16)
    eng.dma_start(w.tri, d["const_tri"]).then_inc(sem, 16)
    eng.dma_start(w.level, d["const_level"]).then_inc(sem, 16)
    eng.dma_start(w.head[0:96, :], d["const_head"]).then_inc(sem, 16)
    return 16 * 12


def stage_L0_attn(k, w):
    nc, ps, x = k.nc, k.ps, k.x
    k.work.clear()
    r = w.region
    gate = r.take(NT, 384)
    vt = r.take(NT, 384)
    beta, decay = r.take(NT, NH0), r.take(NT, NH0)
    qk = k.work.take(4, TOK, rows=96)
    mark = k.work.at, r.at
    vf = r.take(3, TOK)
    small = [k.work.take(NT, NH0) for _ in range(4)]
    sq = k.work.take(2, TOK, rows=96)
    widths = [96] * 4 + [P] * 3
    offs = [96 * n for n in range(4)] + [384 + P * n for n in range(3)]
    dst = lambda n: qk[:, n, :] if n < 4 else vf[:, n - 4, :]
    with k.stage("proj", "conv", "silu", "gate", "gated", "ba", "bac") as (block, s):
        @block.tensor
        def _(pe):
            pe.wait_ge(w.sem, w.loaded)
            for n in range(7):
                if n >= 3:
                    pe.wait_ge(s["conv"], 4 * (n - 3) + 4)
                for half in range(2):
                    for c in range(KC):
                        last = nc.tensor.matmul(ps[0:widths[n], 2 * (n % 3) + half, :], w.qkv[:, c, offs[n]:offs[n] + widths[n]],
                                                k.hT[:, c, half * BANK:(half + 1) * BANK], start=c == 0, stop=c == KC - 1)
                last.then_inc(s["proj"], 1)
                tiles = range(n, n + 1) if n < 6 else range(6, 8)
                for j in tiles:
                    if j >= 2:
                        pe.wait_ge(s["gated"], j - 1)
                    for c in range(KC):
                        last = nc.tensor.matmul(ps[:, 6 + j % 2, 0:384], k.hT[:, c, j * P:(j + 1) * P], w.gate[:, c, :],
                                                start=c == 0, stop=c == KC - 1)
                    last.then_inc(s["gate"], 1)
            pe.wait_ge(s["gated"], NT)
            for j in range(NT):
                for c in range(KC):
                    last = nc.tensor.matmul(ps[:, 6, 12 * j:12 * j + 12], k.hT[:, c, j * P:(j + 1) * P], w.ba[:, c, :],
                                            start=c == 0, stop=c == KC - 1)
            last.then_inc(s["ba"], 1)

        @block.vector
        def _(dve):
            for n in range(7):
                m = widths[n]
                dve.wait_ge(s["proj"], n + 1)
                src = ps[0:m, 2 * (n % 3):2 * (n % 3) + 2, :].rearrange("p a (b t) -> p (a b) t", t=SEQ)
                y = dst(n)[0:m, :].rearrange("p (b t) -> p b t", t=SEQ)
                taps = w.conv[0:m, n, :]
                nc.vector.tensor_scalar(y, src, taps[:, 3:4], None, ALU.mult).then_inc(s["conv"], 1)
                for back in range(1, 4):
                    dve.wait_ge(s["conv"], 4 * n + back)
                    nc.vector.scalar_tensor_tensor(y[:, :, back:], src[:, :, :SEQ - back], taps[:, 3 - back:4 - back], y[:, :, back:],
                                                   ALU.mult, ALU.add).then_inc(s["conv"], 1)

        @block.scalar
        def _(act):
            for n in range(7):
                for j in (range(n, n + 1) if n < 6 else range(6, 8)):
                    act.wait_ge(s["gate"], j + 1)
                    nc.scalar.activation(gate[:, j, :], ps[:, 6 + j % 2, 0:384], ACT.Silu).then_inc(s["gated"], 1)
                act.wait_ge(s["conv"], 4 * n + 4)
                m = widths[n]
                nc.scalar.activation(dst(n)[0:m, :], dst(n)[0:m, :], ACT.Silu).then_inc(s["silu"], 1)
            act.wait_ge(s["ba"], 1)
            ba = ps[:, 6, 0:96].rearrange("p (j e) -> p j e", e=12)
            nc.scalar.copy(decay, ba[:, :, 6:12]).then_inc(s["bac"], 1)
            nc.scalar.activation(beta, ba[:, :, 0:6], ACT.Sigmoid).then_inc(s["bac"], 1)

    z, az, e, lg = small
    rinv = k.hT[0:96]
    with k.stage("z", "az", "e", "ln", "ea", "g", "sq", "ss", "lns", "rinv", "unit", "vT", "vc", "wn") as (block, s):
        @block.tensor
        def _(pe):
            for n in range(4):
                pe.wait_ge(s["sq"], n + 1)
                if n >= 2:
                    pe.wait_ge(s["lns"], n - 1)
                for half in range(2):
                    last = nc.tensor.matmul(ps[0:96, 2 * (n % 2) + half, :], w.head[0:96, :], sq[:, n % 2, half * BANK:(half + 1) * BANK],
                                            start=True, stop=True)
                last.then_inc(s["ss"], 1)
            for j in range(NT):
                if j >= 4:
                    pe.wait_ge(s["vc"], j - 3)
                for c in range(3):
                    last = nc.tensor.transpose(ps[:, 4 + j % 4, c * P:(c + 1) * P], vf[:, c, j * P:(j + 1) * P], k.ident)
                last.then_inc(s["vT"], 1)

        @block.gpsimd
        def _(pool):
            nc.gpsimd.tensor_tensor(gate.rearrange("p j (h d) -> p (j h) d", d=DV0), gate.rearrange("p j (h d) -> p (j h) d", d=DV0),
                                    bc(w.norm, 1, NT * NH0), ALU.mult).then_inc(s["wn"], 1)

        @block.scalar
        def _(act):
            act.wait_ge(s["az"], 1)
            nc.scalar.activation(e, az, ACT.Exp, scale=-1.0).then_inc(s["e"], 1)
            nc.scalar.activation(w.rows[:, 0, :], w.rows[:, 0, :], ACT.Exp).then_inc(s["ea"], 1)
            act.wait_ge(s["e"], 1)
            act.wait_ge(s["e"], 2)
            nc.scalar.activation(lg, e, ACT.Ln).then_inc(s["ln"], 1)
            for n in range(4):
                act.wait_ge(s["ss"], n + 1)
                if n >= 2:
                    act.wait_ge(s["unit"], n - 1)
                nc.scalar.activation(rinv[:, n % 2, :], ps[0:96, 2 * (n % 2):2 * (n % 2) + 2, :].rearrange("p a b -> p (a b)"), ACT.Ln,
                                     bias=1e-6).then_inc(s["lns"], 1)
                act.wait_ge(s["lns"], n + 1)
                nc.scalar.activation(rinv[:, n % 2, :], rinv[:, n % 2, :], ACT.Exp, scale=-0.5).then_inc(s["rinv"], 1)

        @block.vector
        def _(dve):
            nc.vector.tensor_tensor(sq[:, 0, :], qk[:, 0, :], qk[:, 0, :], ALU.mult).then_inc(s["sq"], 1)
            nc.vector.tensor_tensor(sq[:, 1, :], qk[:, 1, :], qk[:, 1, :], ALU.mult).then_inc(s["sq"], 1)
            nc.vector.tensor_tensor(z, decay, bc(w.rows[:, 1, :], 1, NT), ALU.add).then_inc(s["z"], 1)
            dve.wait_ge(s["z"], 1)
            nc.vector.scalar_tensor_tensor(az, z, -1.0, z, ALU.mult, ALU.max).then_inc(s["az"], 1)
            dve.wait_ge(s["e"], 1)
            nc.vector.tensor_scalar(e, e, 1.0, None, ALU.add).then_inc(s["e"], 1)
            dve.wait_ge(s["ln"], 1)
            nc.vector.scalar_tensor_tensor(z, z, 0.0, lg, ALU.max, ALU.add).then_inc(s["z"], 1)
            dve.wait_ge(s["z"], 2)
            dve.wait_ge(s["ea"], 1)
            nc.vector.scalar_tensor_tensor(decay, z, -1.0, bc(w.rows[:, 0, :], 1, NT), ALU.mult, ALU.mult).then_inc(s["g"], 1)
            for n in range(4):
                if n + 2 < 4:
                    dve.wait_ge(s["ss"], n + 1)
                    nc.vector.tensor_tensor(sq[:, n % 2, :], qk[:, n + 2, :], qk[:, n + 2, :], ALU.mult).then_inc(s["sq"], 1)
                dve.wait_ge(s["rinv"], n + 1)
                rv = rinv[:, n % 2, :]
                if n < 2:
                    nc.vector.scalar_tensor_tensor(qk[:, n, :], rv, DH0 ** -0.5, qk[:, n, :], ALU.mult, ALU.mult).then_inc(s["unit"], 1)
                else:
                    nc.vector.tensor_tensor(qk[:, n, :], rv, qk[:, n, :], ALU.mult).then_inc(s["unit"], 1)
            for j in range(NT):
                dve.wait_ge(s["vT"], j + 1)
                nc.vector.tensor_copy(vt[:, j, :], ps[:, 4 + j % 4, 0:384]).then_inc(s["vc"], 1)

    k.work.at, r.at = mark
    ot = k.hT.rearrange("p c t -> p (c t)")
    o_tm = k.work.take(NT, 384)
    spare = Region(k.h.rearrange("p j d -> p (j d)"), NT * D)
    dec = [k.work.take(4, P) for _ in range(2)]
    gm = [spare.take(4, P) for _ in range(2)]
    F = [k.work.take(4, P) for _ in range(2)]
    A = [k.work.take(4, P) for _ in range(2)]
    hTs = Region(ot, KC * TOK)
    Rm = [hTs.take(4, P) for _ in range(2)]
    Fl = [[Rm[a]] + [r.take(4, P) for _ in range(LEVELS - 1)] for a in range(2)]
    Tm = [hTs.take(4, P) for _ in range(2)]
    Wm = [spare.take(4, P) for _ in range(2)]
    Um = [k.work.take(4, DV0) for _ in range(2)]
    flat = lambda t: t.rearrange("p a b -> p (a b)")
    ident4 = bc(k.ident, 1, 4)
    names = ("gm", "X", "KQ", "expd", "dec", "F", "A", "Fl", "R1", "turned", "T1", "W", "Ws", "XX", "R", "T", "U", "Us", "O", "Os")
    with k.stage(*names) as (block, s):
        def nth(g, step, per):
            return 2 * per * (g // 2) + 2 * (step - 1) + g % 2 + 1

        def unit(g, i):
            return g // 2, 4 * (g % 2) + i

        @block.tensor
        def _(pe):
            def products(g):
                a = g % 2
                h = g // 2
                n, rows = h // 3, slice(32 * (h % 3), 32 * (h % 3) + 32)
                pe.wait_ge(s["gm"], g + 1)
                if g >= 2:
                    pe.wait_ge(s["Us"], g - 1)
                    pe.wait_ge(s["Os"], g - 1)
                    pe.wait_ge(s["R"], nth(g - 2, 5, 5))
                nc.tensor.matmul(ps[:, 3 * a, :], w.tri[:, 0, :], flat(gm[a]), start=True, stop=True).then_inc(s["X"], 1)
                for q, bank in ((2, 1), (0, 2)):
                    for i in range(4):
                        j = unit(g, i)[1]
                        last = nc.tensor.matmul(ps[:, 3 * a + bank, i * P:(i + 1) * P], qk[rows, 2 + n, j * P:(j + 1) * P],
                                                qk[rows, q + n, j * P:(j + 1) * P], start=True, stop=True,
                                                tile_position=(32 * (h % 3), 0))
                last.then_inc(s["KQ"], 1)

            def turn(g):
                a = g % 2
                pe.wait_ge(s["R1"], g + 1)
                pe.wait_ge(s["F"], g + 1)
                for i in range(4):
                    last = nc.tensor.transpose(ps[:, 3 * a + 1, i * P:(i + 1) * P], Rm[a][:, i, :], k.ident)
                last.then_inc(s["turned"], 1)

            def first(g, l):
                a = g % 2
                pe.wait_ge(s["Fl"], nth(g, l + 1, 6))
                pe.wait_ge(s["T1"], g + 1)
                if l >= 2:
                    pe.wait_ge(s["T"], nth(g, l - 1, 4))
                for i in range(4):
                    last = nc.tensor.matmul(ps[:, 3 * a, i * P:(i + 1) * P], Fl[a][l][:, i, :], Tm[a][:, i, :], start=True, stop=True)
                last.then_inc(s["W"], 1)

            def second(g, l):
                a = g % 2
                pe.wait_ge(s["Ws"], nth(g, l, 5))
                if l == 1:
                    pe.wait_ge(s["A"], g + 1)
                if l >= 2:
                    pe.wait_ge(s["R"], nth(g, l - 1, 5))
                if l < 5:
                    for i in range(4):
                        nc.tensor.matmul(ps[:, 3 * a + 1, i * P:(i + 1) * P], Rm[a][:, i, :], Wm[a][:, i, :], start=True, stop=True)
                for i in range(4):
                    last = nc.tensor.matmul(ps[:, 3 * a + 2, i * P:(i + 1) * P], Wm[a][:, i, :], Rm[a][:, i, :], start=True, stop=True)
                last.then_inc(s["XX"], 1)

            def solve(g):
                a, h = g % 2, g // 2
                pe.wait_ge(s["R"], nth(g, 5, 5))
                for i in range(4):
                    j = unit(g, i)[1]
                    last = nc.tensor.matmul(ps[:, 3 * a, i * DV0:(i + 1) * DV0], Rm[a][:, i, :], vt[:, j, h * DV0:(h + 1) * DV0],
                                            start=True, stop=True)
                last.then_inc(s["U"], 1)

            def outputs(g):
                a = g % 2
                pe.wait_ge(s["Us"], g + 1)
                for i in range(4):
                    last = nc.tensor.matmul(ps[:, 3 * a + 1, i * DV0:(i + 1) * DV0], A[a][:, i, :], Um[a][:, i, :], start=True, stop=True)
                last.then_inc(s["O"], 1)

            for pair in range(6):
                for g in (2 * pair, 2 * pair + 1):
                    products(g)
                for g in (2 * pair, 2 * pair + 1):
                    turn(g)
                for l in range(1, 6):
                    for g in (2 * pair, 2 * pair + 1):
                        first(g, l)
                    for g in (2 * pair, 2 * pair + 1):
                        second(g, l)
                for g in (2 * pair, 2 * pair + 1):
                    solve(g)
                for g in (2 * pair, 2 * pair + 1):
                    outputs(g)

        @block.gpsimd
        def _(pool):
            for pair in range(6):
                for g in (2 * pair, 2 * pair + 1):
                    a = g % 2
                    if g >= 2:
                        pool.wait_ge(s["X"], g - 1)
                    for i in range(4):
                        h, j = unit(g, i)
                        last = nc.gpsimd.tensor_scalar(gm[a][:, i, :], w.tri[:, 1, :], decay[:, j, h:h + 1], None, ALU.mult)
                    last.then_inc(s["gm"], 1)
                for l in range(6):
                    for g in (2 * pair, 2 * pair + 1):
                        a = g % 2
                        pool.wait_ge(s["F"], g + 1)
                        if g >= 2:
                            pool.wait_ge(s["U"], g - 1)
                            pool.wait_ge(s["W"], nth(g - 2, 5, 5))
                        nc.gpsimd.tensor_tensor(Fl[a][l], F[a], bc(w.level[:, l, :], 1, 4), ALU.mult).then_inc(s["Fl"], 1)

        @block.scalar
        def _(act):
            for pair in range(6):
                for g in (2 * pair, 2 * pair + 1):
                    a = g % 2
                    act.wait_ge(s["X"], g + 1)
                    if g >= 2:
                        act.wait_ge(s["A"], g - 1)
                    nc.scalar.activation(flat(dec[a]), ps[:, 3 * a, :], ACT.Exp).then_inc(s["expd"], 1)
                for l in range(1, 6):
                    for g in (2 * pair, 2 * pair + 1):
                        a = g % 2
                        act.wait_ge(s["W"], nth(g, l, 5))
                        if l >= 2:
                            act.wait_ge(s["XX"], nth(g, l - 1, 5))
                        nc.scalar.copy(flat(Wm[a]), ps[:, 3 * a, :]).then_inc(s["Ws"], 1)
                for g in (2 * pair, 2 * pair + 1):
                    a = g % 2
                    act.wait_ge(s["U"], g + 1)
                    if g >= 2:
                        act.wait_ge(s["O"], g - 1)
                    nc.scalar.copy(flat(Um[a]), ps[:, 3 * a, 0:4 * DV0]).then_inc(s["Us"], 1)
                for g in (2 * pair, 2 * pair + 1):
                    a = g % 2
                    h, j0 = unit(g, 0)
                    act.wait_ge(s["O"], g + 1)
                    nc.scalar.copy(o_tm[:, j0:j0 + 4, h * DV0:(h + 1) * DV0],
                                   ps[:, 3 * a + 1, 0:4 * DV0].rearrange("p (i d) -> p i d", d=DV0)).then_inc(s["Os"], 1)

        @block.vector
        def _(dve):
            for pair in range(6):
                for g in (2 * pair, 2 * pair + 1):
                    a = g % 2
                    dve.wait_ge(s["expd"], g + 1)
                    for i in range(4):
                        h, j = unit(g, i)
                        last = nc.vector.scalar_tensor_tensor(dec[a][:, i, :], dec[a][:, i, :], beta[:, j, h:h + 1], w.tri[:, 1, :],
                                                              ALU.mult, ALU.mult)
                    last.then_inc(s["dec"], 1)
                    dve.wait_ge(s["dec"], g + 1)
                    dve.wait_ge(s["KQ"], g + 1)
                    if g >= 2:
                        dve.wait_ge(s["Fl"], nth(g - 2, 6, 6))
                        dve.wait_ge(s["O"], g - 1)
                    nc.vector.tensor_tensor(flat(F[a]), flat(dec[a]), ps[:, 3 * a + 1, :], ALU.mult).then_inc(s["F"], 1)
                    nc.vector.tensor_tensor(flat(A[a]), flat(dec[a]), ps[:, 3 * a + 2, :], ALU.mult).then_inc(s["A"], 1)
                for g in (2 * pair, 2 * pair + 1):
                    a = g % 2
                    dve.wait_ge(s["Fl"], nth(g, 1, 6))
                    nc.vector.tensor_tensor(Rm[a], ident4, Fl[a][0], ALU.subtract).then_inc(s["R1"], 1)
                for g in (2 * pair, 2 * pair + 1):
                    a = g % 2
                    dve.wait_ge(s["turned"], g + 1)
                    nc.vector.tensor_copy(flat(Tm[a]), ps[:, 3 * a + 1, :]).then_inc(s["T1"], 1)
                for l in range(1, 6):
                    for g in (2 * pair, 2 * pair + 1):
                        a = g % 2
                        dve.wait_ge(s["XX"], nth(g, l, 5))
                        if l < 5:
                            nc.vector.tensor_tensor(flat(Tm[a]), flat(Tm[a]), ps[:, 3 * a + 1, :], ALU.subtract).then_inc(s["T"], 1)
                        nc.vector.tensor_tensor(flat(Rm[a]), flat(Rm[a]), ps[:, 3 * a + 2, :], ALU.subtract).then_inc(s["R"], 1)

    r.at = mark[1]
    k.work.at = mark[0] + NT * 384
    sq, oT = r.take(NT, 384), k.work.take(NT, 3, P)
    ss, std = k.work.take(NT, NH0), k.work.take(NT, NH0)
    heads = lambda t: t.rearrange("p j (h d) -> p j h d", d=DV0)
    with k.stage("sq", "ss", "eps", "std", "rstd", "on", "og", "turned", "copied", "y", "added") as (block, s):
        @block.scalar
        def _(act):
            nc.scalar.activation(sq, o_tm, ACT.Square).then_inc(s["sq"], 1)
            act.wait_ge(s["eps"], 1)
            nc.scalar.activation(std, ss, ACT.Sqrt).then_inc(s["std"], 1)
            for j in range(NT):
                act.wait_ge(s["turned"], j + 1)
                nc.scalar.copy(oT[:, j, :, :].rearrange("p a b -> p (a b)"), ps[:, j % 4, 0:384]).then_inc(s["copied"], 1)

        def add(dve, j):
            dve.wait_ge(s["y"], j + 1)
            nc.vector.tensor_tensor(x[:, j, :], x[:, j, :], ps[:, 4 + j % 4, 0:D], ALU.add).then_inc(s["added"], 1)

        @block.vector
        def _(dve):
            dve.wait_ge(s["sq"], 1)
            nc.vector.tensor_reduce(ss.rearrange("p j h -> p (j h)"), sq.rearrange("p j (h d) -> p (j h) d", d=DV0), AX.X, ALU.add).then_inc(s["ss"], 1)
            dve.wait_ge(s["ss"], 1)
            nc.vector.tensor_scalar(ss, ss, 1.0 / DV0, 1e-5, ALU.mult, ALU.add).then_inc(s["eps"], 1)
            dve.wait_ge(s["std"], 1)
            nc.vector.reciprocal(ss, std).then_inc(s["rstd"], 1)
            dve.wait_ge(s["rstd"], 1)
            for j in range(NT):
                nc.vector.tensor_tensor(heads(o_tm)[:, j], heads(o_tm)[:, j], bc(ss[:, j, :], 2, DV0), ALU.mult).then_inc(s["on"], 1)
                dve.wait_ge(s["on"], j + 1)
                nc.vector.tensor_tensor(o_tm[:, j, :], o_tm[:, j, :], gate[:, j, :], ALU.mult).then_inc(s["og"], 1)
                if j >= 2:
                    add(dve, j - 2)
            for j in range(NT - 2, NT):
                add(dve, j)

        @block.tensor
        def _(pe):
            for j in range(NT + 1):
                if j < NT:
                    pe.wait_ge(s["og"], j + 1)
                    if j >= 4:
                        pe.wait_ge(s["copied"], j - 3)
                    for c in range(3):
                        last = nc.tensor.transpose(ps[:, j % 4, c * P:(c + 1) * P], o_tm[:, j, c * P:(c + 1) * P], k.ident)
                    last.then_inc(s["turned"], 1)
                if j >= 1:
                    i = j - 1
                    pe.wait_ge(s["copied"], i + 1)
                    if i >= 4:
                        pe.wait_ge(s["added"], i - 3)
                    for c in range(3):
                        last = nc.tensor.matmul(ps[:, 4 + i % 4, 0:D], oT[:, i, c, :], w.o[:, c, :], start=c == 0, stop=c == 2)
                    last.then_inc(s["y"], 1)



def no_load(k, w, sem):
    return 0


SUBLAYERS = [
    (load_L0_attn, stage_L0_attn), (load_gqa, stage_gqa), (load_L0_ffn, stage_L0_ffn),
    (load_L1_attn, stage_L1_attn),
    (lambda k, w, sem: load_latent_cross(k, w, sem, "L1_xattn_"), stage_L1_xattn), (load_L1_ffn, stage_L1_ffn),
    (load_L2_attn, stage_L2_attn), (lambda k, w, sem: load_latent_cross(k, w, sem, "L2_xattn_"), stage_L2_xattn), (load_L2_ffn, stage_L2_ffn),
    (load_L3_attn, stage_L3_attn), (load_gqa, stage_gqa), (load_L3_ffn, stage_L3_ffn),
]


def decoder(nc, dram, out):
    with ExitStack() as ctx:
        k = Kit()
        k.nc, k.dram, k.serial, k.former = nc, dram, 0, []
        total, fixed_cols = 53200, 7808
        arena = ctx.enter_context(nc.sbuf_tensor("fixed", [P, fixed_cols], F32))
        wreg = [ctx.enter_context(nc.sbuf_tensor(f"weights{i}", [P, W_COLS], F32)) for i in range(2)]
        work_cols = total - fixed_cols - 2 * W_COLS
        work = ctx.enter_context(nc.sbuf_tensor("work", [P, work_cols], F32))
        k.ps = ctx.enter_context(nc.psum_tensor("ps", [P, 8, BANK], F32))
        fixed = Region(arena, fixed_cols)
        k.fixed = fixed
        k.work = Region(work, work_cols)
        k.x = fixed.take(NT, D)
        k.h = fixed.take(NT, D)
        k.hT = fixed.take(KC, TOK)
        k.ident = fixed.take(P)
        k.ident16 = fixed.take(P, dt=BF16)
        k.rev = fixed.take(32)
        k.causal = fixed.take(NT * SEQ, dt=BF16)
        stored = nc.alloc_semaphore("stored")
        constants(k)
        loads = {}

        def start_loads(n):
            if n < len(STAGES):
                w = Named()
                w.region = Region(wreg[n % 2], W_COLS)
                w.sem = nc.alloc_semaphore(f"weights_of_{STAGES[n]}")
                w.loaded = SUBLAYERS[STAGES[n]][0](k, w, w.sem)
                loads[n] = w

        start_loads(0)
        for n, layer in enumerate(STAGES):
            start_loads(n + 1)
            layernorm(k)
            SUBLAYERS[layer][1](k, loads[n])
        with nc.Block() as block:
            @block.sync
            def _(sp):
                sp.dma_start(out.rearrange("b t d -> (b t) d").rearrange("(j p) d -> p j d", p=P), k.x).then_inc(stored, 16)
                sp.wait_ge(stored, 16)



def lay_out(inputs):
    import numpy as np
    i = {n: np.asarray(a) for n, a in inputs.items()}
    T = lambda a: np.ascontiguousarray(np.swapaxes(a, -1, -2))
    o = {"x": i["x"], "ctx_512": i["ctx_512"]}
    o["ctxT"] = i["ctx_512"].reshape(TOK, 64).T
    o["const_gmask"] = ((np.arange(P)[:, None] // GQA_D) % GQA_G == np.arange(GQA_G)).astype(np.float32)
    def rope(dim, repeat):
        inv = (1.0 / 10000.0 ** (np.arange(0, dim, 2, dtype=np.float32) / np.float32(dim))).astype(np.float32)
        f = np.arange(SEQ, dtype=np.float32)[:, None] * inv[None, :]
        widen = (lambda a: np.repeat(a, 2, 1)) if repeat else (lambda a: np.concatenate([a, a], 1))
        c, s = widen(np.cos(f)), widen(np.sin(f))
        return c, np.concatenate([-s[:, :dim // 2], s[:, dim // 2:]], 1)

    c, s = rope(64, True)
    o["const_rope64"] = np.tile(np.stack([c, s], 1), (2, 1, 1))
    c, s = rope(64, False)
    o["const_rope64b"] = np.tile(np.stack([c, s], 1), (2, 1, 1))
    o["const_rope64T"] = np.tile(np.stack([c.T, s.T], 1), (2, 1, 1))
    c, s = rope(192, True)
    o["const_rope192"] = np.stack([c.T.reshape(2, 96, SEQ), s.T.reshape(2, 96, SEQ)], 1).transpose(2, 1, 0, 3)
    o["const_causal"] = np.tile(np.where(np.arange(SEQ)[None, :] > np.arange(SEQ)[:, None], -1e30, 0), (2, NT)).astype(np.float32)
    o["const_rev"] = np.tile(np.arange(32, 0, -1, dtype=np.float32), (P, 1))
    p = "L0_ffn_"
    for n in ("gate_w", "fc1_w", "fc2_w", "fc2_b", "alpha"):
        o[p + n] = i[p + n]
    o[p + "fc1_b"] = i[p + "fc1_b"].reshape(8, 2, P).transpose(2, 1, 0)
    p = "L1_ffn_"
    for n in ("Wg", "Wu", "Wd", "Gb", "Ub", "Db", "Wr", "temperature"):
        o[p + n] = i[p + n]
    for n in "GUD":
        o[p + n + "aT"] = T(i[p + n + "a"])
    p = "L2_ffn_"
    o[p + "weightT"], o[p + "masksT"], o[p + "routerT"] = T(i[p + "weight"]), T(i[p + "expert_masks"]), T(i[p + "router_w"])
    o[p + "scale"] = i[p + "scale"]
    p = "L3_ffn_"
    o[p + "AT"] = i[p + "A"].reshape(512, D).T
    o[p + "BT"] = T(i[p + "Bw"]).reshape(512, D)
    o[p + "WgT"] = T(i[p + "Wg"])
    p = "L2_attn_"
    for n in ("Wq", "Wk"):
        o[p + n] = i[p + n].transpose(1, 0, 2).reshape(D, D)
    o[p + "Wv"] = i[p + "Wv"].reshape(8, 2, D, 16).transpose(2, 1, 0, 3).reshape(D, D)
    o[p + "Wo"], o[p + "bo"] = i[p + "Wo"], i[p + "bo"]
    o[p + "bias"] = np.stack([i[p + b].reshape(2, P).T for b in ("bq", "bk", "bv")], 1)
    o["const_pmask"] = ((np.arange(P)[:, None] // 16) % 2 == np.arange(2)).astype(np.float32)
    p = "L0_attn_"
    o[p + "WqkvT"] = np.concatenate([T(i[p + n]) for n in ("Wq", "Wk", "Wv")], 1)
    o[p + "WgT"], o[p + "WoT"] = T(i[p + "Wg"]), T(i[p + "Wo"])
    o[p + "WbaT"] = np.concatenate([T(i[p + "Wb"]), T(i[p + "Wa"])], 1)
    o[p + "conv_qk"] = np.concatenate([i[p + "conv_wq"], i[p + "conv_wk"]]).reshape(4, 96, 4).transpose(1, 0, 2)
    o[p + "conv_v"] = i[p + "conv_wv"].reshape(3, P, 4).transpose(1, 0, 2)
    for n in ("A_log", "dt_bias", "norm_w"):
        o[p + n] = i[p + n]
    a, b = np.arange(P)[:, None], np.arange(P)[None, :]
    same = a // SEQ == b // SEQ
    o["const_tri"] = np.stack([(a > b) & same, (a <= b) & same], 1).astype(np.float32)
    o["const_level"] = np.stack([(a // (2 << l) == b // (2 << l)) & (b // (1 << l) % 2 == 1) & (a // (1 << l) % 2 == 0)
                                 for l in range(LEVELS)], 1).astype(np.float32)
    o["const_head"] = (np.arange(96)[:, None] // DH0 == np.arange(96)[None, :] // DH0).astype(np.float32)
    for L in ("L1_xattn_", "L2_xattn_"):
        o[L + "Wq"] = i[L + "Wq"]
        o[L + "w_kc_kv"] = i[L + "w_kc_kv"]
        o[L + "qrT"] = T(i[L + "W_qr"])
        o[L + "krT"] = T(i[L + "W_kr"])
        o[L + "WoT"] = T(i[L + "Wo"])
    o["L1_xattn_kcqT"] = T(i["L1_xattn_w_kc_q"])
    o["L2_xattn_w_kc_q"] = i["L2_xattn_w_kc_q"]
    p = "L3_attn_"
    wqb = i[p + "Wq_b"].reshape(192, NH, 192)
    wkv = i[p + "Wkv_b"].reshape(64, NH, 256)
    swap = lambda a: np.concatenate([a[..., 32:], a[..., :32]], -1)
    o[p + "Wq_rot"], o[p + "Wq_swap"] = wqb[:, :, 128:], swap(wqb[:, :, 128:])
    o[p + "Wq_nopeT"] = wqb[:, :, :128].transpose(2, 1, 0)
    o[p + "WkT"], o[p + "WvT"] = wkv[:, :, :128].transpose(2, 1, 0), wkv[:, :, 128:].transpose(2, 1, 0)
    o[p + "Wo"] = i[p + "Wo"]
    o[p + "Wall"] = np.concatenate([i[p + "Wq_a"], i[p + "Wkv_a"], i[p + "Wk_rope"], swap(i[p + "Wk_rope"])], 1)
    o[p + "q_norm_w"], o[p + "kv_norm_w"] = i[p + "q_norm_w"].reshape(2, 96).T, i[p + "kv_norm_w"]
    o["L1_attn_WabT"] = np.concatenate([T(i["L1_attn_Wa"]), T(i["L1_attn_Wb"])], 1)
    o["L1_attn_WoutT"] = T(i["L1_attn_Wout"])
    o["L1_attn_bab"] = np.stack([i["L1_attn_ba"], i["L1_attn_bb"]], 1)
    o["L1_attn_bout"] = i["L1_attn_bout"]
    return {n: np.ascontiguousarray(a) for n, a in o.items()}


def kernel(**inputs):
    import concourse.bacc as _bacc
    from concourse.bass_utils import run_bass_kernel_spmd as _run

    arrays = lay_out(inputs)
    nc = _bacc.Bacc("TRN2", target_bir_lowering=False, num_devices=1)
    dram = {n: nc.dram_tensor(f"in_{n}", a.shape, mybir.dt.from_np(a.dtype), kind="ExternalInput").ap()
            for n, a in arrays.items()}
    out = nc.dram_tensor("out_0_dram", (BATCH, SEQ, D), F32, kind="ExternalOutput").ap()
    decoder(nc, dram, out)
    r = _run(nc, [{f"in_{n}": a for n, a in arrays.items()}], core_ids=[0])
    return r.results[0]["out_0_dram"]
```

```python
from contextlib import ExitStack, contextmanager

import concourse.bass as bass
from concourse import mybir

P = 128
BATCH, SEQ, D = 16, 64, 256
TOK = BATCH * SEQ
NT = TOK // P
KC = D // P
BANK = 512
EPS_LN = 1e-5

ALU = mybir.AluOpType
ACT = mybir.ActivationFunctionType
AX = mybir.AxisListType
F32 = mybir.dt.float32
BF16 = mybir.dt.bfloat16
F32R = mybir.dt.float32r
U32 = mybir.dt.uint32

W_COLS = 16384
STAGES = list(range(12))


class Region:

    def __init__(self, tensor, cols):
        self.tensor, self.cols, self.at = tensor, cols, 0

    def take(self, *dims, rows=P, dt=F32):
        n = 1
        for d in dims:
            n *= d
        words = (n + 1) // 2 if dt == BF16 else n
        assert self.at + words <= self.cols, (self.at, words, self.cols)
        ap = self.tensor[0:rows, self.at:self.at + words]
        self.at += words
        if dt not in (F32, F32R):
            ap = ap.bitcast(dt)
        if len(dims) > 1:
            names = "abcde"[:len(dims)]
            ap = ap.rearrange("p (" + " ".join(names) + ") -> p " + " ".join(names),
                              **{c: d for c, d in zip(names[1:], dims[1:])})
        return ap

    def clear(self):
        self.at = 0


class Named:
    pass


class Kit:

    @contextmanager
    def stage(self, *names):
        nc = self.nc
        self.serial += 1
        named = {n: nc.alloc_semaphore(f"{n}_{self.serial}") for n in names}
        if self.former:
            nc.clear_and_free_semaphores(self.former)
        self.former = list(named.values())
        with nc.Block() as block:
            yield block, named



class Chain:

    def __init__(self, eng, sem):
        self.eng, self.sem, self.n = eng, sem, 0

    def step(self, ins):
        self.n += 1
        ins.then_inc(self.sem, 1)
        self.eng.wait_ge(self.sem, self.n)

    def add(self, ins):
        self.n += 1
        ins.then_inc(self.sem, 1)

    def settle(self):
        self.eng.wait_ge(self.sem, self.n)


def bc(ap, dim, n):
    lst = [list(p) for p in ap.ap]
    lst.insert(dim, [0, n])
    return bass.AP(tensor=ap.tensor, offset=ap.offset, ap=lst)



def constants(k):
    nc = k.nc
    causal = k.h.rearrange("p j d -> p (j d)")[:, 0:NT * SEQ]
    with k.stage("zeroed", "ident", "x_in", "causal_in", "halves") as (block, s):
        @block.sync
        def _(sp):
            sp.dma_start(k.x, k.dram["x"].rearrange("b t d -> (b t) d").rearrange("(j p) d -> p j d", p=P)).then_inc(s["x_in"], 16)
            sp.dma_start(causal, k.dram["const_causal"]).then_inc(s["causal_in"], 16)
            sp.dma_start(k.rev, k.dram["const_rev"]).then_inc(s["x_in"], 16)
            sp.wait_ge(s["x_in"], 32)

        @block.vector
        def _(dve):
            dve.wait_ge(s["causal_in"], 16)
            nc.vector.tensor_copy(k.causal, causal).then_inc(s["halves"], 1)
            dve.wait_ge(s["ident"], 1)
            nc.vector.tensor_copy(k.ident16, k.ident).then_inc(s["halves"], 1)

        @block.gpsimd
        def _(pool):
            nc.gpsimd.memset(k.ident, 0.0).then_inc(s["zeroed"], 1)
            pool.wait_ge(s["zeroed"], 1)
            nc.gpsimd.affine_select(out=k.ident, in_=k.ident, compare_op=ALU.not_equal, fill=1.0, base=0,
                                    pattern=[[-1, P]], channel_multiplier=1).then_inc(s["ident"], 1)



def layernorm(k, eps=EPS_LN):
    nc, x, h, hT, ps = k.nc, k.x, k.h, k.hT, k.ps
    stats, mv, std, rstd = k.nstats, k.nmv, k.nstd, k.nrstd
    with k.stage("stats", "aggr", "veps", "std", "rstd", "normed", "turned", "hT") as (block, s):
        @block.vector
        def _(dve):
            for j in range(NT):
                nc.vector.bn_stats(stats[:, j, :], x[:, j, :]).then_inc(s["stats"], 1)
            for j in range(NT):
                dve.wait_ge(s["stats"], j + 1)
                nc.vector.bn_aggr(mv[:, j, :], stats[:, j, :]).then_inc(s["aggr"], 1)
            dve.wait_ge(s["aggr"], NT)
            nc.vector.tensor_scalar(std, mv[:, :, 1], eps, None, ALU.add).then_inc(s["veps"], 1)
            dve.wait_ge(s["std"], 1)
            nc.vector.reciprocal(rstd, std).then_inc(s["rstd"], 1)
            dve.wait_ge(s["rstd"], 1)
            for j in range(NT):
                nc.vector.tensor_scalar(h[:, j, :], x[:, j, :], mv[:, j, 0:1], rstd[:, j:j + 1],
                                        ALU.subtract, ALU.mult).then_inc(s["normed"], 1)

        @block.tensor
        def _(pe):
            for j in range(NT):
                pe.wait_ge(s["normed"], j + 1)
                for c in range(KC):
                    at = (j % 4) * P
                    last = nc.tensor.transpose(ps[:, (j // 4) * KC + c, at:at + P], h[:, j, c * P:(c + 1) * P], k.ident)
                last.then_inc(s["turned"], 1)

        @block.scalar
        def _(act):
            act.wait_ge(s["veps"], 1)
            nc.scalar.activation(std, std, ACT.Sqrt).then_inc(s["std"], 1)
            for half in range(2):
                act.wait_ge(s["turned"], 4 * half + 4)
                for c in range(KC):
                    nc.scalar.copy(hT[:, c, half * BANK:(half + 1) * BANK], ps[:, half * KC + c, :]).then_inc(s["hT"], 1)



NORM_SEMS = ("n_stats", "n_aggr", "n_veps", "n_std", "n_rstd", "n_normed", "n_turned", "n_hT")


def norm_front(k, s, dve, i):
    nc = k.nc
    for j in (2 * i, 2 * i + 1):
        nc.vector.bn_stats(k.nstats[:, j, :], k.x[:, j, :]).then_inc(s["n_stats"], 1)
    for j in (2 * i, 2 * i + 1):
        dve.wait_ge(s["n_stats"], j + 1)
        nc.vector.bn_aggr(k.nmv[:, j, :], k.nstats[:, j, :]).then_inc(s["n_aggr"], 1)
    dve.wait_ge(s["n_aggr"], 2 * i + 2)
    nc.vector.tensor_scalar(k.nstd[:, 2 * i:2 * i + 2], k.nmv[:, 2 * i:2 * i + 2, 1], EPS_LN, None, ALU.add).then_inc(s["n_veps"], 1)


def norm_back(k, s, dve, i):
    nc = k.nc
    dve.wait_ge(s["n_std"], i + 1)
    nc.vector.reciprocal(k.nrstd[:, 2 * i:2 * i + 2], k.nstd[:, 2 * i:2 * i + 2]).then_inc(s["n_rstd"], 1)
    dve.wait_ge(s["n_rstd"], i + 1)
    for j in (2 * i, 2 * i + 1):
        nc.vector.tensor_scalar(k.h[:, j, :], k.x[:, j, :], k.nmv[:, j, 0:1], k.nrstd[:, j:j + 1],
                                ALU.subtract, ALU.mult).then_inc(s["n_normed"], 1)


def norm_root(k, s, act, i):
    nc = k.nc
    act.wait_ge(s["n_veps"], i + 1)
    nc.scalar.activation(k.nstd[:, 2 * i:2 * i + 2], k.nstd[:, 2 * i:2 * i + 2], ACT.Sqrt).then_inc(s["n_std"], 1)


def norm_turn(k, s, pe, i, banks):
    nc = k.nc
    if i >= 2:
        pe.wait_ge(s["n_hT"], i - 1)
    for jj in range(2):
        pe.wait_ge(s["n_normed"], 2 * i + jj + 1)
        for c in range(KC):
            last = nc.tensor.transpose(k.ps[:, banks[i % 2], (2 * c + jj) * P:(2 * c + jj + 1) * P],
                                       k.h[:, 2 * i + jj, c * P:(c + 1) * P], k.ident)
    last.then_inc(s["n_turned"], 1)


def norm_copy(k, s, act, i, banks):
    nc = k.nc
    act.wait_ge(s["n_turned"], i + 1)
    nc.scalar.copy(k.hT[:, :, 2 * i * P:(2 * i + 2) * P],
                   k.ps[:, banks[i % 2], :].rearrange("p (c t) -> p c t", c=KC)).then_inc(s["n_hT"], 1)


def norm_scalar_part(k, s, act, banks):
    for i in range(NT // 2):
        norm_root(k, s, act, i)
        if i:
            norm_copy(k, s, act, i - 1, banks)
    norm_copy(k, s, act, NT // 2 - 1, banks)



def load_L1_attn(k, w, sem):
    d, eng = k.dram, k.nc.sync
    w.wab = w.region.take(KC, P)
    w.wout = w.region.take(D, rows=64)
    w.bias = w.region.take(2, rows=64)
    w.bout = w.region.take(D)
    eng.dma_start(w.wab, d["L1_attn_WabT"].rearrange("(c p) s -> p c s", p=P)).then_inc(sem, 16)
    eng.dma_start(w.wout, d["L1_attn_WoutT"]).then_inc(sem, 16)
    eng.dma_start(w.bias, d["L1_attn_bab"]).then_inc(sem, 16)
    eng.dma_start(w.bout, row_on_all(d["L1_attn_bout"])).then_inc(sem, 16)
    return 64


def row_on_all(ap, n=P):
    return bass.AP(tensor=ap.tensor, offset=ap.offset, ap=[[0, n]] + [list(p) for p in ap.ap])


def stage_L1_attn(k, w):
    nc, ps = k.nc, k.ps
    k.work.clear()
    a = k.work.take(TOK, rows=64)
    b = k.work.take(TOK, rows=64)
    hs = k.work.take(TOK, rows=64)
    S = 64
    with k.stage("proj", "tanh", "cut", "scan", "out", "hb", "xh", "xs", *NORM_SEMS) as (block, s):
        @block.tensor
        def _(pe):
            pe.wait_ge(w.sem, w.loaded)
            for g in range(2):
                for half in range(2):
                    for c in range(KC):
                        last = nc.tensor.matmul(ps[0:S, 2 * g + half, :], w.wab[:, c, g * S:(g + 1) * S],
                                                k.hT[:, c, half * BANK:(half + 1) * BANK], start=c == 0, stop=c == KC - 1)
                last.then_inc(s["proj"], 1)
            pe.wait_ge(s["scan"], 1)
            for j in range(NT):
                last = nc.tensor.matmul(ps[:, 4 + j // 2, (j % 2) * D:(j % 2 + 1) * D], hs[:, j * P:(j + 1) * P],
                                        w.wout, start=True, stop=True)
                if j % 2:
                    last.then_inc(s["out"], 1)
            for i in range(NT // 2):
                norm_turn(k, s, pe, i, (0, 1))

        @block.scalar
        def _(act):
            act.wait_ge(w.sem, w.loaded)
            for g, dst in enumerate((a, b)):
                act.wait_ge(s["proj"], g + 1)
                nc.scalar.activation(dst, ps[0:S, 2 * g:2 * g + 2, :].rearrange("p a b -> p (a b)"), ACT.Tanh,
                                     bias=w.bias[:, g:g + 1]).then_inc(s["tanh"], 1)
            norm_scalar_part(k, s, act, (0, 1))

        @block.gpsimd
        def _(pool):
            pool.wait_ge(w.sem, w.loaded)
            nc.gpsimd.tensor_tensor(k.h, k.h, bc(w.bout, 1, NT), ALU.add).then_inc(s["hb"], 1)
            pool.wait_ge(s["hb"], 1)
            nc.gpsimd.tensor_tensor(k.x, k.x, k.h, ALU.add).then_inc(s["xh"], 1)

        @block.vector
        def _(dve):
            dve.wait_ge(s["tanh"], 1)
            nc.vector.memset(a.rearrange("p (b t) -> p b t", t=SEQ)[:, :, 0:1], 0.0).then_inc(s["cut"], 1)
            dve.wait_ge(s["cut"], 1)
            dve.wait_ge(s["tanh"], 2)
            nc.vector.tensor_tensor_scan(hs, a, b, 0.0, ALU.mult, ALU.add).then_inc(s["scan"], 1)
            dve.wait_ge(s["xh"], 1)
            for i in range(NT // 2):
                dve.wait_ge(s["out"], i + 1)
                nc.vector.tensor_tensor(k.x[:, 2 * i:2 * i + 2, :].rearrange("p a b -> p (a b)"),
                                        k.x[:, 2 * i:2 * i + 2, :].rearrange("p a b -> p (a b)"), ps[:, 4 + i, :],
                                        ALU.add).then_inc(s["xs"], 1)
                dve.wait_ge(s["xs"], i + 1)
                norm_front(k, s, dve, i)
                if i:
                    norm_back(k, s, dve, i - 1)
            norm_back(k, s, dve, NT // 2 - 1)



GQA_KV, GQA_G, GQA_D = 8, 4, 8


def load_gqa(k, w, sem):
    d, eng = k.dram, k.nc.sync
    w.krep = w.region.take(2, 2, NT, SEQ)
    w.vt = w.region.take(BATCH, GQA_KV * GQA_D)
    w.gmask = w.region.take(2 * GQA_G)
    n, cols = 4, NT * SEQ
    for row in range(4):
        src = d["ctxK"][row]
        eng.dma_start(w.krep[32 * row:32 * row + 32, :, :, :, :].rearrange("p c i j t -> p (c i) (j t)"),
                      bass.AP(tensor=src.tensor, offset=src.offset, ap=[[0, GQA_G], [n * cols, GQA_D], [cols, n], [1, cols]])).then_inc(sem, 16)
    for half in range(2):
        eng.dma_start(w.vt[64 * half:64 * half + 64, :, :], d["ctx_512"].rearrange("b t d -> t b d")).then_inc(sem, 16)
    eng.dma_start(w.gmask, d["const_gmask"]).then_inc(sem, 16)
    return 16 * (4 + 3)


def stage_gqa(k, w):
    nc, ps, x = k.nc, k.ps, k.x
    k.work.clear()
    hd = w.region.take(3, 2, P)
    kd = w.region.take(3, 2, 2 * GQA_G, SEQ)
    vblk = w.region.take(BATCH, GQA_KV, 2, 9)
    pr = k.work.take(2, 16, SEQ)
    pT = k.work.take(2, 8, P)
    mx = k.work.take(2, 16)
    rs = k.work.take(2, 16)
    o = k.work.take(2, P)
    U = 2 * NT
    scale = float(GQA_D) ** -0.5
    ROOTS_AFTER = {U - 3: (0, 1), U - 1: (2, 3)}

    def pv_bank(u):
        return ps[:, 6 + u % 2, 0:288].rearrange("p (n b g d) -> p n b g d", b=2, g=2, d=9)

    with k.stage("hzero", "hd", "spread", "vzero", "vones", "vals", "scored", "maxed", "centred", "expd", "turned", "copied",
                 "pv", "rsum", "normed", "added", *NORM_SEMS) as (block, s):
        @block.tensor
        def _(pe):
            def scores(u):
                j, ip = divmod(u, 2)
                if u >= 2:
                    pe.wait_ge(s["centred"], u - 1)
                pe.wait_ge(s["hd"], u + 1)
                pe.wait_ge(s["spread"], u + 1)
                for c in range(2):
                    last = nc.tensor.matmul(ps[:, 2 * ip + c, :], hd[:, u % 3, c, :],
                                            kd[:, u % 3, c, :, :].rearrange("p g t -> p (g t)"), start=True, stop=True)
                last.then_inc(s["scored"], 1)

            def turn(u):
                pe.wait_ge(s["expd"], u + 1)
                if u >= 1:
                    pe.wait_ge(s["copied"], 2 * u)
                for n in range(8):
                    last = nc.tensor.transpose(ps[:, 4 + n // 4, (n % 4) * P:(n % 4 + 1) * P],
                                               pr[:, u % 2, 2 * n:2 * n + 2, :].rearrange("p a t -> p (a t)"), k.ident)
                last.then_inc(s["turned"], 1)

            def weigh(u):
                j, ip = divmod(u, 2)
                pe.wait_ge(s["copied"], 2 * u + 2)
                if u >= 2:
                    pe.wait_ge(s["normed"], 2 * u - 2)
                for n in range(8):
                    c, ii = n // 4, (n // 2) % 2
                    last = nc.tensor.matmul(pv_bank(u)[:, n].rearrange("p b g d -> p (b g d)"), pT[:, u % 2, n, :],
                                            vblk[:, 2 * j:2 * j + 2, 4 * c + 2 * ip + ii, :, :].rearrange("p b g d -> p b (g d)"),
                                            start=True, stop=True)
                last.then_inc(s["pv"], 1)

            for u in range(U + 2):
                if u < U:
                    scores(u)
                if u == 2:
                    pe.wait_ge(s["vals"], 2)
                    pe.wait_ge(s["vones"], 2)
                if 1 <= u <= U:
                    turn(u - 1)
                if u >= 2:
                    weigh(u - 2)
            for i in range(NT // 2):
                norm_turn(k, s, pe, i, (0, 1))

        @block.gpsimd
        def _(pool):
            def spread(u):
                j, ip = divmod(u, 2)
                if u >= 3:
                    pool.wait_ge(s["scored"], u - 2)
                nc.gpsimd.tensor_tensor(kd[:, u % 3, :, :, :], bc(w.krep[:, :, ip, j, :], 2, 2 * GQA_G),
                                        bc(bc(w.gmask, 1, 2), 3, SEQ), ALU.mult).then_inc(s["spread"], 1)

            nc.gpsimd.memset(hd, 0.0).then_inc(s["hzero"], 1)
            pool.wait_ge(w.sem, w.loaded)
            spread(0)
            nc.gpsimd.memset(vblk, 0.0).then_inc(s["vzero"], 1)
            spread(1)
            pool.wait_ge(s["vzero"], 1)
            pool.wait_ge(s["spread"], 2)
            for g in range(2):
                nc.gpsimd.memset(vblk[64 * g:64 * g + 64, :, :, g, 8:9], 1.0).then_inc(s["vones"], 1)
            pool.wait_ge(s["vones"], 2)
            for u in range(2, U):
                spread(u)

        @block.scalar
        def _(act):
            def queries(u):
                j, ip = divmod(u, 2)
                if u >= 3:
                    act.wait_ge(s["scored"], u - 2)
                for b in range(2):
                    ins = nc.scalar.copy(hd[64 * b:64 * b + 64, u % 3, :, b * SEQ:(b + 1) * SEQ],
                                         k.hT[64 * ip:64 * ip + 64, :, j * P + b * SEQ:j * P + (b + 1) * SEQ])
                ins.then_inc(s["hd"], 1)

            act.wait_ge(s["hzero"], 1)
            queries(0)
            queries(1)
            for u in range(U):
                if u + 2 < U:
                    queries(u + 2)
                act.wait_ge(s["centred"], u + 1)
                nc.scalar.activation(pr[:, u % 2, :, :], pr[:, u % 2, :, :], ACT.Exp, scale=scale).then_inc(s["expd"], 1)
                if u == 0:
                    act.wait_ge(w.sem, w.loaded)
                    act.wait_ge(s["vzero"], 1)
                    for g in range(2):
                        r = slice(64 * g, 64 * g + 64)
                        nc.scalar.copy(vblk[r, :, :, g, 0:8], w.vt[r, :, :].rearrange("p b (h d) -> p b h d", d=8)).then_inc(s["vals"], 1)
                act.wait_ge(s["turned"], u + 1)
                if u >= 2:
                    act.wait_ge(s["pv"], u - 1)
                for h in range(2):
                    nc.scalar.copy(pT[:, u % 2, 4 * h:4 * h + 4, :].rearrange("p a b -> p (a b)"), ps[:, 4 + h, :]).then_inc(s["copied"], 1)
                if u in ROOTS_AFTER:
                    for i in ROOTS_AFTER[u]:
                        norm_root(k, s, act, i)
            for i in range(NT // 2):
                norm_copy(k, s, act, i, (0, 1))

        @block.vector
        def _(dve):
            def centre(u):
                ip = u % 2
                sc = ps[:, 2 * ip:2 * ip + 2, :].rearrange("p a (h t) -> p (a h) t", t=SEQ)
                dve.wait_ge(s["scored"], u + 1)
                nc.vector.tensor_reduce(mx[:, u % 2, :], sc, AX.X, ALU.max).then_inc(s["maxed"], 1)
                dve.wait_ge(s["maxed"], u + 1)
                if u >= 2:
                    dve.wait_ge(s["turned"], u - 1)
                nc.vector.tensor_tensor(pr[:, u % 2, :, :], sc, bc(mx[:, u % 2, :], 2, SEQ), ALU.subtract).then_inc(s["centred"], 1)

            def finish(u):
                j, ip = divmod(u, 2)
                dve.wait_ge(s["pv"], u + 1)
                ob = o[:, u % 2, :]
                halves = [(slice(64 * b, 64 * b + 64), pv_bank(u)[64 * b:64 * b + 64, :, b]) for b in range(2)]
                for rows, pv in halves:
                    nc.vector.reciprocal(rs[rows, u % 2, :].rearrange("p (n g) -> p n g", g=2), pv[:, :, :, 8]).then_inc(s["rsum"], 1)
                for b, (rows, pv) in enumerate(halves):
                    dve.wait_ge(s["rsum"], 2 * u + b + 1)
                    nc.vector.tensor_tensor(ob[rows, :].rearrange("p (n g d) -> p n g d", g=2, d=8), pv[:, :, :, 0:8],
                                            bc(rs[rows, u % 2, :].rearrange("p (n g) -> p n g", g=2), 3, 8), ALU.mult).then_inc(s["normed"], 1)
                dve.wait_ge(s["normed"], 2 * u + 2)
                xv = x[:, j, :].rearrange("p (c f) -> p c f", c=2)[:, :, 64 * ip:64 * ip + 64]
                nc.vector.tensor_tensor(xv, xv, ob.rearrange("p (c f) -> p c f", c=2), ALU.add).then_inc(s["added"], 1)

            def front(i):
                dve.wait_ge(s["added"], 4 * i + 4)
                norm_front(k, s, dve, i)

            for u in range(U + 1):
                if u < U:
                    centre(u)
                if u >= 2:
                    finish(u - 2)
                    if (u - 2) % 4 == 3:
                        front((u - 2) // 4)
                if u == U - 1:
                    norm_back(k, s, dve, 0)
                    norm_back(k, s, dve, 1)
            finish(U - 1)
            front(NT // 2 - 1)
            norm_back(k, s, dve, NT // 2 - 2)
            norm_back(k, s, dve, NT // 2 - 1)



NH, DH = 16, 64


class Latent:

    def __init__(self, room, more, kk, kvt, pm, turned_room):
        self.kk = kk
        self.kvt = kvt
        self.pm = pm
        self.ctxT = room.take(NH // 2, TOK)
        self.pT = turned_room.take(2, 2, 4, P)
        room = more
        self.pr = room.take(3, NT, SEQ)
        self.mx = room.take(2, NT)
        self.sm = room.take(2, NT)
        self.rs = room.take(2, NT)


CORE_SEMS = ("narrowed", "q_proj", "q_ready", "scored", "maxed", "centred", "expd", "summed", "recip", "probs", "turned",
             "copied", "pv", "ctx", "out", "added", *NORM_SEMS)


def attend(k, block, s, t, key_rows, q_of, q_hooks, scale, causal=None, turn_banks=(2, 3)):
    nc, ps, x = k.nc, k.ps, k.x

    @block.tensor
    def _(pe):
        def scores(h):
            hh = h % 2
            if h >= 2:
                pe.wait_ge(s["centred"], h - 1)
            pe.wait_ge(s["q_ready"], q_hooks["ready"](h))
            if causal is not None:
                nc.tensor.matmul(ps[:, 4 + hh, :], k.ident16, causal, start=True, stop=False, skip_group_check=True)
            r0, r1 = key_rows(h)
            for b in range(BATCH):
                tok, at = b * SEQ, (b // 2) * SEQ
                last = nc.tensor.matmul(ps[64 * (b % 2):64 * (b % 2) + 64, 4 + hh, at:at + SEQ],
                                        q_of(h)[:, tok:tok + SEQ], t.kk[r0:r1, tok:tok + SEQ],
                                        start=causal is None, stop=True, skip_group_check=causal is not None,
                                        tile_position=(r0, 64 * (b % 2)))
            last.then_inc(s["scored"], 1)

        def turn(h):
            pe.wait_ge(s["probs"], h + 1)
            gap = 1 if turn_banks[0] == turn_banks[1] else 2
            if h >= gap:
                pe.wait_ge(s["copied"], h + 1 - gap)
            for jp in range(4):
                last = nc.tensor.transpose(ps[:, turn_banks[h % 2], jp * P:(jp + 1) * P],
                                           t.pr[:, h % 3, 2 * jp:2 * jp + 2, :].rearrange("p a t -> p (a t)"), k.ident)
            last.then_inc(s["turned"], 1)

        def weigh(u):
            pe.wait_ge(s["copied"], 2 * u + 2)
            if u:
                pe.wait_ge(s["ctx"], 4 * u)
            for n in range(8):
                jp, b = divmod(n, 2)
                last = nc.tensor.matmul(ps[:, 6 + jp // 2, (n % 4) * P:(n % 4 + 1) * P],
                                        t.kvt[:, n, :, :].rearrange("p a d -> p (a d)"),
                                        t.pT[:, u % 2, :, jp, b * SEQ:(b + 1) * SEQ], start=True, stop=True)
            last.then_inc(s["pv"], 1)

        for h in range(NH + 5):
            if h < NH:
                q_hooks["pe"](pe, h)
            if h == NH:
                q_hooks.get("pe_last", none)(pe)
            if 2 <= h < NH + 2:
                scores(h - 2)
            if h < NH:
                q_hooks.get("pe_b", none)(pe, h)
            if 4 <= h < NH + 4:
                turn(h - 4)
            if h >= 6 and h % 2 == 0:
                weigh((h - 6) // 2)
        pe.wait_ge(s["ctx"], 2 * NH)
        pe.wait_ge(s["centred"], NH)
        for j in range(NT):
            for u in range(NH // 2):
                last = nc.tensor.matmul(ps[:, (0, 1, 4, 5)[j // 2], (j % 2) * D:(j % 2 + 1) * D],
                                        t.ctxT[:, u, j * P:(j + 1) * P], t.pm[:, u, :],
                                        start=u == 0, stop=u == NH // 2 - 1)
            if j % 2:
                last.then_inc(s["out"], 1)
                if j > 1:
                    norm_turn(k, s, pe, j // 2 - 1, (6, 7))
        norm_turn(k, s, pe, NT // 2 - 1, (6, 7))

    @block.scalar
    def _(act):
        def copy_context(u, hh):
            act.wait_ge(s["pv"], u + 1)
            for jj in range(2):
                dst = t.ctxT[64 * hh:64 * hh + 64, u, :].rearrange("p (a j b q) -> p a j b q", j=2, b=2, q=SEQ)[:, :, jj]
                src = ps[64 * jj:64 * jj + 64, 6:8, :].rearrange("p c (a b e q) -> p (c a) b e q", a=2, b=2, e=2)[:, :, :, hh]
                nc.scalar.copy(dst, src).then_inc(s["ctx"], 1)

        for h in range(NH + 7):
            if h >= 7:
                copy_context((h - 7) // 2, (h - 7) % 2)
            if h < NH:
                q_hooks["act"](act, h)
                q_hooks.get("act_b", none)(act, h)
            if h == NH:
                q_hooks.get("act_last", none)(act)
            if 4 <= h < NH + 4:
                g = h - 4
                act.wait_ge(s["turned"], g + 1)
                if g >= 4:
                    act.wait_ge(s["pv"], g // 2 - 1)
                nc.scalar.copy(t.pT[:, (g // 2) % 2, g % 2, :, :].rearrange("p a b -> p (a b)"), ps[:, turn_banks[g % 2], :]).then_inc(s["copied"], 1)
            if 2 <= h < NH + 2:
                g = h - 2
                act.wait_ge(s["centred"], g + 1)
                nc.scalar.activation(t.pr[:, g % 3, :, :], t.pr[:, g % 3, :, :], ACT.Exp, scale=scale).then_inc(s["expd"], 1)
        norm_scalar_part(k, s, act, (6, 7))

    @block.vector
    def _(dve):
        def normalise(dve, g):
            pr = t.pr[:, g % 3, :, :]
            sm, rs = t.sm[:, g % 2, :], t.rs[:, g % 2, :]
            dve.wait_ge(s["expd"], g + 1)
            nc.vector.tensor_reduce(sm, pr, AX.X, ALU.add).then_inc(s["summed"], 1)
            dve.wait_ge(s["summed"], g + 1)
            nc.vector.reciprocal(rs, sm).then_inc(s["recip"], 1)
            dve.wait_ge(s["recip"], g + 1)
            nc.vector.tensor_tensor(pr, pr, bc(rs, 2, SEQ), ALU.mult).then_inc(s["probs"], 1)

        for h in range(NH + 2):
            if h < NH:
                q_hooks.get("dve", none)(dve, h)
            if h < 2:
                q_hooks.get("dve_b", none)(dve, h)
                continue
            g = h - 2
            sc = ps[:, 4 + g % 2, :].rearrange("p (j t) -> p j t", t=SEQ)
            pr = t.pr[:, g % 3, :, :]
            mx, sm, rs = t.mx[:, g % 2, :], t.sm[:, g % 2, :], t.rs[:, g % 2, :]
            dve.wait_ge(s["scored"], g + 1)
            nc.vector.tensor_reduce(mx, sc, AX.X, ALU.max).then_inc(s["maxed"], 1)
            dve.wait_ge(s["maxed"], g + 1)
            if g >= 3:
                dve.wait_ge(s["turned"], g - 2)
            nc.vector.tensor_tensor(pr, sc, bc(mx, 2, SEQ), ALU.subtract).then_inc(s["centred"], 1)
            if h < NH:
                q_hooks.get("dve_b", none)(dve, h)
            if g >= 1:
                normalise(dve, g - 1)
        normalise(dve, NH - 1)
        for i in range(NT // 2):
            dve.wait_ge(s["out"], i + 1)
            xv = x[:, 2 * i:2 * i + 2, :].rearrange("p a b -> p (a b)")
            nc.vector.tensor_tensor(xv, xv, ps[:, (0, 1, 4, 5)[i], :], ALU.add).then_inc(s["added"], 1)
            dve.wait_ge(s["added"], i + 1)
            norm_front(k, s, dve, i)
            norm_back(k, s, dve, i)


def load_latent_cross(k, w, sem, L):
    d, eng = k.dram, k.nc.sync
    r = w.region
    w.table = r.take(2, 2, SEQ, rows=96)
    w.wq = r.take(NH, D)
    w.qr = r.take(NH // 2, 192)
    w.kr = r.take(NH // 2, DH)
    w.kckv = r.take(NH, DH)
    w.wo = r.take(NH, D)
    w.raw = r.take(8, DH)
    w.rope = r.take(2, DH)
    eng.dma_start(w.wq, d[L + "Wq"].rearrange("(h p) d -> p h d", p=P)).then_inc(sem, 16)
    n = 16
    if L == "L1_xattn_":
        w.kcqT = r.take(NH, 2, P, rows=96)
        eng.dma_start(w.kcqT, d[L + "kcqT"].rearrange("h (a q) p -> q h a p", a=2)).then_inc(sem, 16)
    else:
        w.kcq = r.take(NH, 192)
        eng.dma_start(w.table, d["const_rope192"]).then_inc(sem, 16)
        n = 32
        eng.dma_start(w.kcq, d[L + "w_kc_q"].rearrange("h p q -> p h q")).then_inc(sem, 16)
    for hh in range(2):
        rows = slice(64 * hh, 64 * hh + 64)
        eng.dma_start(w.qr[rows, :, :], d[L + "qrT"].rearrange("(a e) r q -> e r a q", e=2)[hh]).then_inc(sem, 16)
        eng.dma_start(w.kr[rows, :, :], d[L + "krT"].rearrange("(a e) r q -> e r a q", e=2)[hh]).then_inc(sem, 16)
        for jp in range(4):
            b0 = 4 * jp + 2 * hh
            eng.dma_start(w.raw[rows, 2 * jp:2 * jp + 2, :], d["ctx_512"][b0:b0 + 2].rearrange("b t d -> t b d")).then_inc(sem, 16)
    eng.dma_start(w.kckv, d[L + "w_kc_kv"].rearrange("h p q -> p h q")).then_inc(sem, 16)
    eng.dma_start(w.wo, d[L + "WoT"].rearrange("(h p) d -> p h d", p=P)).then_inc(sem, 16)
    eng.dma_start(w.rope, d["const_rope64"]).then_inc(sem, 16)
    return 16 * (1 + 12 + 3) + n


def fold_cross(k, w, t, c1, nf, qf):
    nc, ps = k.nc, k.ps
    spare = Region(k.h.rearrange("p j d -> p (j d)"), NT * D)
    kvd = spare.take(8, 2, DH)
    tmp = spare.take(8, DH)
    c2 = spare.take(4, DH)
    with k.stage("vzero", "vals", "c1", "c1s", "c2", "c2s", "nf", "nfs", "pm", "pms", "qf", "qfs", "rope", "dup", "kkT", "kks") as (block, s):
        @block.tensor
        def _(pe):
            pe.wait_ge(w.sem, w.loaded)
            def first_products(g):
                if g >= 2:
                    pe.wait_ge(s["c1s"], g - 1)
                for a in range(2):
                    for i in range(4):
                        h = 4 * g + i
                        r = slice(64 * (h % 2), 64 * (h % 2) + 64)
                        last = nc.tensor.matmul(ps[0:96, 5 * (g % 2) + h % 2, (2 * a + i // 2) * DH:(2 * a + i // 2 + 1) * DH],
                                                w.qr[r, h // 2, a * 96:(a + 1) * 96], w.kr[r, h // 2, :],
                                                start=True, stop=True, tile_position=(64 * (h % 2), 0))
                last.then_inc(s["c1"], 1)

            def output_products(g):
                if g:
                    pe.wait_ge(s["pms"], g)
                for i in range(4):
                    h = 4 * g + i
                    last = nc.tensor.matmul(ps[64 * (h % 2):64 * (h % 2) + 64, 2, (i // 2) * D:(i // 2 + 1) * D],
                                            w.kckv[:, h, :], w.wo[:, h, :], start=True, stop=True,
                                            tile_position=(0, 64 * (h % 2)))
                last.then_inc(s["pm"], 1)

            first_products(0)
            output_products(0)
            for g in range(4):
                if nf is not None:
                    if g < 3:
                        first_products(g + 1)
                    pe.wait_ge(s["c1s"], g + 1)
                    if g:
                        pe.wait_ge(s["c2s"], g)
                    for i in range(4):
                        for a in range(2):
                            last = nc.tensor.matmul(ps[:, 3, i * DH:(i + 1) * DH], w.kcqT[:, 4 * g + i, a, :],
                                                    c1[:, a, 4 * g + i, :], start=a == 0, stop=a == 1)
                    last.then_inc(s["c2"], 1)
                    if g < 3:
                        output_products(g + 1)
                    pe.wait_ge(s["c2s"], g + 1)
                    if g:
                        pe.wait_ge(s["nfs"], g)
                    for i in range(4):
                        for c in range(KC):
                            last = nc.tensor.matmul(ps[:, 4, (c * 4 + i) * DH:(c * 4 + i + 1) * DH],
                                                    w.wq[:, 4 * g + i, c * P:(c + 1) * P], c2[:, i, :], start=True, stop=True)
                    last.then_inc(s["nf"], 1)
                else:
                    for i in range(4):
                        h = 4 * g + i
                        if h >= 2:
                            pe.wait_ge(s["qfs"], h - 1)
                        for c in range(KC):
                            last = nc.tensor.matmul(ps[:, 3 + h % 2, c * 192:(c + 1) * 192],
                                                    w.wq[:, h, c * P:(c + 1) * P], w.kcq[:, h, :], start=True, stop=True)
                        last.then_inc(s["qf"], 1)
                    if g < 3:
                        first_products(g + 1)
                        output_products(g + 1)
            pe.wait_ge(s["c1s"], 4)
            pe.wait_ge(s["dup"], 1)
            for n in range(8):
                last = nc.tensor.transpose(ps[:, 6 + n // 4, (n % 4) * P:(n % 4 + 1) * P],
                                           kvd[:, n, :, :].rearrange("p a d -> p (a d)"), k.ident)
            last.then_inc(s["kkT"], 1)

        @block.gpsimd
        def _(pool):
            nc.gpsimd.memset(t.kvt, 0.0).then_inc(s["vzero"], 1)

        def copy_folded(act, g):
            act.wait_ge(s["nf"], g + 1)
            nc.scalar.copy(nf[:, :, 4 * g:4 * g + 4, :].rearrange("p c h d -> p c (h d)"),
                           ps[:, 4, :].rearrange("p (c f) -> p c f", c=2)).then_inc(s["nfs"], 1)

        @block.scalar
        def _(act):
            for g in range(4):
                act.wait_ge(s["c1"], g + 1)
                cv = c1[:, :, 4 * g:4 * g + 4, :].rearrange("p a (i e) d -> p e a i d", e=2)
                for e in range(2):
                    ins = nc.scalar.copy(cv[:, e], ps[0:96, 5 * (g % 2) + e, 0:256].rearrange("p (a i d) -> p a i d", a=2, i=2))
                ins.then_inc(s["c1s"], 1)
                act.wait_ge(s["pm"], g + 1)
                nc.scalar.copy(t.pm[:, 2 * g:2 * g + 2, :].rearrange("p a d -> p (a d)"), ps[:, 2, :]).then_inc(s["pms"], 1)
                if nf is not None and g:
                    copy_folded(act, g - 1)
            if nf is not None:
                copy_folded(act, 3)

        @block.vector
        def _(dve):
            dve.wait_ge(w.sem, w.loaded)
            cos, sin = bc(w.rope[:, 0, :], 1, 8), w.rope[:, 1, :]
            for e in range(2):
                o, i = slice(32 * e, 32 * e + 32), slice(32 - 32 * e, 64 - 32 * e)
                nc.vector.tensor_tensor(tmp[:, :, o], w.raw[:, :, i], bc(sin[:, o], 1, 8), ALU.mult).then_inc(s["rope"], 1)
            dve.wait_ge(s["rope"], 2)
            nc.vector.tensor_tensor(w.raw, w.raw, cos, ALU.mult).then_inc(s["rope"], 1)
            dve.wait_ge(s["rope"], 3)
            nc.vector.tensor_tensor(w.raw, w.raw, tmp, ALU.add).then_inc(s["rope"], 1)
            dve.wait_ge(s["rope"], 4)
            nc.vector.tensor_copy(kvd, bc(w.raw, 2, 2)).then_inc(s["dup"], 1)
            dve.wait_ge(s["vzero"], 1)
            for jj in range(2):
                rows = slice(64 * jj, 64 * jj + 64)
                nc.vector.tensor_copy(t.kvt[rows, :, jj, :], w.raw[rows, :, :]).then_inc(s["vals"], 1)
            if nf is not None:
                for g in range(4):
                    dve.wait_ge(s["c2"], g + 1)
                    if g:
                        dve.wait_ge(s["nf"], g)
                    nc.vector.tensor_copy(c2, ps[:, 3, 0:256].rearrange("p (i d) -> p i d", d=DH)).then_inc(s["c2s"], 1)
            else:
                for h in range(NH):
                    dve.wait_ge(s["qf"], h + 1)
                    nc.vector.tensor_copy(qf[:, :, h, :], ps[:, 3 + h % 2, 0:384].rearrange("p (c q) -> p c q", c=2)).then_inc(s["qfs"], 1)
            dve.wait_ge(s["kkT"], 1)
            kkv = t.kk.rearrange("p (a j b t) -> p a b j t", a=4, j=2, b=2)
            for jp in range(4):
                at = (jp % 2) * 256
                nc.vector.tensor_copy(kkv[:, jp], ps[:, 6 + jp // 2, at:at + 256].rearrange("p (b j t) -> p b j t", b=2, j=2)).then_inc(s["kks"], 1)


def stage_L1_xattn(k, w):
    nc, ps = k.nc, k.ps
    k.work.clear()
    nf = k.work.take(KC, NH, DH)
    pm = k.work.take(NH // 2, D)
    kk = k.work.take(TOK)
    kvt = k.work.take(8, 2, DH)
    mark = k.work.at
    c1 = k.work.take(2, NH, DH, rows=96)

    f = Named()
    f.pm, f.kk, f.kvt = pm, kk, kvt
    fold_cross(k, w, f, c1, nf, None)
    k.work.at = mark
    w.region.clear()
    t = Latent(w.region, w.region, kk, kvt, pm, w.region)
    qb = w.region.take(2, TOK)
    with k.stage(*CORE_SEMS) as (block, s):
        def pe_q(pe, h):
            u, half = divmod(h, 2)
            if u >= 1:
                pe.wait_ge(s["q_ready"], 2 * u - 1 + half)
            for c in range(KC):
                last = nc.tensor.matmul(ps[:, half, :], nf[:, c, 2 * u:2 * u + 2, :].rearrange("p h d -> p (h d)"),
                                        k.hT[:, c, half * BANK:(half + 1) * BANK], start=c == 0, stop=c == KC - 1)
            last.then_inc(s["q_proj"], 1)

        def act_q(act, h):
            u, half = divmod(h, 2)
            act.wait_ge(s["q_proj"], h + 1)
            if u >= 2:
                act.wait_ge(s["scored"], 2 * u - 2)
            nc.scalar.copy(qb[:, u % 2, half * BANK:(half + 1) * BANK], ps[:, half, :]).then_inc(s["q_ready"], 1)

        attend(k, block, s, t, lambda h: (64 * (h % 2), 64 * (h % 2) + 64),
               lambda h: qb[64 * (h % 2):64 * (h % 2) + 64, (h // 2) % 2, :],
               {"pe": pe_q, "act": act_q, "ready": lambda h: 2 * (h // 2) + 2}, 1.0)


def none(*_):
    pass


def stage_L2_xattn(k, w):
    nc, ps = k.nc, k.ps
    k.work.clear()
    qf = k.work.take(KC, NH, 192)
    pm = k.work.take(NH // 2, D)
    kk = k.work.take(TOK)
    kvt = k.work.take(8, 2, DH)
    c1 = k.work.take(2, NH, DH, rows=96)
    f = Named()
    f.pm, f.kk, f.kvt = pm, kk, kvt
    fold_cross(k, w, f, c1, None, qf)
    w.region.at = 2 * 2 * SEQ
    t = Latent(w.region, w.region, kk, kvt, pm, w.region)
    qb = w.region.take(2, TOK)
    ro = w.region.take(2, 2, BANK, rows=96)
    sn = k.h.rearrange("p j d -> p (j d)")[0:96, 0:2 * BANK].rearrange("p (a t) -> p a t", a=2)
    swapped = ps[0:96, 0:2, :].rearrange("p a (b t) -> p a b t", t=SEQ)
    swapped = bass.AP(tensor=swapped.tensor, offset=swapped.offset + BANK,
                      ap=[list(swapped.ap[0]), [-BANK, 2]] + [list(e) for e in swapped.ap[2:]])
    with k.stage("cosed", "sined", "roped", *CORE_SEMS) as (block, s):
        def project(pe, v):
            h, half = divmod(v, 2)
            if v:
                pe.wait_ge(s["sined"], v)
            for a in range(2):
                for c in range(KC):
                    last = nc.tensor.matmul(ps[0:96, a, :], qf[:, c, h, 96 * a:96 * a + 96],
                                            k.hT[:, c, half * BANK:(half + 1) * BANK], start=c == 0, stop=c == KC - 1)
            last.then_inc(s["q_proj"], 1)

        def narrow(pe, v):
            h = v // 2
            pe.wait_ge(s["roped"], v + 1)
            if v:
                pe.wait_ge(s["q_ready"], v)
            for a in range(2):
                last = nc.tensor.matmul(ps[64 * (h % 2):64 * (h % 2) + 64, 2, :], c1[:, a, h, :], ro[:, v % 2, a, :],
                                        start=a == 0, stop=a == 1, tile_position=(0, 64 * (h % 2)))
            last.then_inc(s["narrowed"], 1)

        def pe_q(pe, v):
            project(pe, v)
            if v:
                narrow(pe, v - 1)

        def dve_q(dve, v):
            dve.wait_ge(s["q_proj"], v + 1)
            if v >= 2:
                dve.wait_ge(s["narrowed"], v - 1)
            rv = ro[:, v % 2, :, :].rearrange("p a (b t) -> p a b t", t=SEQ)
            nc.vector.tensor_tensor(rv, ps[0:96, 0:2, :].rearrange("p a (b t) -> p a b t", t=SEQ),
                                    bc(w.table[:, 0, :, :], 2, 8), ALU.mult).then_inc(s["cosed"], 1)
            if v:
                dve.wait_ge(s["roped"], v)
            nc.vector.tensor_tensor(sn.rearrange("p a (b t) -> p a b t", t=SEQ), swapped,
                                    bc(w.table[:, 1, :, :], 2, 8), ALU.mult).then_inc(s["sined"], 1)

        def copy_q(act, v):
            h, half = divmod(v, 2)
            act.wait_ge(s["narrowed"], v + 1)
            if h >= 4:
                act.wait_ge(s["scored"], h - 3)
            r = slice(64 * (h % 2), 64 * (h % 2) + 64)
            nc.scalar.copy(qb[r, (h // 2) % 2, half * BANK:(half + 1) * BANK], ps[r, 2, :]).then_inc(s["q_ready"], 1)

        def act_q(act, h):
            if h:
                copy_q(act, 2 * h - 1)

        @block.gpsimd
        def _(pool):
            for v in range(2 * NH):
                pool.wait_ge(s["cosed"], v + 1)
                pool.wait_ge(s["sined"], v + 1)
                nc.gpsimd.tensor_tensor(ro[:, v % 2, :, :], ro[:, v % 2, :, :], sn, ALU.add).then_inc(s["roped"], 1)

        attend(k, block, s, t, lambda h: (64 * (h % 2), 64 * (h % 2) + 64),
               lambda h: qb[64 * (h % 2):64 * (h % 2) + 64, (h // 2) % 2, :],
               {"pe": lambda pe, h: pe_q(pe, 2 * h), "pe_b": lambda pe, h: pe_q(pe, 2 * h + 1),
                "act": act_q, "act_b": lambda act, h: copy_q(act, 2 * h),
                "dve": lambda dve, h: dve_q(dve, 2 * h), "dve_b": lambda dve, h: dve_q(dve, 2 * h + 1), "ready": lambda h: 2 * h + 2,
                "pe_last": lambda pe: narrow(pe, 2 * NH - 1), "act_last": lambda act: copy_q(act, 2 * NH - 1)},
               1.0, turn_banks=(3, 3))


def load_L3_attn(k, w, sem):
    d, eng, r = k.dram, k.nc.sync, w.region
    w.nr = r.take(2, NH, P, rows=96)
    w.sw = r.take(2, NH, DH, rows=96)
    w.all = r.take(KC, 384)
    w.mark = r.at
    w.qnT = r.take(NH, 192)
    w.kT = r.take(NH, DH)
    w.vT = r.take(NH, DH)
    w.wo = r.take(NH, D)
    w.rope = k.fixed.take(2, DH)
    w.ropeT = k.fixed.take(2, SEQ)
    w.qw = k.fixed.take(2, rows=96)
    w.kw = k.fixed.take(DH)
    p = "L3_attn_"
    for a in range(2):
        eng.dma_start(w.nr[:, a, :, 64:128], d[p + "Wq_rot"][96 * a:96 * a + 96]).then_inc(sem, 16)
        eng.dma_start(w.sw[:, a, :, :], d[p + "Wq_swap"][96 * a:96 * a + 96]).then_inc(sem, 16)
    eng.dma_start(w.all, d[p + "Wall"].rearrange("(c p) s -> p c s", p=P)).then_inc(sem, 16)
    eng.dma_start(w.qnT, d[p + "Wq_nopeT"]).then_inc(sem, 16)
    eng.dma_start(w.kT, d[p + "WkT"]).then_inc(sem, 16)
    eng.dma_start(w.vT, d[p + "WvT"]).then_inc(sem, 16)
    eng.dma_start(w.wo, d[p + "Wo"].rearrange("(h p) d -> p h d", p=P)).then_inc(sem, 16)
    eng.dma_start(w.rope, d["const_rope64b"]).then_inc(sem, 16)
    eng.dma_start(w.ropeT, d["const_rope64T"]).then_inc(sem, 16)
    eng.dma_start(w.qw, d[p + "q_norm_w"]).then_inc(sem, 16)
    eng.dma_start(w.kw, row_on_all(d[p + "kv_norm_w"])).then_inc(sem, 16)
    return 16 * 13


def stage_L3_attn(k, w):
    nc, ps = k.nc, k.ps
    k.work.clear()
    EPS = 1e-6
    pm = k.work.take(NH // 2, D)
    kk = k.work.take(TOK)
    kvt = k.work.take(8, 2, DH)
    qnT = k.work.take(2, TOK, rows=96)
    ss = k.work.take(2, NT)
    rstd = k.work.take(2, NT)
    qb = k.work.take(3, TOK)
    sn = k.work.take(BANK)
    qn = k.h.rearrange("p j d -> p (j d)")[:, 0:NT * 192].rearrange("p (j d) -> p j d", j=NT)
    km = qb[:, 0, :].rearrange("p (j d) -> p j d", j=NT)
    sq = qb[:, 1, 0:192]
    kr = qb[:, 2, :].rearrange("p (a d) -> p a d", d=DH)
    with k.stage("lat", "sq", "mean", "std", "rstd", "qn", "km", "kvn", "kra", "krb") as (block, s):
        @block.tensor
        def _(pe):
            pe.wait_ge(w.sem, w.loaded)
            for j in range(NT):
                for c in range(KC):
                    last = nc.tensor.matmul(ps[:, j, 0:384], k.hT[:, c, j * P:(j + 1) * P], w.all[:, c, :],
                                            start=c == 0, stop=c == KC - 1)
                last.then_inc(s["lat"], 1)

        @block.scalar
        def _(act):
            for j in range(NT):
                act.wait_ge(s["lat"], j + 1)
                if j:
                    act.wait_ge(s["sq"], 2 * j)
                nc.scalar.activation(sq, ps[:, j, 0:192], ACT.Square, accum_out=ss[:, 0, j:j + 1]).then_inc(s["sq"], 1)
                act.wait_ge(s["sq"], 2 * j + 1)
                nc.scalar.activation(sq[:, 0:64], ps[:, j, 192:256], ACT.Square, accum_out=ss[:, 1, j:j + 1]).then_inc(s["sq"], 1)
            act.wait_ge(s["mean"], 2)
            nc.scalar.activation(rstd, ss, ACT.Sqrt).then_inc(s["std"], 1)

        @block.vector
        def _(dve):
            dve.wait_ge(s["lat"], NT)
            dve.wait_ge(s["sq"], 2 * NT)
            dve.wait_ge(w.sem, w.loaded)
            krv = kr[:, 0:8, :]
            nc.vector.tensor_tensor(km[:, :, 64:128], ps[:, :, 256:320], bc(w.rope[:, 0, :], 1, NT), ALU.mult).then_inc(s["kra"], 1)
            nc.vector.tensor_tensor(krv, ps[:, :, 320:384], bc(w.rope[:, 1, :], 1, NT), ALU.mult).then_inc(s["kra"], 1)
            dve.wait_ge(s["kra"], 2)
            nc.vector.tensor_tensor(km[:, :, 64:128], km[:, :, 64:128], krv, ALU.add).then_inc(s["krb"], 1)
            for g, n in ((0, 192), (1, 64)):
                nc.vector.tensor_scalar(ss[:, g, :], ss[:, g, :], 1.0 / n, EPS, ALU.mult, ALU.add).then_inc(s["mean"], 1)
            dve.wait_ge(s["std"], 1)
            nc.vector.reciprocal(ss, rstd).then_inc(s["rstd"], 1)
            dve.wait_ge(s["rstd"], 1)
            for j in range(NT):
                nc.vector.tensor_scalar(qn[:, j, :], ps[:, j, 0:192], ss[:, 0, j:j + 1], None, ALU.mult).then_inc(s["qn"], 1)
                nc.vector.scalar_tensor_tensor(km[:, j, 0:64], ps[:, j, 192:256], ss[:, 1, j:j + 1], w.kw,
                                               ALU.mult, ALU.mult).then_inc(s["kvn"], 1)

    lat = qb[0:64, 1, :]
    with k.stage("vzero", "t_qn", "t_km", "c_qn", "c_km", "c_lat", "t_kv", "nope", "noped", "pm", "pms", "kvs") as (block, s):
        @block.tensor
        def _(pe):
            for g in range(2):
                for i in range(4):
                    j = 4 * g + i
                    for a in range(2):
                        last = nc.tensor.transpose(ps[0:96, 2 * g + a, i * P:(i + 1) * P], qn[:, j, 96 * a:96 * a + 96], k.ident)
                last.then_inc(s["t_qn"], 1)
                for i in range(4):
                    last = nc.tensor.transpose(ps[:, 4 + g, i * P:(i + 1) * P], km[:, 4 * g + i, :], k.ident)
                last.then_inc(s["t_km"], 1)
            for g in range(4):
                if g:
                    pe.wait_ge(s["noped"], g)
                for i in range(4):
                    for a in range(2):
                        last = nc.tensor.matmul(ps[0:96, 6, (a * 4 + i) * DH:(a * 4 + i + 1) * DH],
                                                w.qnT[:, 4 * g + i, 96 * a:96 * a + 96], w.kT[:, 4 * g + i, :], start=True, stop=True)
                last.then_inc(s["nope"], 1)
                if g:
                    pe.wait_ge(s["pms"], g)
                for i in range(4):
                    h = 4 * g + i
                    last = nc.tensor.matmul(ps[64 * (h % 2):64 * (h % 2) + 64, 7, (i // 2) * D:(i // 2 + 1) * D],
                                            w.vT[:, h, :], w.wo[:, h, :], start=True, stop=True, tile_position=(0, 64 * (h % 2)))
                last.then_inc(s["pm"], 1)
            pe.wait_ge(s["c_qn"], 2)
            pe.wait_ge(s["c_lat"], 2)
            for n in range(8):
                last = nc.tensor.transpose(ps[:, 0, n * DH:(n + 1) * DH], lat[:, n * P:(n + 1) * P], k.ident[0:64, 0:64])
            last.then_inc(s["t_kv"], 1)

        @block.gpsimd
        def _(pool):
            nc.gpsimd.memset(kvt, 0.0).then_inc(s["vzero"], 1)

        @block.scalar
        def _(act):
            for g in range(4):
                act.wait_ge(s["pm"], g + 1)
                nc.scalar.copy(pm[:, 2 * g:2 * g + 2, :].rearrange("p a d -> p (a d)"), ps[:, 7, :]).then_inc(s["pms"], 1)

        @block.vector
        def _(dve):
            for g in range(2):
                dve.wait_ge(s["t_qn"], g + 1)
                for a in range(2):
                    ins = nc.vector.tensor_scalar(qnT[:, a, g * BANK:(g + 1) * BANK], ps[0:96, 2 * g + a, :], w.qw[:, a:a + 1], None,
                                                  ALU.mult)
                ins.then_inc(s["c_qn"], 1)
                dve.wait_ge(s["t_km"], g + 1)
                nc.vector.tensor_copy(kk[:, g * BANK:(g + 1) * BANK], ps[:, 4 + g, :]).then_inc(s["c_km"], 1)
                for jp in range(2):
                    ins = nc.vector.tensor_copy(
                        lat[:, (2 * g + jp) * 256:(2 * g + jp + 1) * 256].rearrange("p (b j t) -> p b j t", b=2, j=2),
                        ps[0:64, 4 + g, jp * 256:(jp + 1) * 256].rearrange("p (j b t) -> p b j t", j=2, b=2))
                ins.then_inc(s["c_lat"], 1)
            for g in range(4):
                dve.wait_ge(s["nope"], g + 1)
                nc.vector.tensor_copy(w.nr[:, :, 4 * g:4 * g + 4, 0:64],
                                      ps[0:96, 6, :].rearrange("p (a i d) -> p a i d", a=2, i=4)).then_inc(s["noped"], 1)
            dve.wait_ge(s["t_kv"], 1)
            dve.wait_ge(s["vzero"], 1)
            for jj in range(2):
                rows = slice(64 * jj, 64 * jj + 64)
                nc.vector.tensor_copy(kvt[rows, :, jj, :], ps[rows, 0, :].rearrange("p (n d) -> p n d", d=DH)).then_inc(s["kvs"], 1)

    w.region.at = w.mark
    t = Latent(w.region, k.work, kk, kvt, pm, Region(k.h.rearrange("p j d -> p (j d)"), NT * D))
    hi = slice(64, 128)
    with k.stage("q_top", "cosed", "sined", *CORE_SEMS) as (block, s):
        def pe_q(pe, v):
            h, half = divmod(v, 2)
            if v:
                pe.wait_ge(s["sined"], v)
                pe.wait_ge(s["q_top"], v)
            tok = slice(half * BANK, (half + 1) * BANK)
            for a in range(2):
                nc.tensor.matmul(ps[:, 0, :], w.nr[:, a, h, :], qnT[:, a, tok], start=a == 0, stop=a == 1)
            for a in range(2):
                last = nc.tensor.matmul(ps[hi, 1, :], w.sw[:, a, h, :], qnT[:, a, tok], start=a == 0, stop=a == 1,
                                        tile_position=(0, 64))
            last.then_inc(s["q_proj"], 1)

        def act_q(act, v):
            h = v // 2
            act.wait_ge(s["q_proj"], v + 1)
            if h >= 3:
                act.wait_ge(s["scored"], h - 2)
            nc.scalar.copy(qb[0:64, h % 3, (v % 2) * BANK:(v % 2 + 1) * BANK], ps[0:64, 0, :]).then_inc(s["q_top"], 1)

        def dve_q(dve, v):
            h = v // 2
            dve.wait_ge(s["q_proj"], v + 1)
            if h >= 3:
                dve.wait_ge(s["scored"], h - 2)
            tab = lambda i: bc(w.ropeT[hi, i, :], 1, 8)
            nc.vector.tensor_tensor(qb[hi, h % 3, (v % 2) * BANK:(v % 2 + 1) * BANK].rearrange("p (b t) -> p b t", t=SEQ),
                                    ps[hi, 0, :].rearrange("p (b t) -> p b t", t=SEQ), tab(0), ALU.mult).then_inc(s["cosed"], 1)
            if v:
                dve.wait_ge(s["q_ready"], v)
            nc.vector.tensor_tensor(sn[hi, :].rearrange("p (b t) -> p b t", t=SEQ),
                                    ps[hi, 1, :].rearrange("p (b t) -> p b t", t=SEQ), tab(1), ALU.mult).then_inc(s["sined"], 1)

        @block.gpsimd
        def _(pool):
            for v in range(2 * NH):
                q = qb[hi, (v // 2) % 3, (v % 2) * BANK:(v % 2 + 1) * BANK]
                pool.wait_ge(s["q_top"], v + 1)
                pool.wait_ge(s["cosed"], v + 1)
                pool.wait_ge(s["sined"], v + 1)
                nc.gpsimd.tensor_tensor(q, q, sn[hi, :], ALU.add).then_inc(s["q_ready"], 1)

        attend(k, block, s, t, lambda h: (0, P), lambda h: qb[:, h % 3, :],
               {"pe": lambda pe, h: pe_q(pe, 2 * h), "pe_b": lambda pe, h: pe_q(pe, 2 * h + 1),
                "act": lambda act, h: act_q(act, 2 * h), "act_b": lambda act, h: act_q(act, 2 * h + 1),
                "dve": lambda dve, h: dve_q(dve, 2 * h), "dve_b": lambda dve, h: dve_q(dve, 2 * h + 1), "ready": lambda h: 2 * h + 2}, 192 ** -0.5, causal=k.causal)



class First:

    def __init__(self, room, E):
        self.mx, self.eq, self.mr = room.take(NT), room.take(NT, E), room.take(NT)


def pick_first(k, chain, vals, f, sel):
    nc = k.nc
    E = vals.shape[-1]
    chain.step(nc.vector.tensor_reduce(f.mx, vals, AX.X, ALU.max))
    chain.step(nc.vector.tensor_tensor(f.eq, vals, bc(f.mx, 2, E), ALU.is_equal))
    chain.step(nc.vector.tensor_tensor(f.eq, f.eq, bc(k.rev[:, 0:E], 1, NT), ALU.mult))
    chain.step(nc.vector.tensor_reduce(f.mr, f.eq, AX.X, ALU.max))
    chain.step(nc.vector.tensor_tensor(sel, f.eq, bc(f.mr, 2, E), ALU.is_equal))


def softmax_rows(k, dve, chain, s, logits, pr, mx, sm):
    nc = k.nc
    E = pr.shape[-1]
    chain.step(nc.vector.tensor_reduce(mx, logits, AX.X, ALU.max))
    nc.vector.tensor_tensor(pr, logits, bc(mx, 2, E), ALU.subtract).then_inc(s["shifted"], 1)
    dve.wait_ge(s["exps"], 1)
    chain.step(nc.vector.tensor_reduce(sm, pr, AX.X, ALU.add))
    chain.step(nc.vector.reciprocal(sm, sm))
    chain.step(nc.vector.tensor_tensor(pr, pr, bc(sm, 2, E), ALU.mult))


def route_logits(k, pe, w_router, E, bank, sem):
    for j in range(NT):
        for c in range(KC):
            last = k.nc.tensor.matmul(k.ps[:, bank, j * E:(j + 1) * E], k.hT[:, c, j * P:(j + 1) * P],
                                      w_router[:, c, :], start=c == 0, stop=c == KC - 1)
    last.then_inc(sem, 1)


def load_L0_ffn(k, w, sem):
    d, eng, r = k.dram, k.nc.sync, w.region
    w.fc1, w.fc2 = r.take(8, KC, D), r.take(8, KC, D)
    w.gate, w.b1, w.b2, w.alpha = r.take(KC, 8), r.take(2, 8), r.take(D, rows=8), r.take(8)
    p = "L0_ffn_"
    eng.dma_start(w.gate, d[p + "gate_w"].rearrange("(c p) e -> p c e", p=P)).then_inc(sem, 16)
    eng.dma_start(w.b1, d[p + "fc1_b"]).then_inc(sem, 16)
    eng.dma_start(w.b2, d[p + "fc2_b"]).then_inc(sem, 16)
    eng.dma_start(w.alpha, row_on_all(d[p + "alpha"])).then_inc(sem, 16)
    for e in range(8):
        eng.dma_start(w.fc1[:, e], d[p + "fc1_w"][e].rearrange("(c p) i -> p c i", p=P)).then_inc(sem, 16)
        eng.dma_start(w.fc2[:, e], d[p + "fc2_w"][e].rearrange("(c p) i -> p c i", p=P)).then_inc(sem, 16)
    return 16 * 20


def stage_L0_ffn(k, w):
    nc, ps, x, E = k.nc, k.ps, k.x, 8
    k.work.clear()
    r = k.work
    pr, sel, sel2, rest, comb = (r.take(NT, E) for _ in range(5))
    f = First(r, E)
    mx, sm = r.take(NT), r.take(NT)
    act1 = r.take(2, KC, TOK)
    combT = r.take(TOK, rows=E)
    h_top, h_rest = k.rounded.take(KC, TOK, dt=F32R), k.rounded.take(KC, TOK, dt=F32R)
    w_top, w_rest = k.rounded.take(2, KC, P, dt=F32R), k.rounded.take(2, KC, P, dt=F32R)
    half_weights = lambda q: w.fc1[:, q // 2, :, (q % 2) * P:(q % 2 + 1) * P]
    with k.stage("h_top", "h_rest", "w_top", "w_rest", "logits", "shifted", "exps", "chain", "comb", "combT", "cT", "h1", "gelu", "y", "acc", "bias", "biased",
                 *NORM_SEMS) as (block, s):
        def accumulate_bank(i):
            return ps[:, 4 + i, :].rearrange("p (a d) -> p a d", a=2)

        @block.tensor
        def _(pe):
            pe.wait_ge(w.sem, w.loaded)
            route_logits(k, pe, w.gate, E, 7, s["logits"])
            for e in range(E + 1):
                if e < E:
                    for m in range(2):
                        q = 2 * e + m
                        pe.wait_ge(s["w_rest"], q + 1)
                        if e == 0:
                            pe.wait_ge(s["h_rest"], KC)
                        for half in range(2):
                            n = 4 * e + 2 * m + half
                            if e:
                                pe.wait_ge(s["gelu"], n - 3)
                            for c in range(KC):
                                for part, (a, b) in enumerate(((w_top, h_top), (w_top, h_rest), (w_rest, h_top))):
                                    last = nc.tensor.matmul(ps[:, 2 * m + half, :], a[:, q % 2, c, :],
                                                            b[:, c, half * BANK:(half + 1) * BANK],
                                                            start=c == 0 and part == 0, stop=c == KC - 1 and part == 2)
                            last.then_inc(s["h1"], 1)
                if e == 0:
                    pe.wait_ge(s["comb"], 1)
                    for j in range(NT):
                        last = nc.tensor.transpose(ps[0:E, 5 + j // 4, (j % 4) * P:(j % 4 + 1) * P], comb[:, j, :], k.ident)
                    last.then_inc(s["combT"], 1)
                    pe.wait_ge(s["cT"], 1)
                    for i in range(4):
                        for jj in range(2):
                            j = 2 * i + jj
                            last = nc.tensor.matmul(ps[:, 4 + i, jj * D:(jj + 1) * D], combT[:, j * P:(j + 1) * P], w.b2,
                                                    start=True, stop=True)
                        last.then_inc(s["bias"], 1)
                if e >= 1:
                    pe.wait_ge(s["gelu"], 4 * e)
                    for i in range(4):
                        if e >= 2:
                            pe.wait_ge(s["acc"], 8 * (e - 2) + 2 * i + 2)
                        else:
                            pe.wait_ge(s["biased"], i + 1)
                        for jj in range(2):
                            j = 2 * i + jj
                            for c in range(KC):
                                last = nc.tensor.matmul(ps[:, 4 + i, jj * D:(jj + 1) * D], act1[:, (e - 1) % 2, c, j * P:(j + 1) * P],
                                                        w.fc2[:, e - 1, c, :], start=c == 0, stop=c == KC - 1)
                        last.then_inc(s["y"], 1)
            for i in range(NT // 2):
                norm_turn(k, s, pe, i, (0, 1))

        @block.gpsimd
        def _(pool):
            for q in range(2 * E):
                pool.wait_ge(s["w_top"], q + 1)
                nc.gpsimd.tensor_tensor(w_rest[:, q % 2], half_weights(q), w_top[:, q % 2], ALU.subtract).then_inc(s["w_rest"], 1)

        def round_weights(act, q):
            nc.scalar.copy(w_top[:, q % 2], half_weights(q)).then_inc(s["w_top"], 1)

        @block.scalar
        def _(act):
            for c in range(KC):
                nc.scalar.copy(h_top[:, c, :], k.hT[:, c, :]).then_inc(s["h_top"], 1)
            act.wait_ge(w.sem, w.loaded)
            round_weights(act, 0)
            round_weights(act, 1)
            act.wait_ge(s["shifted"], 1)
            nc.scalar.activation(pr, pr, ACT.Exp).then_inc(s["exps"], 1)
            for e in range(E):
                if e >= 2:
                    act.wait_ge(s["y"], 4 * (e - 1))
                for m in range(2):
                    for half in range(2):
                        act.wait_ge(s["h1"], 4 * e + 2 * m + half + 1)
                        nc.scalar.activation(act1[:, e % 2, m, half * BANK:(half + 1) * BANK], ps[:, 2 * m + half, :], ACT.Gelu,
                                             bias=w.b1[:, m, e:e + 1]).then_inc(s["gelu"], 1)
                    if e + 1 < E:
                        round_weights(act, 2 * e + m + 2)
            norm_scalar_part(k, s, act, (0, 1))

        @block.vector
        def _(dve):
            chain = Chain(dve, s["chain"])
            for c in range(KC):
                dve.wait_ge(s["h_top"], c + 1)
                nc.vector.tensor_tensor(h_rest[:, c, :], k.hT[:, c, :], h_top[:, c, :], ALU.subtract).then_inc(s["h_rest"], 1)
            dve.wait_ge(w.sem, w.loaded)
            dve.wait_ge(s["logits"], 1)
            softmax_rows(k, dve, chain, s, ps[:, 7, 0:NT * E].rearrange("p (j e) -> p j e", e=E), pr, mx, sm)
            pick_first(k, chain, pr, f, sel)
            chain.step(nc.vector.scalar_tensor_tensor(rest, sel, -2.0, pr, ALU.mult, ALU.add))
            pick_first(k, chain, rest, f, sel2)
            chain.step(nc.vector.tensor_tensor(sel, sel, sel2, ALU.add))
            chain.step(nc.vector.tensor_tensor(pr, pr, sel, ALU.mult))
            chain.step(nc.vector.tensor_reduce(sm, pr, AX.X, ALU.add))
            chain.step(nc.vector.reciprocal(sm, sm))
            chain.step(nc.vector.tensor_tensor(pr, pr, bc(sm, 2, E), ALU.mult))
            nc.vector.tensor_tensor(comb, pr, bc(w.alpha, 1, NT), ALU.mult).then_inc(s["comb"], 1)
            dve.wait_ge(s["combT"], 1)
            nc.vector.tensor_copy(combT, ps[0:E, 5:7, :].rearrange("p a b -> p (a b)")).then_inc(s["cT"], 1)
            for i in range(4):
                dve.wait_ge(s["bias"], i + 1)
                nc.vector.tensor_tensor(x[:, 2 * i:2 * i + 2, :], x[:, 2 * i:2 * i + 2, :], accumulate_bank(i), ALU.add).then_inc(s["biased"], 1)
            dve.wait_ge(s["biased"], 4)
            for e in range(E):
                for j in range(NT):
                    if j % 2 == 0:
                        dve.wait_ge(s["y"], 4 * e + j // 2 + 1)
                    if e:
                        dve.wait_ge(s["acc"], 8 * (e - 1) + j + 1)
                    nc.vector.scalar_tensor_tensor(x[:, j, :], accumulate_bank(j // 2)[:, j % 2, :], comb[:, j, e:e + 1], x[:, j, :],
                                                   ALU.mult, ALU.add).then_inc(s["acc"], 1)
                    if e == E - 1 and j % 2:
                        dve.wait_ge(s["acc"], 8 * e + j + 1)
                        norm_front(k, s, dve, j // 2)
                        if j > 1:
                            norm_back(k, s, dve, j // 2 - 1)
            norm_back(k, s, dve, NT // 2 - 1)


def load_L1_ffn(k, w, sem):
    d, eng, r = k.dram, k.nc.sync, w.region
    w.g, w.u, w.d = r.take(8, KC, D), r.take(8, KC, D), r.take(8, KC, D)
    w.low = [(r.take(2, D, rows=64), r.take(2, D, rows=64)) for _ in range(3)]
    w.router, w.temp = r.take(KC, 8), r.take(1)
    p = "L1_ffn_"
    eng.dma_start(w.router, d[p + "Wr"].rearrange("(c p) e -> p c e", p=P)).then_inc(sem, 16)
    eng.dma_start(w.temp, row_on_all(d[p + "temperature"])).then_inc(sem, 16)
    for (a, b), n in zip(w.low, "GUD"):
        eng.dma_start(a, d[p + n + "aT"].rearrange("e r d -> r e d")).then_inc(sem, 16)
        eng.dma_start(b, d[p + n + "b"].rearrange("e r d -> r e d")).then_inc(sem, 16)
    for e in range(8):
        for t, n in ((w.g, "Wg"), (w.u, "Wu"), (w.d, "Wd")):
            eng.dma_start(t[:, e], d[p + n][e].rearrange("(c p) i -> p c i", p=P)).then_inc(sem, 16)
    return 16 * (8 + 24)


def stage_L1_ffn(k, w):
    import math
    nc, ps, x, E = k.nc, k.ps, k.x, 8
    CENTER, LOWER, UPPER = 1.0 / math.e, 0.5 - math.log(4.0 / 3.0), 0.5
    k.work.clear()
    r = k.work
    z, dist, fb, sel, sel2, zone, wt = (r.take(NT, E) for _ in range(7))
    f = First(r, E)
    sm, sm2, ne = r.take(NT), r.take(NT), r.take(NT)
    mid = r.take(2, KC, TOK)
    sil = r.take(2, BANK)
    h_top, h_rest = k.rounded.take(KC, TOK, dt=F32R), k.rounded.take(KC, TOK, dt=F32R)
    w_top, w_rest = k.rounded.take(2, 2, KC, P, dt=F32R), k.rounded.take(2, 2, KC, P, dt=F32R)
    half_weights = lambda q: [t[:, q // 2, :, (q % 2) * P:(q % 2 + 1) * P] for t in (w.g, w.u)]
    with k.stage("h_top", "h_rest", "w_top", "w_rest", "low", "lowed", "logits", "z", "sig", "dist", "expd", "chain", "gu", "silu", "mid", "y", "acc",
                 *NORM_SEMS) as (block, s):
        def low_targets():
            return [(t, e, c, ab) for t, ab in zip((w.g, w.u, w.d), w.low) for e in range(2) for c in range(KC)]

        @block.tensor
        def _(pe):
            pe.wait_ge(w.sem, w.loaded)
            route_logits(k, pe, w.router, E, 7, s["logits"])
            for n, (_, e, c, (a, b)) in enumerate(low_targets()):
                last = nc.tensor.matmul(ps[:, n // 2, (n % 2) * D:(n % 2 + 1) * D], a[:, e, c * P:(c + 1) * P], b[:, e, :],
                                        start=True, stop=True)
            last.then_inc(s["low"], 1)
            pe.wait_ge(s["lowed"], 6)
            pe.wait_ge(s["h_rest"], KC)
            for e in range(E + 1):
                if e < E:
                    for m in range(2):
                        q = 2 * e + m
                        pe.wait_ge(s["w_rest"], 2 * q + 2)
                        for half in range(2):
                            n = 4 * e + 2 * m + half
                            if n >= 2:
                                pe.wait_ge(s["mid"], n - 1)
                            for i in range(2):
                                for c in range(KC):
                                    for part, (a, b) in enumerate(((w_top, h_top), (w_top, h_rest), (w_rest, h_top))):
                                        last = nc.tensor.matmul(ps[:, 2 * (n % 2) + i, :], a[:, q % 2, i, c, :],
                                                                b[:, c, half * BANK:(half + 1) * BANK],
                                                                start=c == 0 and part == 0, stop=c == KC - 1 and part == 2)
                            last.then_inc(s["gu"], 1)
                if e >= 1:
                    pe.wait_ge(s["mid"], 4 * e)
                    for i in range(4):
                        if e >= 2:
                            pe.wait_ge(s["acc"], 8 * (e - 2) + 2 * i + 2)
                        for jj in range(2):
                            j = 2 * i + jj
                            for c in range(KC):
                                last = nc.tensor.matmul(ps[:, 4 + i, jj * D:(jj + 1) * D], mid[:, (e - 1) % 2, c, j * P:(j + 1) * P],
                                                        w.d[:, e - 1, c, :], start=c == 0, stop=c == KC - 1)
                        last.then_inc(s["y"], 1)
            for i in range(NT // 2):
                norm_turn(k, s, pe, i, (0, 1))

        @block.gpsimd
        def _(pool):
            for q in range(2 * E):
                pool.wait_ge(s["w_top"], 2 * q + 2)
                for i, t in enumerate(half_weights(q)):
                    nc.gpsimd.tensor_tensor(w_rest[:, q % 2, i], t, w_top[:, q % 2, i], ALU.subtract).then_inc(s["w_rest"], 1)

        def round_weights(act, q):
            for i, t in enumerate(half_weights(q)):
                nc.scalar.copy(w_top[:, q % 2, i], t).then_inc(s["w_top"], 1)

        @block.scalar
        def _(act):
            for c in range(KC):
                nc.scalar.copy(h_top[:, c, :], k.hT[:, c, :]).then_inc(s["h_top"], 1)
            act.wait_ge(w.sem, w.loaded)
            act.wait_ge(s["lowed"], 6)
            round_weights(act, 0)
            act.wait_ge(s["z"], 1)
            nc.scalar.activation(z, z, ACT.Sigmoid).then_inc(s["sig"], 1)
            act.wait_ge(s["dist"], 1)
            nc.scalar.activation(wt, dist, ACT.Exp, scale=-1.0 / 0.1).then_inc(s["expd"], 1)
            nc.scalar.activation(fb, dist, ACT.Exp, scale=-1.0 / 0.3).then_inc(s["expd"], 1)
            for n in range(4 * E):
                act.wait_ge(s["gu"], n + 1)
                if n >= 2:
                    act.wait_ge(s["mid"], n - 1)
                nc.scalar.activation(sil[:, n % 2, :], ps[:, 2 * (n % 2), :], ACT.Silu).then_inc(s["silu"], 1)
                if n % 2 == 0 and n // 2 + 1 < 2 * E:
                    round_weights(act, n // 2 + 1)
            norm_scalar_part(k, s, act, (0, 1))

        @block.vector
        def _(dve):
            chain = Chain(dve, s["chain"])
            for c in range(KC):
                dve.wait_ge(s["h_top"], c + 1)
                nc.vector.tensor_tensor(h_rest[:, c, :], k.hT[:, c, :], h_top[:, c, :], ALU.subtract).then_inc(s["h_rest"], 1)
            dve.wait_ge(w.sem, w.loaded)
            dve.wait_ge(s["logits"], 1)
            chain.step(nc.vector.reciprocal(w.temp, w.temp))
            nc.vector.tensor_scalar(z, ps[:, 7, 0:NT * E].rearrange("p (j e) -> p j e", e=E), w.temp, None, ALU.mult).then_inc(s["z"], 1)
            dve.wait_ge(s["low"], 1)
            for n in range(0, 12, 2):
                t, e = low_targets()[n][0:2]
                nc.vector.tensor_tensor(t[:, e], t[:, e], ps[:, n // 2, :].rearrange("p (c d) -> p c d", c=2), ALU.add).then_inc(s["lowed"], 1)
            dve.wait_ge(s["sig"], 1)
            chain.step(nc.vector.tensor_scalar(zone, z, LOWER, None, ALU.is_ge))
            chain.step(nc.vector.scalar_tensor_tensor(zone, z, UPPER, zone, ALU.is_le, ALU.mult))
            chain.step(nc.vector.tensor_scalar(dist, z, CENTER, None, ALU.subtract))
            nc.vector.scalar_tensor_tensor(dist, dist, -1.0, dist, ALU.mult, ALU.max).then_inc(s["dist"], 1)
            dve.wait_ge(s["expd"], 2)
            chain.step(nc.vector.tensor_tensor(wt, wt, zone, ALU.mult))
            chain.step(nc.vector.tensor_reduce(sm, wt, AX.X, ALU.add))
            chain.step(nc.vector.tensor_scalar(ne, sm, 1e-8, None, ALU.is_lt))
            pick_first(k, chain, fb, f, sel)
            chain.step(nc.vector.scalar_tensor_tensor(zone, sel, -2.0, fb, ALU.mult, ALU.add))
            pick_first(k, chain, zone, f, sel2)
            chain.step(nc.vector.tensor_tensor(sel, sel, sel2, ALU.add))
            chain.step(nc.vector.tensor_tensor(fb, fb, sel, ALU.mult))
            chain.step(nc.vector.tensor_reduce(sm2, fb, AX.X, ALU.add))
            chain.step(nc.vector.tensor_scalar(sm2, sm2, 1e-8, None, ALU.max))
            chain.step(nc.vector.reciprocal(sm2, sm2))
            chain.step(nc.vector.tensor_tensor(sm2, sm2, ne, ALU.mult))
            chain.step(nc.vector.tensor_tensor(fb, fb, bc(sm2, 2, E), ALU.mult))
            chain.step(nc.vector.tensor_scalar(ne, ne, -1.0, 1.0, ALU.mult, ALU.add))
            chain.step(nc.vector.tensor_tensor(wt, wt, bc(ne, 2, E), ALU.mult))
            chain.step(nc.vector.tensor_tensor(wt, wt, fb, ALU.add))
            chain.step(nc.vector.tensor_reduce(sm, wt, AX.X, ALU.add))
            chain.step(nc.vector.tensor_scalar(sm, sm, 1e-8, None, ALU.max))
            chain.step(nc.vector.reciprocal(sm, sm))
            chain.step(nc.vector.tensor_tensor(wt, wt, bc(sm, 2, E), ALU.mult))

            def products(e):
                for i in range(4):
                    n = 4 * e + i
                    dve.wait_ge(s["silu"], n + 1)
                    if i == 0 and e >= 2:
                        dve.wait_ge(s["y"], 4 * (e - 1))
                    nc.vector.tensor_tensor(mid[:, e % 2, i // 2, (i % 2) * BANK:(i % 2 + 1) * BANK], sil[:, n % 2, :],
                                            ps[:, 2 * (n % 2) + 1, :], ALU.mult).then_inc(s["mid"], 1)

            def accumulate(e):
                for j in range(NT):
                    if j % 2 == 0:
                        dve.wait_ge(s["y"], 4 * e + j // 2 + 1)
                    if e:
                        dve.wait_ge(s["acc"], 8 * (e - 1) + j + 1)
                    nc.vector.scalar_tensor_tensor(x[:, j, :], ps[:, 4 + j // 2, (j % 2) * D:(j % 2 + 1) * D], wt[:, j, e:e + 1], x[:, j, :],
                                                   ALU.mult, ALU.add).then_inc(s["acc"], 1)
                    if e == E - 1 and j % 2:
                        dve.wait_ge(s["acc"], 8 * e + j + 1)
                        norm_front(k, s, dve, j // 2)
                        if j > 1:
                            norm_back(k, s, dve, j // 2 - 1)

            for e in range(E):
                products(e)
                if e:
                    accumulate(e - 1)
            accumulate(E - 1)
            norm_back(k, s, dve, NT // 2 - 1)


def load_L2_ffn(k, w, sem):
    d, eng, r = k.dram, k.nc.sync, w.region
    w.mask = r.take(32, KC, D)
    w.wT, w.router, w.scale = k.fixed.take(KC, D), k.fixed.take(KC, 32), k.fixed.take(D)
    p = "L2_ffn_"
    eng.dma_start(w.wT, d[p + "weightT"].rearrange("(c p) o -> p c o", p=P)).then_inc(sem, 16)
    eng.dma_start(w.router, d[p + "routerT"].rearrange("(c p) e -> p c e", p=P)).then_inc(sem, 16)
    eng.dma_start(w.scale, row_on_all(d[p + "scale"])).then_inc(sem, 16)
    for e in range(32):
        eng.dma_start(w.mask[:, e], d[p + "masksT"][e].rearrange("(c p) o -> p c o", p=P)).then_inc(sem, 16)
    return 16 * 35


def stage_L2_ffn(k, w):
    nc, ps, x, E = k.nc, k.ps, k.x, 32
    MAGIC = 1.5 * 2 ** 23
    k.work.clear()
    r = k.work
    pr, sel = r.take(NT, E), r.take(NT, E)
    f = First(r, E)
    mx, sm = r.take(NT), r.take(NT)
    acc = k.h
    h_top, h_rest = k.rounded.take(KC, TOK, dt=F32R), k.rounded.take(KC, TOK, dt=F32R)
    w_top, w_rest = k.rounded.take(2, KC, D, dt=F32R), k.rounded.take(2, KC, D, dt=F32R)
    with k.stage("logits", "shifted", "exps", "chain", "ternary", "masked", "h_top", "h_rest", "w_top", "w_rest", "y", "acc", "zero", "scaled", "added",
                 *NORM_SEMS) as (block, s):
        @block.tensor
        def _(pe):
            pe.wait_ge(w.sem, w.loaded)
            route_logits(k, pe, w.router, E, 7, s["logits"])
            pe.wait_ge(s["shifted"], 1)
            pe.wait_ge(s["h_rest"], KC)
            for e in range(E):
                pe.wait_ge(s["w_rest"], e + 1)
                for i in range(4):
                    n = 4 * e + i
                    if n >= 8:
                        pe.wait_ge(s["acc"], 2 * (n - 8) + 2)
                    for jj in range(2):
                        j = 2 * i + jj
                        for c in range(KC):
                            for part, (a, b) in enumerate(((h_top, w_top), (h_top, w_rest), (h_rest, w_top))):
                                last = nc.tensor.matmul(ps[:, n % 8, jj * D:(jj + 1) * D], a[:, c, j * P:(j + 1) * P],
                                                        b[:, e % 2, c, :], start=c == 0 and part == 0, stop=c == KC - 1 and part == 2)
                    last.then_inc(s["y"], 1)
            pe.wait_ge(s["acc"], 8 * (E - 1))
            for i in range(NT // 2):
                norm_turn(k, s, pe, i, (0, 1))

        @block.scalar
        def _(act):
            for c in range(KC):
                nc.scalar.copy(h_top[:, c, :], k.hT[:, c, :]).then_inc(s["h_top"], 1)
            for e in range(E):
                act.wait_ge(s["masked"], e + 1)
                if e >= 2:
                    act.wait_ge(s["y"], 4 * e - 4)
                nc.scalar.copy(w_top[:, e % 2], w.mask[:, e]).then_inc(s["w_top"], 1)
                if e == 0:
                    act.wait_ge(s["shifted"], 1)
                    nc.scalar.activation(pr, pr, ACT.Exp).then_inc(s["exps"], 1)
            norm_scalar_part(k, s, act, (0, 1))

        @block.gpsimd
        def _(pool):
            nc.gpsimd.memset(acc, 0.0).then_inc(s["zero"], 1)
            pool.wait_ge(s["ternary"], 1)
            for e in range(E):
                nc.gpsimd.tensor_tensor(w.mask[:, e], w.mask[:, e], w.wT, ALU.mult).then_inc(s["masked"], 1)

        @block.vector
        def _(dve):
            chain = Chain(dve, s["chain"])
            dve.wait_ge(w.sem, w.loaded)
            chain.step(nc.vector.tensor_scalar(w.wT, w.wT, 2.0, 1.0, ALU.mult, ALU.min))
            chain.step(nc.vector.tensor_scalar(w.wT, w.wT, -1.0, MAGIC, ALU.max, ALU.add))
            nc.vector.tensor_scalar(w.wT, w.wT, MAGIC, None, ALU.subtract).then_inc(s["ternary"], 1)
            for c in range(KC):
                dve.wait_ge(s["h_top"], c + 1)
                nc.vector.tensor_tensor(h_rest[:, c, :], k.hT[:, c, :], h_top[:, c, :], ALU.subtract).then_inc(s["h_rest"], 1)

            def rest(e):
                dve.wait_ge(s["w_top"], e + 1)
                nc.vector.tensor_tensor(w_rest[:, e % 2], w.mask[:, e], w_top[:, e % 2], ALU.subtract).then_inc(s["w_rest"], 1)

            rest(0)
            dve.wait_ge(s["logits"], 1)
            softmax_rows(k, dve, chain, s, ps[:, 7, 0:NT * E].rearrange("p (j e) -> p j e", e=E), pr, mx, sm)
            pick_first(k, chain, pr, f, sel)
            chain.step(nc.vector.tensor_tensor(sel, sel, bc(f.mx, 2, E), ALU.mult))
            dve.wait_ge(s["zero"], 1)
            for e in range(E):
                if e + 1 < E:
                    rest(e + 1)
                for j in range(NT):
                    n = 4 * e + j // 2
                    if j % 2 == 0:
                        dve.wait_ge(s["y"], n + 1)
                    if e:
                        dve.wait_ge(s["acc"], 8 * (e - 1) + j + 1)
                    nc.vector.scalar_tensor_tensor(acc[:, j, :], ps[:, n % 8, (j % 2) * D:(j % 2 + 1) * D], sel[:, j, e:e + 1],
                                                   acc[:, j, :], ALU.mult, ALU.add).then_inc(s["acc"], 1)
                    if e == E - 1 and j % 2:
                        i = j // 2
                        pair = slice(2 * i, 2 * i + 2)
                        dve.wait_ge(s["acc"], 8 * e + j + 1)
                        nc.vector.tensor_tensor(acc[:, pair, :], acc[:, pair, :], bc(w.scale, 1, 2), ALU.mult).then_inc(s["scaled"], 1)
                        dve.wait_ge(s["scaled"], i + 1)
                        nc.vector.tensor_tensor(x[:, pair, :], x[:, pair, :], acc[:, pair, :], ALU.add).then_inc(s["added"], 1)
                        dve.wait_ge(s["added"], i + 1)
                        norm_front(k, s, dve, i)
                        if i:
                            norm_back(k, s, dve, i - 1)
            norm_back(k, s, dve, NT // 2 - 1)


def load_L3_ffn(k, w, sem):
    d, eng, r = k.dram, k.nc.sync, w.region
    w.a, w.b, w.router = r.take(KC, BANK), r.take(4, D), r.take(KC, 8)
    p = "L3_ffn_"
    eng.dma_start(w.a, d[p + "AT"].rearrange("(c p) r -> p c r", p=P)).then_inc(sem, 16)
    eng.dma_start(w.b, d[p + "BT"].rearrange("(q p) o -> p q o", p=P)).then_inc(sem, 16)
    eng.dma_start(w.router, d[p + "WgT"].rearrange("(c p) e -> p c e", p=P)).then_inc(sem, 16)
    return 48


def stage_L3_ffn(k, w):
    nc, ps, x, E, R = k.nc, k.ps, k.x, 8, 64
    SCALING = 64.0 / 16.0
    k.work.clear()
    r = k.work
    pr, sel = r.take(NT, E), r.take(NT, E)
    f = First(r, E)
    mx, sm = r.take(NT), r.take(NT)
    low, lowT = r.take(2, BANK), r.take(2, BANK)
    with k.stage("logits", "shifted", "exps", "chain", "low", "kept", "turned", "copied", "y", "added") as (block, s):
        @block.tensor
        def _(pe):
            pe.wait_ge(w.sem, w.loaded)
            route_logits(k, pe, w.router, E, 7, s["logits"])
            for i in range(NT + 2):
                if i < NT:
                    if i >= 2:
                        pe.wait_ge(s["kept"], i - 1)
                    for c in range(KC):
                        last = nc.tensor.matmul(ps[:, i % 2, :], k.hT[:, c, i * P:(i + 1) * P], w.a[:, c, :], start=c == 0, stop=c == KC - 1)
                    last.then_inc(s["low"], 1)
                if 1 <= i <= NT:
                    j = i - 1
                    pe.wait_ge(s["kept"], j + 1)
                    if j >= 2:
                        pe.wait_ge(s["copied"], j - 1)
                    for q in range(4):
                        last = nc.tensor.transpose(ps[:, 2 + j % 2, q * P:(q + 1) * P], low[:, j % 2, q * P:(q + 1) * P], k.ident)
                    last.then_inc(s["turned"], 1)
                if i >= 2:
                    j = i - 2
                    pe.wait_ge(s["copied"], j + 1)
                    if j >= 2:
                        pe.wait_ge(s["added"], j - 1)
                    for q in range(4):
                        last = nc.tensor.matmul(ps[:, 4 + j % 2, 0:D], lowT[:, j % 2, q * P:(q + 1) * P], w.b[:, q, :], start=q == 0, stop=q == 3)
                    last.then_inc(s["y"], 1)

        @block.scalar
        def _(act):
            act.wait_ge(s["shifted"], 1)
            nc.scalar.activation(pr, pr, ACT.Exp).then_inc(s["exps"], 1)
            for j in range(NT):
                act.wait_ge(s["turned"], j + 1)
                if j >= 2:
                    act.wait_ge(s["y"], j - 1)
                nc.scalar.copy(lowT[:, j % 2, :], ps[:, 2 + j % 2, :]).then_inc(s["copied"], 1)

        @block.vector
        def _(dve):
            chain = Chain(dve, s["chain"])
            dve.wait_ge(s["logits"], 1)
            softmax_rows(k, dve, chain, s, ps[:, 7, 0:NT * E].rearrange("p (j e) -> p j e", e=E), pr, mx, sm)
            pick_first(k, chain, pr, f, sel)
            chain.step(nc.vector.tensor_tensor(sel, sel, bc(f.mx, 2, E), ALU.mult))
            chain.step(nc.vector.tensor_scalar(sel, sel, SCALING, None, ALU.mult))
            for j in range(NT + 2):
                if j < NT:
                    dve.wait_ge(s["low"], j + 1)
                    if j >= 2:
                        dve.wait_ge(s["turned"], j - 1)
                    nc.vector.tensor_tensor(low[:, j % 2, :].rearrange("p (e r) -> p e r", r=R),
                                            ps[:, j % 2, :].rearrange("p (e r) -> p e r", r=R), bc(sel[:, j, :], 2, R), ALU.mult).then_inc(s["kept"], 1)
                if j >= 2:
                    dve.wait_ge(s["y"], j - 1)
                    nc.vector.tensor_tensor(x[:, j - 2, :], x[:, j - 2, :], ps[:, 4 + j % 2, 0:D], ALU.add).then_inc(s["added"], 1)



def load_L2_attn(k, w, sem):
    d, eng, r = k.dram, k.nc.sync, w.region
    w.q, w.k, w.v, w.o = (r.take(KC, D) for _ in range(4))
    w.bias = r.take(3, KC)
    w.bo, w.pmask = r.take(D), r.take(2)
    p = "L2_attn_"
    for t, n in ((w.q, "Wq"), (w.k, "Wk"), (w.v, "Wv"), (w.o, "Wo")):
        eng.dma_start(t, d[p + n].rearrange("(c p) o -> p c o", p=P)).then_inc(sem, 16)
    eng.dma_start(w.bias, d[p + "bias"]).then_inc(sem, 16)
    eng.dma_start(w.bo, row_on_all(d[p + "bo"])).then_inc(sem, 16)
    eng.dma_start(w.pmask, d["const_pmask"]).then_inc(sem, 16)
    return 16 * 7


def stage_L2_attn(k, w):
    nc, ps, x = k.nc, k.ps, k.x
    k.work.clear()
    r = w.region
    qT, kexp = r.take(KC, TOK), r.take(KC, 2, TOK)
    vblk = r.take(BATCH, 8, 2, 16)
    bk = r.take(2, KC)
    yT = k.work.take(KC, TOK)
    pr, pT = k.work.take(2, 16, SEQ), k.work.take(2, NT, P)
    mx, sm, rs = k.work.take(2, 16), k.work.take(2, 16), k.work.take(2, 16)
    with k.stage("bk", "qk", "copied", "xb") as (block, s):
        @block.tensor
        def _(pe):
            pe.wait_ge(w.sem, w.loaded)
            for i, t in enumerate((w.q, w.k)):
                for m in range(2):
                    for half in range(2):
                        for c in range(KC):
                            last = nc.tensor.matmul(ps[:, 4 * i + 2 * m + half, :], t[:, c, m * P:(m + 1) * P],
                                                    k.hT[:, c, half * BANK:(half + 1) * BANK], start=c == 0, stop=c == KC - 1)
                    last.then_inc(s["qk"], 1)

        @block.gpsimd
        def _(pool):
            pool.wait_ge(w.sem, w.loaded)
            nc.gpsimd.tensor_tensor(x, x, bc(w.bo, 1, NT), ALU.add).then_inc(s["xb"], 1)

        @block.vector
        def _(dve):
            dve.wait_ge(w.sem, w.loaded)
            for g in range(2):
                nc.vector.tensor_scalar(bk[:, g, :], w.bias[:, 1, :], w.pmask[:, g:g + 1], None, ALU.mult).then_inc(s["bk"], 1)
            for m in range(2):
                dve.wait_ge(s["qk"], m + 1)
                nc.vector.tensor_scalar(qT[:, m, :], ps[:, 2 * m:2 * m + 2, :].rearrange("p a b -> p (a b)"), w.bias[:, 0, m:m + 1], None,
                                        ALU.add).then_inc(s["copied"], 1)

        @block.scalar
        def _(act):
            act.wait_ge(w.sem, w.loaded)
            act.wait_ge(s["bk"], 2)
            for m in range(2):
                act.wait_ge(s["qk"], m + 3)
                for g in range(2):
                    nc.scalar.activation(kexp[:, m, g, :], ps[:, 4 + 2 * m:6 + 2 * m, :].rearrange("p a b -> p (a b)"), ACT.Identity,
                                         bias=bk[:, g, m:m + 1], scale=w.pmask[:, g:g + 1]).then_inc(s["copied"], 1)

    with k.stage("v", "vzero", "vals", "scored", "maxed", "centred", "expd", "summed", "recip", "probs", "turned", "copied", "pv",
                 "yT", "out", "added", *NORM_SEMS) as (block, s):
        @block.tensor
        def _(pe):
            for b in range(BATCH):
                for g in range(2):
                    for c in range(KC):
                        last = nc.tensor.matmul(ps[64 * g:64 * g + 64, b // 4, (b % 4) * P:(b % 4 + 1) * P],
                                                k.hT[:, c, b * SEQ:(b + 1) * SEQ], w.v[:, c, g * P:(g + 1) * P],
                                                start=c == 0, stop=c == KC - 1, tile_position=(0, 64 * g))
                if b % 4 == 3:
                    last.then_inc(s["v"], 1)

            def scores(u):
                c, i = divmod(u, 4)
                at = 6 * (u % 2)
                if u == 0:
                    pe.wait_ge(s["vals"], 4)
                elif u >= 2:
                    pe.wait_ge(s["centred"], u - 1)
                rows = slice(32 * i, 32 * i + 32)
                for bank in range(2):
                    nc.tensor.matmul(ps[:, at + bank, :], k.ident16, k.causal, start=True, stop=False, skip_group_check=True)
                for b in range(BATCH):
                    j = b // 2
                    last = nc.tensor.matmul(ps[64 * (b % 2):64 * (b % 2) + 64, at + j // 4, (j % 4) * P:(j % 4 + 1) * P],
                                            qT[rows, c, b * SEQ:(b + 1) * SEQ], kexp[rows, c, :, b * SEQ:(b + 1) * SEQ],
                                            start=False, stop=True, skip_group_check=True, tile_position=(32 * i, 64 * (b % 2)))
                last.then_inc(s["scored"], 1)

            def turn(u):
                pe.wait_ge(s["probs"], u + 1)
                if u:
                    pe.wait_ge(s["copied"], 2 * u)
                for j in range(NT):
                    last = nc.tensor.transpose(ps[:, 2 + j // 4, (j % 4) * P:(j % 4 + 1) * P],
                                               pr[:, u % 2, 2 * j:2 * j + 2, :].rearrange("p a t -> p (a t)"), k.ident)
                last.then_inc(s["turned"], 1)

            def weigh(u):
                c, i = divmod(u, 4)
                pe.wait_ge(s["copied"], 2 * u + 2)
                if c:
                    pe.wait_ge(s["yT"], 1)
                for b in range(BATCH):
                    last = nc.tensor.matmul(ps[32 * i:32 * i + 32, 4 + b // 8, (b % 8) * SEQ:(b % 8 + 1) * SEQ],
                                            vblk[:, b, u, :, :].rearrange("p g d -> p (g d)"),
                                            pT[:, u % 2, b // 2, 64 * (b % 2):64 * (b % 2) + 64], start=True, stop=True,
                                            tile_position=(0, 32 * i))
                last.then_inc(s["pv"], 1)

            for u in range(8 + 3):
                if u < 8:
                    scores(u)
                if 2 <= u < 10:
                    turn(u - 2)
                if u >= 3:
                    weigh(u - 3)
            pe.wait_ge(s["yT"], KC)
            pe.wait_ge(s["centred"], 8)
            pe.wait_ge(s["copied"], 16)
            for j in range(NT):
                for c in range(KC):
                    last = nc.tensor.matmul(ps[:, j // 2, (j % 2) * D:(j % 2 + 1) * D], yT[:, c, j * P:(j + 1) * P], w.o[:, c, :],
                                            start=c == 0, stop=c == KC - 1)
                if j % 2:
                    last.then_inc(s["out"], 1)
            for i in range(NT // 2):
                norm_turn(k, s, pe, i, (4, 5))

        @block.gpsimd
        def _(pool):
            nc.gpsimd.memset(vblk, 0.0).then_inc(s["vzero"], 1)

        def copy_turned(act, u):
            act.wait_ge(s["turned"], u + 1)
            if u >= 2:
                act.wait_ge(s["pv"], u - 1)
            for n in range(2):
                nc.scalar.copy(pT[:, u % 2, 4 * n:4 * n + 4, :].rearrange("p a b -> p (a b)"), ps[:, 2 + n, :]).then_inc(s["copied"], 1)

        def copy_out(act, c):
            act.wait_ge(s["pv"], 4 * c + 4)
            nc.scalar.activation(yT[:, c, :], ps[:, 4:6, :].rearrange("p a b -> p (a b)"), ACT.Identity,
                                 bias=w.bias[:, 2, c:c + 1]).then_inc(s["yT"], 1)

        @block.scalar
        def _(act):
            for u in range(8):
                act.wait_ge(s["centred"], u + 1)
                nc.scalar.activation(pr[:, u % 2, :, :], pr[:, u % 2, :, :], ACT.Exp, scale=0.25).then_inc(s["expd"], 1)
                if u >= 2:
                    copy_turned(act, u - 2)
                if u == 6:
                    copy_out(act, 0)
            copy_turned(act, 6)
            copy_turned(act, 7)
            copy_out(act, 1)
            norm_scalar_part(k, s, act, (4, 5))

        @block.vector
        def _(dve):
            dve.wait_ge(s["vzero"], 1)
            for n in range(4):
                dve.wait_ge(s["v"], n + 1)
                for g in range(2):
                    rows = slice(64 * g, 64 * g + 64)
                    ins = nc.vector.tensor_copy(vblk[rows, 4 * n:4 * n + 4, :, g, :],
                                                ps[rows, n, :].rearrange("p (b h d) -> p b h d", b=4, d=16))
                ins.then_inc(s["vals"], 1)

            def centre(u):
                sc = ps[:, 6 * (u % 2):6 * (u % 2) + 2, :].rearrange("p a (h t) -> p (a h) t", t=SEQ)
                dve.wait_ge(s["scored"], u + 1)
                nc.vector.tensor_reduce(mx[:, u % 2, :], sc, AX.X, ALU.max).then_inc(s["maxed"], 1)
                dve.wait_ge(s["maxed"], u + 1)
                if u >= 2:
                    dve.wait_ge(s["turned"], u - 1)
                nc.vector.tensor_tensor(pr[:, u % 2, :, :], sc, bc(mx[:, u % 2, :], 2, SEQ), ALU.subtract).then_inc(s["centred"], 1)

            def normalise(u):
                p, a, b = pr[:, u % 2, :, :], sm[:, u % 2, :], rs[:, u % 2, :]
                dve.wait_ge(s["expd"], u + 1)
                nc.vector.tensor_reduce(a, p, AX.X, ALU.add).then_inc(s["summed"], 1)
                dve.wait_ge(s["summed"], u + 1)
                nc.vector.reciprocal(b, a).then_inc(s["recip"], 1)
                dve.wait_ge(s["recip"], u + 1)
                nc.vector.tensor_tensor(p, p, bc(b, 2, SEQ), ALU.mult).then_inc(s["probs"], 1)

            for u in range(8):
                centre(u)
                if u:
                    normalise(u - 1)
            normalise(7)
            for i in range(4):
                dve.wait_ge(s["out"], i + 1)
                xv = x[:, 2 * i:2 * i + 2, :].rearrange("p a b -> p (a b)")
                nc.vector.tensor_tensor(xv, xv, ps[:, i, :], ALU.add).then_inc(s["added"], 1)
                dve.wait_ge(s["added"], i + 1)
                norm_front(k, s, dve, i)
                if i:
                    norm_back(k, s, dve, i - 1)
            norm_back(k, s, dve, NT // 2 - 1)



DH0, DV0, NH0 = 32, 64, 6
LEVELS = 6


def load_L0_attn(k, w, sem):
    d, eng, r = k.dram, k.nc.sync, w.region
    w.qkv = r.take(KC, 768)
    w.gate = r.take(KC, 384)
    w.ba = r.take(KC, 12)
    w.o = r.take(3, D)
    w.conv = r.take(7, 4)
    w.rows = r.take(2, NH0)
    w.norm = r.take(DV0)
    w.tri = r.take(2, P)
    w.level = r.take(LEVELS, P)
    w.head = r.take(96)
    p = "L0_attn_"
    eng.dma_start(w.qkv, d[p + "WqkvT"].rearrange("(c p) s -> p c s", p=P)).then_inc(sem, 16)
    eng.dma_start(w.gate, d[p + "WgT"].rearrange("(c p) s -> p c s", p=P)).then_inc(sem, 16)
    eng.dma_start(w.ba, d[p + "WbaT"].rearrange("(c p) s -> p c s", p=P)).then_inc(sem, 16)
    eng.dma_start(w.o, d[p + "WoT"].rearrange("(c p) s -> p c s", p=P)).then_inc(sem, 16)
    eng.dma_start(w.conv[0:96, 0:4, :], d[p + "conv_qk"]).then_inc(sem, 16)
    eng.dma_start(w.conv[:, 4:7, :], d[p + "conv_v"]).then_inc(sem, 16)
    eng.dma_start(w.rows[:, 0, :], row_on_all(d[p + "A_log"])).then_inc(sem, 16)
    eng.dma_start(w.rows[:, 1, :], row_on_all(d[p + "dt_bias"])).then_inc(sem, 16)
    eng.dma_start(w.norm, row_on_all(d[p + "norm_w"])).then_inc(sem, 16)
    eng.dma_start(w.tri, d["const_tri"]).then_inc(sem, 16)
    eng.dma_start(w.level, d["const_level"]).then_inc(sem, 16)
    eng.dma_start(w.head[0:96, :], d["const_head"]).then_inc(sem, 16)
    return 16 * 12


def stage_L0_attn(k, w):
    nc, ps, x = k.nc, k.ps, k.x
    k.work.clear()
    r = w.region
    gate = r.take(NT, 384)
    vt = r.take(NT, 384)
    beta, decay = r.take(NT, NH0), r.take(NT, NH0)
    qk = k.work.take(4, TOK, rows=96)
    mark = k.work.at, r.at
    vf = r.take(3, TOK)
    small = [k.work.take(NT, NH0) for _ in range(4)]
    sq = k.work.take(2, TOK, rows=96)
    widths = [96] * 4 + [P] * 3
    offs = [96 * n for n in range(4)] + [384 + P * n for n in range(3)]
    dst = lambda n: qk[:, n, :] if n < 4 else vf[:, n - 4, :]
    with k.stage("proj", "conv", "silu", "gate", "gated", "ba", "bac") as (block, s):
        @block.tensor
        def _(pe):
            pe.wait_ge(w.sem, w.loaded)
            for n in range(7):
                if n >= 3:
                    pe.wait_ge(s["conv"], 4 * (n - 3) + 4)
                for half in range(2):
                    for c in range(KC):
                        last = nc.tensor.matmul(ps[0:widths[n], 2 * (n % 3) + half, :], w.qkv[:, c, offs[n]:offs[n] + widths[n]],
                                                k.hT[:, c, half * BANK:(half + 1) * BANK], start=c == 0, stop=c == KC - 1)
                last.then_inc(s["proj"], 1)
                tiles = range(n, n + 1) if n < 6 else range(6, 8)
                for j in tiles:
                    if j >= 2:
                        pe.wait_ge(s["gated"], j - 1)
                    for c in range(KC):
                        last = nc.tensor.matmul(ps[:, 6 + j % 2, 0:384], k.hT[:, c, j * P:(j + 1) * P], w.gate[:, c, :],
                                                start=c == 0, stop=c == KC - 1)
                    last.then_inc(s["gate"], 1)
            pe.wait_ge(s["gated"], NT)
            for j in range(NT):
                for c in range(KC):
                    last = nc.tensor.matmul(ps[:, 6, 12 * j:12 * j + 12], k.hT[:, c, j * P:(j + 1) * P], w.ba[:, c, :],
                                            start=c == 0, stop=c == KC - 1)
            last.then_inc(s["ba"], 1)

        @block.vector
        def _(dve):
            for n in range(7):
                m = widths[n]
                dve.wait_ge(s["proj"], n + 1)
                src = ps[0:m, 2 * (n % 3):2 * (n % 3) + 2, :].rearrange("p a (b t) -> p (a b) t", t=SEQ)
                y = dst(n)[0:m, :].rearrange("p (b t) -> p b t", t=SEQ)
                taps = w.conv[0:m, n, :]
                nc.vector.tensor_scalar(y, src, taps[:, 3:4], None, ALU.mult).then_inc(s["conv"], 1)
                for back in range(1, 4):
                    dve.wait_ge(s["conv"], 4 * n + back)
                    nc.vector.scalar_tensor_tensor(y[:, :, back:], src[:, :, :SEQ - back], taps[:, 3 - back:4 - back], y[:, :, back:],
                                                   ALU.mult, ALU.add).then_inc(s["conv"], 1)

        @block.scalar
        def _(act):
            for n in range(7):
                for j in (range(n, n + 1) if n < 6 else range(6, 8)):
                    act.wait_ge(s["gate"], j + 1)
                    nc.scalar.activation(gate[:, j, :], ps[:, 6 + j % 2, 0:384], ACT.Silu).then_inc(s["gated"], 1)
                act.wait_ge(s["conv"], 4 * n + 4)
                m = widths[n]
                nc.scalar.activation(dst(n)[0:m, :], dst(n)[0:m, :], ACT.Silu).then_inc(s["silu"], 1)
            act.wait_ge(s["ba"], 1)
            ba = ps[:, 6, 0:96].rearrange("p (j e) -> p j e", e=12)
            nc.scalar.copy(decay, ba[:, :, 6:12]).then_inc(s["bac"], 1)
            nc.scalar.activation(beta, ba[:, :, 0:6], ACT.Sigmoid).then_inc(s["bac"], 1)

    z, az, e, lg = small
    rinv = k.hT[0:96]
    with k.stage("z", "az", "e", "ln", "ea", "g", "sq", "ss", "lns", "rinv", "unit", "vT", "vc", "wn") as (block, s):
        @block.tensor
        def _(pe):
            for n in range(4):
                pe.wait_ge(s["sq"], n + 1)
                if n >= 2:
                    pe.wait_ge(s["lns"], n - 1)
                for half in range(2):
                    last = nc.tensor.matmul(ps[0:96, 2 * (n % 2) + half, :], w.head[0:96, :], sq[:, n % 2, half * BANK:(half + 1) * BANK],
                                            start=True, stop=True)
                last.then_inc(s["ss"], 1)
            for j in range(NT):
                if j >= 4:
                    pe.wait_ge(s["vc"], j - 3)
                for c in range(3):
                    last = nc.tensor.transpose(ps[:, 4 + j % 4, c * P:(c + 1) * P], vf[:, c, j * P:(j + 1) * P], k.ident)
                last.then_inc(s["vT"], 1)

        @block.gpsimd
        def _(pool):
            nc.gpsimd.tensor_tensor(gate.rearrange("p j (h d) -> p (j h) d", d=DV0), gate.rearrange("p j (h d) -> p (j h) d", d=DV0),
                                    bc(w.norm, 1, NT * NH0), ALU.mult).then_inc(s["wn"], 1)

        @block.scalar
        def _(act):
            act.wait_ge(s["az"], 1)
            nc.scalar.activation(e, az, ACT.Exp, scale=-1.0).then_inc(s["e"], 1)
            nc.scalar.activation(w.rows[:, 0, :], w.rows[:, 0, :], ACT.Exp).then_inc(s["ea"], 1)
            act.wait_ge(s["e"], 1)
            act.wait_ge(s["e"], 2)
            nc.scalar.activation(lg, e, ACT.Ln).then_inc(s["ln"], 1)
            for n in (0, 2):
                for m in (n, n + 1):
                    act.wait_ge(s["ss"], m + 1)
                    if m >= 2:
                        act.wait_ge(s["unit"], m - 1)
                    nc.scalar.activation(rinv[:, m % 2, :], ps[0:96, 2 * (m % 2):2 * (m % 2) + 2, :].rearrange("p a b -> p (a b)"), ACT.Ln,
                                         bias=1e-6).then_inc(s["lns"], 1)
                for m in (n, n + 1):
                    act.wait_ge(s["lns"], m + 1)
                    nc.scalar.activation(rinv[:, m % 2, :], rinv[:, m % 2, :], ACT.Exp, scale=-0.5).then_inc(s["rinv"], 1)

        @block.vector
        def _(dve):
            nc.vector.tensor_tensor(sq[:, 0, :], qk[:, 0, :], qk[:, 0, :], ALU.mult).then_inc(s["sq"], 1)
            nc.vector.tensor_tensor(sq[:, 1, :], qk[:, 1, :], qk[:, 1, :], ALU.mult).then_inc(s["sq"], 1)
            nc.vector.tensor_tensor(z, decay, bc(w.rows[:, 1, :], 1, NT), ALU.add).then_inc(s["z"], 1)
            dve.wait_ge(s["z"], 1)
            nc.vector.scalar_tensor_tensor(az, z, -1.0, z, ALU.mult, ALU.max).then_inc(s["az"], 1)
            dve.wait_ge(s["e"], 1)
            nc.vector.tensor_scalar(e, e, 1.0, None, ALU.add).then_inc(s["e"], 1)
            dve.wait_ge(s["ln"], 1)
            nc.vector.scalar_tensor_tensor(z, z, 0.0, lg, ALU.max, ALU.add).then_inc(s["z"], 1)
            dve.wait_ge(s["z"], 2)
            dve.wait_ge(s["ea"], 1)
            nc.vector.scalar_tensor_tensor(decay, z, -1.0, bc(w.rows[:, 0, :], 1, NT), ALU.mult, ALU.mult).then_inc(s["g"], 1)
            for n in range(4):
                if n + 2 < 4:
                    dve.wait_ge(s["ss"], n + 1)
                    nc.vector.tensor_tensor(sq[:, n % 2, :], qk[:, n + 2, :], qk[:, n + 2, :], ALU.mult).then_inc(s["sq"], 1)
                dve.wait_ge(s["rinv"], n + 1)
                rv = rinv[:, n % 2, :]
                if n < 2:
                    nc.vector.scalar_tensor_tensor(qk[:, n, :], rv, DH0 ** -0.5, qk[:, n, :], ALU.mult, ALU.mult).then_inc(s["unit"], 1)
                else:
                    nc.vector.tensor_tensor(qk[:, n, :], rv, qk[:, n, :], ALU.mult).then_inc(s["unit"], 1)
            for j in range(NT):
                dve.wait_ge(s["vT"], j + 1)
                nc.vector.tensor_copy(vt[:, j, :], ps[:, 4 + j % 4, 0:384]).then_inc(s["vc"], 1)

    k.work.at, r.at = mark
    ot = k.hT.rearrange("p c t -> p (c t)")
    o_tm = k.work.take(NT, 384)
    spare = Region(k.h.rearrange("p j d -> p (j d)"), NT * D)
    dec = [k.work.take(4, P) for _ in range(2)]
    gm = [spare.take(4, P) for _ in range(2)]
    F = [k.work.take(4, P) for _ in range(2)]
    A = [k.work.take(4, P) for _ in range(2)]
    hTs = Region(ot, KC * TOK)
    Rm = [hTs.take(4, P) for _ in range(2)]
    Fl = [[Rm[a]] + [r.take(4, P) for _ in range(LEVELS - 1)] for a in range(2)]
    Tm = [hTs.take(4, P) for _ in range(2)]
    Wm = [spare.take(4, P) for _ in range(2)]
    Um = [k.work.take(4, DV0) for _ in range(2)]
    flat = lambda t: t.rearrange("p a b -> p (a b)")
    ident4 = bc(k.ident, 1, 4)
    names = ("gm", "X", "KQ", "expd", "dec", "F", "A", "Fl", "R1", "turned", "T1", "W", "Ws", "XX", "R", "T", "U", "Us", "O", "Os")
    with k.stage(*names) as (block, s):
        def nth(g, step, per):
            return 2 * per * (g // 2) + 2 * (step - 1) + g % 2 + 1

        def unit(g, i):
            return g // 2, 4 * (g % 2) + i

        @block.tensor
        def _(pe):
            def products(g):
                a = g % 2
                h = g // 2
                n, rows = h // 3, slice(32 * (h % 3), 32 * (h % 3) + 32)
                pe.wait_ge(s["gm"], g + 1)
                if g >= 2:
                    pe.wait_ge(s["Us"], g - 1)
                    pe.wait_ge(s["Os"], g - 1)
                    pe.wait_ge(s["R"], nth(g - 2, 5, 5))
                nc.tensor.matmul(ps[:, 3 * a, :], w.tri[:, 0, :], flat(gm[a]), start=True, stop=True).then_inc(s["X"], 1)
                for q, bank in ((2, 1), (0, 2)):
                    for i in range(4):
                        j = unit(g, i)[1]
                        last = nc.tensor.matmul(ps[:, 3 * a + bank, i * P:(i + 1) * P], qk[rows, 2 + n, j * P:(j + 1) * P],
                                                qk[rows, q + n, j * P:(j + 1) * P], start=True, stop=True,
                                                tile_position=(32 * (h % 3), 0))
                last.then_inc(s["KQ"], 1)

            def turn(g):
                a = g % 2
                pe.wait_ge(s["R1"], g + 1)
                pe.wait_ge(s["F"], g + 1)
                for i in range(4):
                    last = nc.tensor.transpose(ps[:, 3 * a + 1, i * P:(i + 1) * P], Rm[a][:, i, :], k.ident)
                last.then_inc(s["turned"], 1)

            def first(g, l):
                a = g % 2
                pe.wait_ge(s["Fl"], nth(g, l + 1, 6))
                pe.wait_ge(s["T1"], g + 1)
                if l >= 2:
                    pe.wait_ge(s["T"], nth(g, l - 1, 4))
                for i in range(4):
                    last = nc.tensor.matmul(ps[:, 3 * a, i * P:(i + 1) * P], Fl[a][l][:, i, :], Tm[a][:, i, :], start=True, stop=True)
                last.then_inc(s["W"], 1)

            def second(g, l):
                a = g % 2
                pe.wait_ge(s["Ws"], nth(g, l, 5))
                if l == 1:
                    pe.wait_ge(s["A"], g + 1)
                if l >= 2:
                    pe.wait_ge(s["R"], nth(g, l - 1, 5))
                if l < 5:
                    for i in range(4):
                        nc.tensor.matmul(ps[:, 3 * a + 1, i * P:(i + 1) * P], Rm[a][:, i, :], Wm[a][:, i, :], start=True, stop=True)
                for i in range(4):
                    last = nc.tensor.matmul(ps[:, 3 * a + 2, i * P:(i + 1) * P], Wm[a][:, i, :], Rm[a][:, i, :], start=True, stop=True)
                last.then_inc(s["XX"], 1)

            def solve(g):
                a, h = g % 2, g // 2
                pe.wait_ge(s["R"], nth(g, 5, 5))
                for i in range(4):
                    j = unit(g, i)[1]
                    last = nc.tensor.matmul(ps[:, 3 * a, i * DV0:(i + 1) * DV0], Rm[a][:, i, :], vt[:, j, h * DV0:(h + 1) * DV0],
                                            start=True, stop=True)
                last.then_inc(s["U"], 1)

            def outputs(g):
                a = g % 2
                pe.wait_ge(s["Us"], g + 1)
                for i in range(4):
                    last = nc.tensor.matmul(ps[:, 3 * a + 1, i * DV0:(i + 1) * DV0], A[a][:, i, :], Um[a][:, i, :], start=True, stop=True)
                last.then_inc(s["O"], 1)

            for pair in range(6):
                for g in (2 * pair, 2 * pair + 1):
                    products(g)
                for g in (2 * pair, 2 * pair + 1):
                    turn(g)
                for l in range(1, 6):
                    for g in (2 * pair, 2 * pair + 1):
                        first(g, l)
                    for g in (2 * pair, 2 * pair + 1):
                        second(g, l)
                for g in (2 * pair, 2 * pair + 1):
                    solve(g)
                for g in (2 * pair, 2 * pair + 1):
                    outputs(g)

        @block.gpsimd
        def _(pool):
            for pair in range(6):
                for g in (2 * pair, 2 * pair + 1):
                    a = g % 2
                    if g >= 2:
                        pool.wait_ge(s["X"], g - 1)
                    for i in range(4):
                        h, j = unit(g, i)
                        last = nc.gpsimd.tensor_scalar(gm[a][:, i, :], w.tri[:, 1, :], decay[:, j, h:h + 1], None, ALU.mult)
                    last.then_inc(s["gm"], 1)
                for l in range(6):
                    for g in (2 * pair, 2 * pair + 1):
                        a = g % 2
                        pool.wait_ge(s["F"], g + 1)
                        if g >= 2:
                            pool.wait_ge(s["U"], g - 1)
                            pool.wait_ge(s["W"], nth(g - 2, 5, 5))
                        nc.gpsimd.tensor_tensor(Fl[a][l], F[a], bc(w.level[:, l, :], 1, 4), ALU.mult).then_inc(s["Fl"], 1)

        @block.scalar
        def _(act):
            for pair in range(6):
                for g in (2 * pair, 2 * pair + 1):
                    a = g % 2
                    act.wait_ge(s["X"], g + 1)
                    if g >= 2:
                        act.wait_ge(s["A"], g - 1)
                    nc.scalar.activation(flat(dec[a]), ps[:, 3 * a, :], ACT.Exp).then_inc(s["expd"], 1)
                for l in range(1, 6):
                    for g in (2 * pair, 2 * pair + 1):
                        a = g % 2
                        act.wait_ge(s["W"], nth(g, l, 5))
                        if l >= 2:
                            act.wait_ge(s["XX"], nth(g, l - 1, 5))
                        nc.scalar.copy(flat(Wm[a]), ps[:, 3 * a, :]).then_inc(s["Ws"], 1)
                for g in (2 * pair, 2 * pair + 1):
                    a = g % 2
                    act.wait_ge(s["U"], g + 1)
                    if g >= 2:
                        act.wait_ge(s["O"], g - 1)
                    nc.scalar.copy(flat(Um[a]), ps[:, 3 * a, 0:4 * DV0]).then_inc(s["Us"], 1)
                for g in (2 * pair, 2 * pair + 1):
                    a = g % 2
                    h, j0 = unit(g, 0)
                    act.wait_ge(s["O"], g + 1)
                    nc.scalar.copy(o_tm[:, j0:j0 + 4, h * DV0:(h + 1) * DV0],
                                   ps[:, 3 * a + 1, 0:4 * DV0].rearrange("p (i d) -> p i d", d=DV0)).then_inc(s["Os"], 1)

        @block.vector
        def _(dve):
            for pair in range(6):
                for g in (2 * pair, 2 * pair + 1):
                    a = g % 2
                    dve.wait_ge(s["expd"], g + 1)
                    for i in range(4):
                        h, j = unit(g, i)
                        last = nc.vector.scalar_tensor_tensor(dec[a][:, i, :], dec[a][:, i, :], beta[:, j, h:h + 1], w.tri[:, 1, :],
                                                              ALU.mult, ALU.mult)
                    last.then_inc(s["dec"], 1)
                    dve.wait_ge(s["dec"], g + 1)
                    dve.wait_ge(s["KQ"], g + 1)
                    if g >= 2:
                        dve.wait_ge(s["Fl"], nth(g - 2, 6, 6))
                        dve.wait_ge(s["O"], g - 1)
                    nc.vector.tensor_tensor(flat(F[a]), flat(dec[a]), ps[:, 3 * a + 1, :], ALU.mult).then_inc(s["F"], 1)
                    nc.vector.tensor_tensor(flat(A[a]), flat(dec[a]), ps[:, 3 * a + 2, :], ALU.mult).then_inc(s["A"], 1)
                for g in (2 * pair, 2 * pair + 1):
                    a = g % 2
                    dve.wait_ge(s["Fl"], nth(g, 1, 6))
                    nc.vector.tensor_tensor(Rm[a], ident4, Fl[a][0], ALU.subtract).then_inc(s["R1"], 1)
                for g in (2 * pair, 2 * pair + 1):
                    a = g % 2
                    dve.wait_ge(s["turned"], g + 1)
                    nc.vector.tensor_copy(flat(Tm[a]), ps[:, 3 * a + 1, :]).then_inc(s["T1"], 1)
                for l in range(1, 6):
                    for g in (2 * pair, 2 * pair + 1):
                        a = g % 2
                        dve.wait_ge(s["XX"], nth(g, l, 5))
                        if l < 5:
                            nc.vector.tensor_tensor(flat(Tm[a]), flat(Tm[a]), ps[:, 3 * a + 1, :], ALU.subtract).then_inc(s["T"], 1)
                        nc.vector.tensor_tensor(flat(Rm[a]), flat(Rm[a]), ps[:, 3 * a + 2, :], ALU.subtract).then_inc(s["R"], 1)

    r.at = mark[1]
    k.work.at = mark[0] + NT * 384
    sq, oT = r.take(NT, 384), k.work.take(NT, 3, P)
    ss, std = k.work.take(NT, NH0), k.work.take(NT, NH0)
    heads = lambda t: t.rearrange("p j (h d) -> p j h d", d=DV0)
    with k.stage("sq", "ss", "eps", "std", "rstd", "on", "og", "turned", "copied", "y", "added",
                 *NORM_SEMS) as (block, s):
        @block.scalar
        def _(act):
            nc.scalar.activation(sq, o_tm, ACT.Square).then_inc(s["sq"], 1)
            act.wait_ge(s["eps"], 1)
            nc.scalar.activation(std, ss, ACT.Sqrt).then_inc(s["std"], 1)
            for j in range(NT):
                act.wait_ge(s["turned"], j + 1)
                nc.scalar.copy(oT[:, j, :, :].rearrange("p a b -> p (a b)"), ps[:, j % 4, 0:384]).then_inc(s["copied"], 1)
                if j >= 5 and j % 2:
                    norm_root(k, s, act, (j - 5) // 2)
            norm_root(k, s, act, 2)
            norm_root(k, s, act, 3)
            for i in range(NT // 2):
                norm_copy(k, s, act, i, (0, 1))

        def add(dve, j):
            dve.wait_ge(s["y"], j + 1)
            nc.vector.tensor_tensor(x[:, j, :], x[:, j, :], ps[:, 4 + j % 4, 0:D], ALU.add).then_inc(s["added"], 1)

        def layernorm_pair(dve, i):
            dve.wait_ge(s["added"], 2 * i + 2)
            norm_front(k, s, dve, i)
            norm_back(k, s, dve, i)

        @block.vector
        def _(dve):
            dve.wait_ge(s["sq"], 1)
            nc.vector.tensor_reduce(ss.rearrange("p j h -> p (j h)"), sq.rearrange("p j (h d) -> p (j h) d", d=DV0), AX.X, ALU.add).then_inc(s["ss"], 1)
            dve.wait_ge(s["ss"], 1)
            nc.vector.tensor_scalar(ss, ss, 1.0 / DV0, 1e-5, ALU.mult, ALU.add).then_inc(s["eps"], 1)
            dve.wait_ge(s["std"], 1)
            nc.vector.reciprocal(ss, std).then_inc(s["rstd"], 1)
            dve.wait_ge(s["rstd"], 1)
            for j in range(NT):
                nc.vector.tensor_tensor(heads(o_tm)[:, j], heads(o_tm)[:, j], bc(ss[:, j, :], 2, DV0), ALU.mult).then_inc(s["on"], 1)
                dve.wait_ge(s["on"], j + 1)
                nc.vector.tensor_tensor(o_tm[:, j, :], o_tm[:, j, :], gate[:, j, :], ALU.mult).then_inc(s["og"], 1)
                if j >= 4:
                    add(dve, j - 4)
                    if j % 2:
                        layernorm_pair(dve, (j - 4) // 2)
            for j in range(NT - 4, NT):
                add(dve, j)
                if j % 2:
                    layernorm_pair(dve, j // 2)

        @block.tensor
        def _(pe):
            for j in range(NT + 1):
                if j < NT:
                    pe.wait_ge(s["og"], j + 1)
                    if j >= 4:
                        pe.wait_ge(s["copied"], j - 3)
                    for c in range(3):
                        last = nc.tensor.transpose(ps[:, j % 4, c * P:(c + 1) * P], o_tm[:, j, c * P:(c + 1) * P], k.ident)
                    last.then_inc(s["turned"], 1)
                if j >= 1:
                    i = j - 1
                    pe.wait_ge(s["copied"], i + 1)
                    if i >= 4:
                        pe.wait_ge(s["added"], i - 3)
                    for c in range(3):
                        last = nc.tensor.matmul(ps[:, 4 + i % 4, 0:D], oT[:, i, c, :], w.o[:, c, :], start=c == 0, stop=c == 2)
                    last.then_inc(s["y"], 1)
            for i in range(NT // 2):
                norm_turn(k, s, pe, i, (0, 1))



def no_load(k, w, sem):
    return 0


SUBLAYERS = [
    (load_L0_attn, stage_L0_attn), (load_gqa, stage_gqa), (load_L0_ffn, stage_L0_ffn),
    (load_L1_attn, stage_L1_attn),
    (lambda k, w, sem: load_latent_cross(k, w, sem, "L1_xattn_"), stage_L1_xattn), (load_L1_ffn, stage_L1_ffn),
    (load_L2_attn, stage_L2_attn), (lambda k, w, sem: load_latent_cross(k, w, sem, "L2_xattn_"), stage_L2_xattn), (load_L2_ffn, stage_L2_ffn),
    (load_L3_attn, stage_L3_attn), (load_gqa, stage_gqa), (load_L3_ffn, stage_L3_ffn),
]


ROUNDED_COLS = {2: 5120, 5: 6144, 8: 6144}


def decoder(nc, dram, out):
    with ExitStack() as ctx:
        k = Kit()
        k.nc, k.dram, k.serial, k.former = nc, dram, 0, []
        total, fixed_cols = 53200, 7904
        arena = ctx.enter_context(nc.sbuf_tensor("fixed", [P, fixed_cols], F32))
        wreg = [ctx.enter_context(nc.sbuf_tensor(f"weights{i}", [P, W_COLS], F32)) for i in range(2)]
        work_cols = total - fixed_cols - 2 * W_COLS
        k.ps = ctx.enter_context(nc.psum_tensor("ps", [P, 8, BANK], F32))
        fixed = Region(arena, fixed_cols)
        k.fixed = fixed
        k.x = fixed.take(NT, D)
        k.h = fixed.take(NT, D)
        k.hT = fixed.take(KC, TOK)
        k.ident = fixed.take(P)
        k.ident16 = fixed.take(P, dt=BF16)
        k.rev = fixed.take(32)
        k.causal = fixed.take(NT * SEQ, dt=BF16)
        k.nstats, k.nmv = fixed.take(NT, 6), fixed.take(NT, 2)
        k.nstd, k.nrstd = fixed.take(NT), fixed.take(NT)
        stored = nc.alloc_semaphore("stored")
        constants(k)
        loads = {}

        def start_loads(n):
            if n < len(STAGES):
                w = Named()
                w.region = Region(wreg[n % 2], W_COLS)
                w.sem = nc.alloc_semaphore(f"weights_of_{STAGES[n]}")
                w.loaded = SUBLAYERS[STAGES[n]][0](k, w, w.sem)
                loads[n] = w

        start_loads(0)
        for n, layer in enumerate(STAGES):
            start_loads(n + 1)
            rounded = ROUNDED_COLS.get(layer, 0)
            with ExitStack() as room:
                k.work = Region(room.enter_context(nc.sbuf_tensor(f"work_{n}", [P, work_cols - rounded], F32)), work_cols - rounded)
                if rounded:
                    k.rounded = Region(room.enter_context(nc.sbuf_tensor(f"rounded_{n}", [P, rounded], F32R)), rounded)
                if n == 0:
                    layernorm(k)
                SUBLAYERS[layer][1](k, loads[n])
        with nc.Block() as block:
            @block.sync
            def _(sp):
                sp.dma_start(out.rearrange("b t d -> (b t) d").rearrange("(j p) d -> p j d", p=P), k.x).then_inc(stored, 16)
                sp.wait_ge(stored, 16)



def lay_out(inputs):
    import numpy as np
    i = {n: np.asarray(a) for n, a in inputs.items()}
    T = lambda a: np.ascontiguousarray(np.swapaxes(a, -1, -2))
    o = {"x": i["x"], "ctx_512": i["ctx_512"]}
    o["ctxK"] = i["ctx_512"].reshape(TOK, 64).T.reshape(2, 2, 2, 8, NT, 2, SEQ).transpose(5, 2, 3, 0, 1, 4, 6).reshape(4, 8, 4, NT * SEQ)
    o["const_gmask"] = ((np.arange(P)[:, None] // GQA_D) % (2 * GQA_G) == np.arange(2 * GQA_G)).astype(np.float32)
    def rope(dim, repeat):
        inv = (1.0 / 10000.0 ** (np.arange(0, dim, 2, dtype=np.float32) / np.float32(dim))).astype(np.float32)
        f = np.arange(SEQ, dtype=np.float32)[:, None] * inv[None, :]
        widen = (lambda a: np.repeat(a, 2, 1)) if repeat else (lambda a: np.concatenate([a, a], 1))
        c, s = widen(np.cos(f)), widen(np.sin(f))
        return c, np.concatenate([-s[:, :dim // 2], s[:, dim // 2:]], 1)

    c, s = rope(64, True)
    o["const_rope64"] = np.tile(np.stack([c, s], 1), (2, 1, 1))
    c, s = rope(64, False)
    o["const_rope64b"] = np.tile(np.stack([c, s], 1), (2, 1, 1))
    o["const_rope64T"] = np.tile(np.stack([c.T, s.T], 1), (2, 1, 1))
    c, s = rope(192, True)
    o["const_rope192"] = np.stack([c.T.reshape(2, 96, SEQ), s.T.reshape(2, 96, SEQ)], 1).transpose(2, 1, 0, 3)
    o["const_causal"] = np.tile(np.where(np.arange(SEQ)[None, :] > np.arange(SEQ)[:, None], -1e30, 0), (2, NT)).astype(np.float32)
    o["const_rev"] = np.tile(np.arange(32, 0, -1, dtype=np.float32), (P, 1))
    p = "L0_ffn_"
    for n in ("gate_w", "fc1_w", "fc2_w", "fc2_b", "alpha"):
        o[p + n] = i[p + n]
    o[p + "fc1_b"] = i[p + "fc1_b"].reshape(8, 2, P).transpose(2, 1, 0)
    p = "L1_ffn_"
    for n in ("Wg", "Wu", "Wd", "Gb", "Ub", "Db", "Wr", "temperature"):
        o[p + n] = i[p + n]
    for n in "GUD":
        o[p + n + "aT"] = T(i[p + n + "a"])
    p = "L2_ffn_"
    o[p + "weightT"], o[p + "masksT"], o[p + "routerT"] = T(i[p + "weight"]), T(i[p + "expert_masks"]), T(i[p + "router_w"])
    o[p + "scale"] = i[p + "scale"]
    p = "L3_ffn_"
    o[p + "AT"] = i[p + "A"].reshape(512, D).T
    o[p + "BT"] = T(i[p + "Bw"]).reshape(512, D)
    o[p + "WgT"] = T(i[p + "Wg"])
    p = "L2_attn_"
    for n in ("Wq", "Wk"):
        o[p + n] = i[p + n].transpose(1, 0, 2).reshape(D, D)
    o[p + "Wv"] = i[p + "Wv"].reshape(8, 2, D, 16).transpose(2, 1, 0, 3).reshape(D, D)
    o[p + "Wo"], o[p + "bo"] = i[p + "Wo"], i[p + "bo"]
    o[p + "bias"] = np.stack([i[p + b].reshape(2, P).T for b in ("bq", "bk", "bv")], 1)
    o["const_pmask"] = ((np.arange(P)[:, None] // 16) % 2 == np.arange(2)).astype(np.float32)
    p = "L0_attn_"
    o[p + "WqkvT"] = np.concatenate([T(i[p + n]) for n in ("Wq", "Wk", "Wv")], 1)
    o[p + "WgT"], o[p + "WoT"] = T(i[p + "Wg"]), T(i[p + "Wo"])
    o[p + "WbaT"] = np.concatenate([T(i[p + "Wb"]), T(i[p + "Wa"])], 1)
    o[p + "conv_qk"] = np.concatenate([i[p + "conv_wq"], i[p + "conv_wk"]]).reshape(4, 96, 4).transpose(1, 0, 2)
    o[p + "conv_v"] = i[p + "conv_wv"].reshape(3, P, 4).transpose(1, 0, 2)
    for n in ("A_log", "dt_bias", "norm_w"):
        o[p + n] = i[p + n]
    a, b = np.arange(P)[:, None], np.arange(P)[None, :]
    same = a // SEQ == b // SEQ
    o["const_tri"] = np.stack([(a > b) & same, (a <= b) & same], 1).astype(np.float32)
    o["const_level"] = np.stack([(a // (2 << l) == b // (2 << l)) & (b // (1 << l) % 2 == 1) & (a // (1 << l) % 2 == 0)
                                 for l in range(LEVELS)], 1).astype(np.float32)
    o["const_head"] = (np.arange(96)[:, None] // DH0 == np.arange(96)[None, :] // DH0).astype(np.float32)
    for L in ("L1_xattn_", "L2_xattn_"):
        o[L + "Wq"] = i[L + "Wq"]
        o[L + "w_kc_kv"] = i[L + "w_kc_kv"]
        o[L + "qrT"] = T(i[L + "W_qr"])
        o[L + "krT"] = T(i[L + "W_kr"])
        o[L + "WoT"] = T(i[L + "Wo"])
    o["L1_xattn_kcqT"] = T(i["L1_xattn_w_kc_q"])
    o["L2_xattn_w_kc_q"] = i["L2_xattn_w_kc_q"]
    p = "L3_attn_"
    wqb = i[p + "Wq_b"].reshape(192, NH, 192)
    wkv = i[p + "Wkv_b"].reshape(64, NH, 256)
    swap = lambda a: np.concatenate([a[..., 32:], a[..., :32]], -1)
    o[p + "Wq_rot"], o[p + "Wq_swap"] = wqb[:, :, 128:], swap(wqb[:, :, 128:])
    o[p + "Wq_nopeT"] = wqb[:, :, :128].transpose(2, 1, 0)
    o[p + "WkT"], o[p + "WvT"] = wkv[:, :, :128].transpose(2, 1, 0), wkv[:, :, 128:].transpose(2, 1, 0)
    o[p + "Wo"] = i[p + "Wo"]
    o[p + "Wall"] = np.concatenate([i[p + "Wq_a"], i[p + "Wkv_a"], i[p + "Wk_rope"], swap(i[p + "Wk_rope"])], 1)
    o[p + "q_norm_w"], o[p + "kv_norm_w"] = i[p + "q_norm_w"].reshape(2, 96).T, i[p + "kv_norm_w"]
    o["L1_attn_WabT"] = np.concatenate([T(i["L1_attn_Wa"]), T(i["L1_attn_Wb"])], 1)
    o["L1_attn_WoutT"] = T(i["L1_attn_Wout"])
    o["L1_attn_bab"] = np.stack([i["L1_attn_ba"], i["L1_attn_bb"]], 1)
    o["L1_attn_bout"] = i["L1_attn_bout"]
    return {n: np.ascontiguousarray(a) for n, a in o.items()}


def kernel(**inputs):
    import concourse.bacc as _bacc
    from concourse.bass_utils import run_bass_kernel_spmd as _run

    arrays = lay_out(inputs)
    nc = _bacc.Bacc("TRN2", target_bir_lowering=False, num_devices=1)
    dram = {n: nc.dram_tensor(f"in_{n}", a.shape, mybir.dt.from_np(a.dtype), kind="ExternalInput").ap()
            for n, a in arrays.items()}
    out = nc.dram_tensor("out_0_dram", (BATCH, SEQ, D), F32, kind="ExternalOutput").ap()
    decoder(nc, dram, out)
    r = _run(nc, [{f"in_{n}": a for n, a in arrays.items()}], core_ids=[0])
    return r.results[0]["out_0_dram"]
```
